# Optimizing a Trainium2 kernel written in Bass

```python
import numpy as np
import jax
import jax.numpy as jnp

def _softmax(x, axis=-1):
    return jax.nn.softmax(x, axis=axis)

def _gelu(x):
    return jax.nn.gelu(x, approximate=True)

def _silu(x):
    return jax.nn.silu(x)

def _sigmoid(x):
    return jax.nn.sigmoid(x)

def _layernorm(x, axis=-1, eps=1e-05):
    m = jnp.mean(x, axis=axis, keepdims=True)
    v = jnp.var(x, axis=axis, keepdims=True)
    return (x - m) / jnp.sqrt(v + eps)

def _scatter_add(tgt, idx, src, axis=0):
    return tgt.at[idx].add(src)

def _segment_sum(src, seg, n):
    return jax.ops.segment_sum(src, seg, n)
kernel_name = 'mk_hybrid_d1_jaxref_r4_1b3341'

def setup_inputs(seed: int=0):
    np.random.seed(seed)
    _w = jnp.asarray

    def _L0_attn_a_setup():
        import jax, jax.numpy as jnp
        import numpy as np
        EPS = 1e-06

        def elu1(x):
            return jax.nn.elu(x) + 1.0
        key = jax.random.key(seed)
        ks = jax.random.split(key, 8)
        B, S, H, NH, M = (1, 512, 256, 16, 4)
        D = H // NH
        scale = 1.0 / np.sqrt(H)
        return {'hidden_states': jax.random.normal(ks[0], (B, S, H), jnp.float32), 'w_q': jax.random.normal(ks[1], (H, H), jnp.float32) * scale, 'w_k': jax.random.normal(ks[2], (H, H), jnp.float32) * scale, 'w_v': jax.random.normal(ks[3], (H, H), jnp.float32) * scale, 'w_o': jax.random.normal(ks[4], (H, H), jnp.float32) * scale, 'gate': jax.random.normal(ks[5], (NH,), jnp.float32), 'memories': jax.random.uniform(ks[6], (M, NH, D, D), jnp.float32), 'memory_norms': jax.random.uniform(ks[7], (M, NH, D), jnp.float32)}
    _L0_attn_a_in = _L0_attn_a_setup()

    def _L0_attn_b_setup():
        import jax, jax.numpy as jnp
        import numpy as np
        NUM_HEADS = 16
        THETA = 10000.0

        def _rope(x, theta):
            S, d_k = (x.shape[1], x.shape[-1])
            k = jnp.arange(d_k // 2, dtype=jnp.float32)
            inv_freq = theta ** (-2.0 * k / d_k)
            ang = jnp.arange(S, dtype=jnp.float32)[:, None] * inv_freq
            cos = jnp.cos(ang)[None, :, None, :]
            sin = jnp.sin(ang)[None, :, None, :]
            x_even = x[..., 0::2]
            x_odd = x[..., 1::2]
            y_even = cos * x_even - sin * x_odd
            y_odd = sin * x_even + cos * x_odd
            y = jnp.stack([y_even, y_odd], axis=-1)
            return y.reshape(x.shape)
        key = jax.random.key(seed)
        ks = jax.random.split(key, 5)
        B, S, D = (2, 512, 256)
        std = 1.0 / np.sqrt(D)
        return {'in_features': jax.random.normal(ks[0], (B, S, D), dtype=jnp.float32), 'W_Q': jax.random.normal(ks[1], (D, D), dtype=jnp.float32) * std, 'W_K': jax.random.normal(ks[2], (D, D), dtype=jnp.float32) * std, 'W_V': jax.random.normal(ks[3], (D, D), dtype=jnp.float32) * std, 'W_O': jax.random.normal(ks[4], (D, D), dtype=jnp.float32) * std}
    _L0_attn_b_in = _L0_attn_b_setup()

    def _L0_ffn_setup():
        import jax, jax.numpy as jnp
        import numpy as np
        EPS = 1e-05

        def _quantize(W):
            gamma = jnp.mean(jnp.abs(W))
            return jnp.clip(jnp.round(W / (gamma + EPS)), -1.0, 1.0)
        key = jax.random.key(seed)
        k_x, k_w1, k_b1, k_w2, k_b2 = jax.random.split(key, 5)
        n_embd = 256
        d_ff = 4 * n_embd
        B, S = (4, 1024)
        bound1 = 1.0 / np.sqrt(n_embd)
        bound2 = 1.0 / np.sqrt(d_ff)
        x = jax.random.normal(k_x, (B, S, n_embd), dtype=jnp.float32)
        W1 = jax.random.uniform(k_w1, (d_ff, n_embd), jnp.float32, -bound1, bound1)
        b1 = jax.random.uniform(k_b1, (d_ff,), jnp.float32, -bound1, bound1)
        W2 = jax.random.uniform(k_w2, (n_embd, d_ff), jnp.float32, -bound2, bound2)
        b2 = jax.random.uniform(k_b2, (n_embd,), jnp.float32, -bound2, bound2)
        return {'x': x, 'W1': W1, 'b1': b1, 'W2': W2, 'b2': b2}
    _L0_ffn_in = _L0_ffn_setup()
    _d = {'L0_attn_a_hidden_states': _L0_attn_a_in['hidden_states'], 'L0_attn_a_w_q': _L0_attn_a_in['w_q'], 'L0_attn_a_w_k': _L0_attn_a_in['w_k'], 'L0_attn_a_w_v': _L0_attn_a_in['w_v'], 'L0_attn_a_w_o': _L0_attn_a_in['w_o'], 'L0_attn_a_gate': _L0_attn_a_in['gate'], 'L0_attn_a_memories': _L0_attn_a_in['memories'], 'L0_attn_a_memory_norms': _L0_attn_a_in['memory_norms'], 'L0_attn_b_W_Q': _L0_attn_b_in['W_Q'], 'L0_attn_b_W_K': _L0_attn_b_in['W_K'], 'L0_attn_b_W_V': _L0_attn_b_in['W_V'], 'L0_attn_b_W_O': _L0_attn_b_in['W_O'], 'L0_ffn_W1': _L0_ffn_in['W1'], 'L0_ffn_b1': _L0_ffn_in['b1'], 'L0_ffn_W2': _L0_ffn_in['W2'], 'L0_ffn_b2': _L0_ffn_in['b2']}
    _x0 = _d['L0_attn_a_hidden_states']
    _d['L0_attn_a_hidden_states'] = jax.random.normal(jax.random.fold_in(jax.random.key(seed), 1), (16, 512, 256), dtype=_x0.dtype)
    del _x0
    return _d

def reference(L0_attn_a_hidden_states, L0_attn_a_w_q, L0_attn_a_w_k, L0_attn_a_w_v, L0_attn_a_w_o, L0_attn_a_gate, L0_attn_a_memories, L0_attn_a_memory_norms, L0_attn_b_W_Q, L0_attn_b_W_K, L0_attn_b_W_V, L0_attn_b_W_O, L0_ffn_W1, L0_ffn_b1, L0_ffn_W2, L0_ffn_b2):

    def _L0_attn_a_ref(hidden_states, w_q, w_k, w_v, w_o, gate, memories, memory_norms):
        import jax, jax.numpy as jnp
        import numpy as np
        EPS = 1e-06

        def elu1(x):
            return jax.nn.elu(x) + 1.0
        B, S, H = hidden_states.shape
        NH = gate.shape[0]
        D = H // NH

        def proj(w):
            return (hidden_states @ w.T).reshape(B, S, NH, D).transpose(0, 2, 1, 3)
        q, k, v = (proj(w_q), proj(w_k), proj(w_v))
        sq = elu1(q)
        sk = elu1(k)
        out_m = jnp.einsum('bhsd,mhde->mbhse', sq, memories)
        rel = jnp.einsum('bhsd,mhd->mbhs', sq, memory_norms)
        out_m = out_m / jnp.clip(rel, EPS, None)[..., None]
        weights = jax.nn.softmax(rel.mean(axis=-1), axis=0)
        mem_out = jnp.einsum('mbhse,mbh->bhse', out_m, weights)
        kv = jnp.einsum('bhsd,bhse->bhsde', sk, v)
        kv_cum = jnp.cumsum(kv, axis=2)
        k_cum = jnp.cumsum(sk, axis=2)
        num = jnp.einsum('bhsd,bhsde->bhse', sq, kv_cum)
        den = jnp.clip(jnp.einsum('bhsd,bhsd->bhs', sq, k_cum), EPS, None)
        local = num / den[..., None]
        g = jax.nn.sigmoid(gate)[None, :, None, None]
        out = g * mem_out + (1.0 - g) * local
        out = out.transpose(0, 2, 1, 3).reshape(B, S, H)
        return out @ w_o.T

    def _L0_attn_b_ref(in_features, W_Q, W_K, W_V, W_O):
        import jax, jax.numpy as jnp
        import numpy as np
        NUM_HEADS = 16
        THETA = 10000.0

        def _rope(x, theta):
            S, d_k = (x.shape[1], x.shape[-1])
            k = jnp.arange(d_k // 2, dtype=jnp.float32)
            inv_freq = theta ** (-2.0 * k / d_k)
            ang = jnp.arange(S, dtype=jnp.float32)[:, None] * inv_freq
            cos = jnp.cos(ang)[None, :, None, :]
            sin = jnp.sin(ang)[None, :, None, :]
            x_even = x[..., 0::2]
            x_odd = x[..., 1::2]
            y_even = cos * x_even - sin * x_odd
            y_odd = sin * x_even + cos * x_odd
            y = jnp.stack([y_even, y_odd], axis=-1)
            return y.reshape(x.shape)
        B, S, D = in_features.shape
        H = NUM_HEADS
        d_k = D // H
        scale = 1.0 / np.sqrt(np.float32(d_k))
        q = jnp.einsum('kd,bsd->bsk', W_Q, in_features).reshape(B, S, H, d_k)
        k = jnp.einsum('kd,bsd->bsk', W_K, in_features).reshape(B, S, H, d_k)
        v = jnp.einsum('vd,bsd->bsv', W_V, in_features).reshape(B, S, H, d_k)
        q = _rope(q, THETA)
        k = _rope(k, THETA)
        q = q.transpose(0, 2, 1, 3)
        k = k.transpose(0, 2, 1, 3)
        v = v.transpose(0, 2, 1, 3)
        scores = jnp.einsum('bhqd,bhkd->bhqk', q, k) * scale
        causal = jnp.tril(jnp.ones((S, S), dtype=bool))
        scores = jnp.where(causal[None, None], scores, -jnp.inf)
        attn = jax.nn.softmax(scores, axis=-1)
        out = jnp.einsum('bhqk,bhkd->bhqd', attn, v)
        out = out.transpose(0, 2, 1, 3).reshape(B, S, D)
        return jnp.einsum('dv,bsv->bsd', W_O, out)

    def _L0_ffn_ref(x, W1, b1, W2, b2):
        import jax, jax.numpy as jnp
        import numpy as np
        EPS = 1e-05

        def _quantize(W):
            gamma = jnp.mean(jnp.abs(W))
            return jnp.clip(jnp.round(W / (gamma + EPS)), -1.0, 1.0)
        Wq1 = _quantize(W1)
        Wq2 = _quantize(W2)
        h = jax.nn.relu(jnp.einsum('bsd,fd->bsf', x, Wq1) + b1)
        out = jnp.einsum('bsf,df->bsd', h, Wq2) + b2
        return out
    x = L0_attn_a_hidden_states
    x = x + _L0_attn_a_ref(_layernorm(x, axis=-1), L0_attn_a_w_q, L0_attn_a_w_k, L0_attn_a_w_v, L0_attn_a_w_o, L0_attn_a_gate, L0_attn_a_memories, L0_attn_a_memory_norms)
    x = x + _L0_ffn_ref(_layernorm(x, axis=-1), L0_ffn_W1, L0_ffn_b1, L0_ffn_W2, L0_ffn_b2)
    x = x + _L0_attn_b_ref(_layernorm(x, axis=-1), L0_attn_b_W_Q, L0_attn_b_W_K, L0_attn_b_W_V, L0_attn_b_W_O)
    x = x + _L0_ffn_ref(_layernorm(x, axis=-1), L0_ffn_W1, L0_ffn_b1, L0_ffn_W2, L0_ffn_b2)
    return x

_drawn_inputs = setup_inputs


def setup_inputs(seed=0):
    import zlib

    import numpy as np

    out = dict(_drawn_inputs(seed))
    spreads = {}
    factors = {'L0_attn_a_w_k': 7.356,
     'L0_attn_b_W_Q': 8.0,
     'L0_attn_b_W_K': 8.0,
     'L0_attn_b_W_V': 8.0,
     'L0_attn_b_W_O': 8.0,
     'L0_ffn_b1': 8.0,
     'L0_ffn_b2': 8.0}
    for name, (base, spread) in spreads.items():
        noise = np.random.default_rng([zlib.crc32(name.encode()), seed]).standard_normal(out[name].shape)
        drawn = base * np.exp(spread * noise) if base else spread * noise
        out[name] = jnp.asarray(drawn.astype(out[name].dtype))
    for name, factor in factors.items():
        out[name] = (out[name] * factor).astype(out[name].dtype)
    return out
```

```python
from contextlib import ExitStack

import numpy as np

import concourse.bass as bass
from concourse import mybir

F32 = mybir.dt.float32
F16 = mybir.dt.float16
BF16 = mybir.dt.bfloat16
ALU = mybir.AluOpType
ACT = mybir.ActivationFunctionType
AX = mybir.AxisListType.X

P = 128
B, S, H, NH, M = 16, 512, 256, 16, 4
D = H // NH
FF = 4 * H
KH = H // P
HH8 = NH // KH
NT = S // P
FT = FF // P
LN_EPS = 1e-5
MEM_EPS = 1e-6
Q_EPS = 1e-5
THETA = 10000.0

WS = 128.0
VS = 8.0
AS = 2.0 ** -6
RS = 16.0
MASKED = -1e30
VW = 2 * D + 1
MW = D + 1
STK = 96
AQ, AK, AV, AO, BQ, BK, BV, BO, BQR, BKR = range(10)
NMAT = 10

PER = dict(
    bn=16, tick=4, mv=16, ve=4, rstd=4, xn=16, xt=8, xh=8, xl=8,
    proj=4, e=4, r=4, sq=4, sh=8, sl=8, v=4, vh=4, vl=4, sk=3, skt=3,
    ssb=2, rm=1, rmax=1, rdif=1, rexp=1, rsum=1, rrec=1, rcoef=2,
    st=6, bf=6, bh=6, bl=6, a=16, am=16, ah=16, al_pool=8, al_dve=8,
    om=8, clip=24, rec=8, coef=8, t6=24, ot=4, oh=4, ol=4, wo=4, xres=4,
    up=16, hf=16, hh=16, hl_pool=8, hl_dve=8, xb=2, dn=4, xffn=4,
    pr=8, t12=8, y=4, s1=64, mx=64, nh=4, nl=4, nm=4, nmt=4, s2=48, pexp=48, phi=48,
    plo_pool=32, plo_dve=16, pv=16, prec=8, tb=16, xin=16, store=16,
)
STACK_PER = 2 * 8 * 16


def work_jobs():
    jobs = []
    xl, vl, ol, xres, hf, xffn = 0, 0, 0, 0, 0, 0

    def turn(st):
        nonlocal xl
        for k in range(KH):
            xl += 1
            jobs.append((("T", st, k), "xl", xl))

    def values(st):
        nonlocal vl
        for j in range(2):
            vl += 1
            jobs.append((("V", st, j), "vl", vl))

    def outs(st):
        nonlocal ol, xres
        for half in range(KH):
            ol += 1
            jobs.append((("OT", st, half), "ol", ol))
        for j in range(2):
            xres += 1
            jobs.append((("WO", st, j), "xres", xres))

    def ffn(st):
        nonlocal hf, xffn
        turn(st)
        for m in range(FT):
            hf += 1
            jobs.append((("UP", st, m), "hf", hf))
        for j in range(2):
            xffn += 1
            jobs.append((("DN", st, j), "xffn", xffn))

    turn(0)
    for t in range(4):
        jobs.append((("PA", t), "r", t + 1))
    values(0)
    for c in range(NT - 1):
        jobs.append((("SK", c), "skt", c + 1))
    jobs.append((("RM",), "rdif", 1))
    for n in range(6):
        jobs.append((("ST", n), "bf", n + 1))
    outs(0)
    ffn(1)
    turn(2)
    for t in range(4):
        for r in range(2):
            jobs.append((("PB", t, r), "t12", 2 * t + r + 1))
    values(2)
    for n in range(20):
        if n >= 4 and n % 4 == 0:
            jobs.append((("NM", n // 4 - 1), "nmt", n // 4))
        if n >= 5 and (n - 5) % 2 == 0:
            jobs.append((("PV", (n - 5) // 2), "tb", n - 5 + 2))
    outs(2)
    ffn(3)
    return jobs


NWORK = 3
WORK = work_jobs()
WORK_AT = {job: n for n, (job, _, _) in enumerate(WORK)}
S2_TILES = [[0], [1, 3], [2]]
S2_COL = [0, 512, 1024]
KT_AT = {0: 0, 1: 512, 3: 512 + 384, 2: 1024}


def build(nc, x, wall, mem, gate, w1t, b1t, w2t, b2, cos, sin, out):
    assert len(WORK) % NWORK == 0 or True
    ctx = ExitStack()
    with ctx:
        def sb(name, shape, dt):
            return ctx.enter_context(nc.sbuf_tensor(name, shape, dt))

        def sem(name):
            return ctx.enter_context(nc.semaphore(name))

        wh = sb("wh", [P, NMAT, KH, H], F16)
        wl = sb("wl", [P, NMAT, KH, H], F16)
        w1q = sb("w1q", [P, KH, FF], F16)
        w2q = sb("w2q", [P, FT, H], F16)
        b1c = sb("b1c", [P, FT], F32)
        b2bc = sb("b2bc", [P, H], F32)
        cost = sb("cost", [P, S], F32)
        sint = sb("sint", [P, S], F32)
        ident = sb("ident", [P, P], F32)
        identh = sb("identh", [P, P], F16)
        identb = sb("identb", [P, P], BF16)
        onesf = sb("onesf", [P, P], F32)
        tri = sb("tri", [P, P], F32)
        mask_qk = sb("mask_qk", [P, P], BF16)
        mask_kq = sb("mask_kq", [P, P], BF16)
        bdmask = sb("bdmask", [P, HH8, VW], F32)
        sel = sb("sel", [P, NH * NT, P], BF16)
        bm = sb("bm", [P, KH, M, HH8, MW], F32)
        bmh = sb("bmh", [P, KH, M, HH8, MW], F16)
        bml = sb("bml", [P, KH, M, HH8, MW], F16)
        gates = sb("gates", [P, 4, NH], F32)
        small = sb("small", [P, 16], F32)
        halfc = sb("halfc", [P, NT], F32)
        x0, x13, x2, x4 = (sb(name, [P, NT, H], F32) for name in ("x0", "x13", "x2", "x4"))
        xs = [x0, x13, x2, x13, x4]
        xn = sb("xn", [P, NT, H], F32)
        stats = sb("stats", [P, NT, 6], F32)
        mv = sb("mv", [P, NT, 2], F32)
        tick = sb("tick", [P, 1], F32)
        ve = sb("ve", [P, NT], F32)
        rstd = sb("rstd", [P, NT], F32)
        xh = sb("xh", [P, KH, S], F16)
        xlo = sb("xlo", [P, KH, S], F16)
        qst = sb("qst", [P, NH, S], F16)
        kst = sb("kst", [P, NH, S], F16)
        sth = sb("sth", [P, 4, S], F16)
        stl = sb("stl", [P, 4, S], F16)
        vp = sb("vp", [P, NT, NH, VW], F16)
        skt = sb("skt", [P, NT - 1, 4, P], F16)
        ssum = sb("ssum", [P, KH], F32)
        ssb = sb("ssb", [P, KH, P], F32)
        wmax = sb("wmax", [P, NH], F32)
        wdif = sb("wdif", [P, KH, M, HH8], F32)
        wexp = sb("wexp", [P, KH, M, HH8], F32)
        wsum = sb("wsum", [P, NH], F32)
        wrec = sb("wrec", [P, NH], F32)
        wnum = sb("wnum", [P, KH, M, HH8], F32)
        wc = sb("wc", [P, KH, M + 1, HH8], F32)
        bf = sb("bf", [P, 2, HH8 * VW], F32)
        bsh = sb("bsh", [P, 6, HH8 * VW], F16)
        bsl = sb("bsl", [P, 6, HH8 * VW], F16)
        am = sb("am", [P, 2, S], F32)
        big_h = sb("big_h", [P, NH, S], F16)
        big_l = sb("big_l", [P, NH, S], F16)
        den = sb("den", [P, 2, M + 1, HH8], F32)
        drec = sb("drec", [P, 2, M + 1, HH8], F32)
        coef = sb("coef", [P, 2, M + 1, HH8], F32)
        tbuf = sb("tbuf", [P, NT, 2, NH, D], F32)
        oth = sb("oth", [P, KH, S], F16)
        otl = sb("otl", [P, KH, S], F16)
        pf = sb("pf", [P, 2, 1280], F32)
        nt = sb("nt", [P, 2, NH * NT], BF16)
        nmt = sb("nmt", [P, 2, P], BF16)
        mxs = sb("mxs", [P, NH * NT], F32)
        prec = sb("prec", [P, 2, 2, NT], F32)
        pfl = pf[:, :, :].rearrange("p a b -> p (a b)")
        ebuf = pfl[:, 0:4 * S].rearrange("p (t s) -> p t s", t=4)
        t6 = pfl[:, 0:2 * (M + 2) * P].rearrange("p (r t s) -> p r t s", r=2, t=M + 2)
        rbuf = am
        sqb = tbuf[:, :, :, :, :].rearrange("p i t h d -> p (i t h d)").rearrange("p (t s) -> p t s", t=4)
        t12 = am
        hf = am
        hh = big_h[:, 0:FT, :]
        hl = big_l[:, 0:FT, :]
        ph = big_h[:, FT:FT + 5, :].rearrange("p a b -> p (a b)").rearrange("p (r n) -> p r n", r=2)
        pl = big_l[:, FT:FT + 5, :].rearrange("p a b -> p (a b)").rearrange("p (r n) -> p r n", r=2)

        work = [ctx.enter_context(nc.psum_tensor(f"work{n}", [P, 512], F32)) for n in range(NWORK)]
        sc = [ctx.enter_context(nc.psum_tensor(f"sc{n}", [P, 512], F32)) for n in range(2)]
        wide = [ctx.enter_context(nc.psum_tensor(f"wide{n}", [P, 512], F32)) for n in range(3)]

        s = {name: sem(name) for name in PER}
        landed = [sem(f"landed{h}") for h in range(NH)]
        w_in = sem("w_in")
        c_in = sem("c_in")
        g_in = sem("g_in")
        m_in = sem("m_in")
        pool_const = sem("pool_const")
        dve_setup = sem("dve_setup")
        act_setup = sem("act_setup")
        pe_setup = sem("pe_setup")
        primed = sem("primed")
        DVE_SETUP = 25
        block = ctx.enter_context(nc.Block())

        def due(name, it, n):
            return it * PER[name] + n + 1

        def ring(job):
            return work[WORK_AT[job] % NWORK]

        def x_of(ap):
            return ap.rearrange("(b j p) f -> b p j f", b=B, p=P)

        x_in, x_out = x_of(x), x_of(out)

        w_stage_a = qst[:, :, :].rearrange("p a b -> p (a b)").bitcast(F32)
        w_stage_b = kst[:, :, :].rearrange("p a b -> p (a b)").bitcast(F32)
        f_stage = big_h[:, :, :].rearrange("p a b -> p (a b)").bitcast(F32)
        f_tmp = big_l[:, :, :].rearrange("p a b -> p (a b)")
        NFW = KH * FF

        @block.sync
        def _(sp):
            wv = wall.rearrange("n (k p) f -> p n k f", p=P)
            for n in range(NMAT):
                stage = w_stage_a if n < 8 else w_stage_b
                at = (n % 8) * KH * H
                sp.dma_start(stage[:, at:at + KH * H].rearrange("p (k f) -> p k f", k=KH), wv[:, n]).then_inc(w_in, 16)
            sp.dma_start(f_stage[:, 0:NFW].rearrange("p (k f) -> p k f", k=KH),
                         w1t.rearrange("(k p) f -> p k f", p=P)).then_inc(w_in, 16)
            sp.dma_start(f_stage[:, NFW:2 * NFW].rearrange("p (k f) -> p k f", k=FT),
                         w2t.rearrange("(k p) f -> p k f", p=P)).then_inc(w_in, 16)
            sp.dma_start(b1c[:, :], b1t).then_inc(c_in, 16)
            sp.dma_start(b2bc[:, :], b2.broadcast_to([P, H])).then_inc(c_in, 16)
            sp.dma_start(cost[:, :], cos).then_inc(c_in, 16)
            sp.dma_start(sint[:, :], sin).then_inc(c_in, 16)
            sp.dma_start(gates[:, 0, :], gate.broadcast_to([P, NH])).then_inc(g_in, 16)
            sp.wait_ge(pool_const, 1)
            for half in range(KH):
                for h in range(HH8):
                    at = slice(h * D, (h + 1) * D)
                    sp.dma_start(bm[at, half, :, h, :], mem[half * HH8 + h]).then_inc(m_in, 16)
            sp.wait_ge(dve_setup, DVE_SETUP)
            sp.wait_ge(primed, 1)
            with sp.Fori(0, B) as it:
                sp.wait_ge(s["xres"], due("xres", it, 0))
                sp.dma_start(xs[0][:, :, :], x_in[bass.ds(it, 1)].rearrange("o p j f -> p (o j) f")).then_inc(s["xin"], 16)
                for st in range(2):
                    for h in range(NH):
                        half, r = divmod(h, HH8)
                        if r == 0:
                            if half == 0:
                                sp.wait_ge(s["xt"], due("xt", it, 4 * st + 2))
                            sp.wait_ge(s["sh"], due("sh", it, 4 * st + 2 * half + 2))
                            sp.wait_ge(s["sl"], due("sl", it, 4 * st + 2 * half + 2))
                        rows = slice(r * D, (r + 1) * D)
                        for k, (tq, tk) in enumerate(((sth, sth), (sth, stl), (stl, sth), (stl, stl))):
                            to = slice(k * D, (k + 1) * D)
                            sp.dma_start(qst[to, h, :], tq[rows, 2 * half, :]).then_inc(landed[h], 16)
                            sp.dma_start(kst[to, h, :], tk[rows, 2 * half + 1, :]).then_inc(landed[h], 16)

        @block.gpsimd
        def _(pool):
            nc.gpsimd.memset(bm[:, :, :, :, :], 0.0).then_inc(pool_const, 1)
            nc.gpsimd.memset(ident[:, :], 0.0).then_inc(pool_const, 1)
            nc.gpsimd.memset(tri[:, :], 1.0).then_inc(pool_const, 1)
            nc.gpsimd.memset(mask_qk[:, :], 0.0).then_inc(pool_const, 1)
            nc.gpsimd.memset(mask_kq[:, :], 0.0).then_inc(pool_const, 1)
            nc.gpsimd.memset(bdmask[:, :, :], 1.0).then_inc(pool_const, 1)
            nc.gpsimd.memset(halfc[:, :], -0.5).then_inc(pool_const, 1)
            nc.gpsimd.memset(nt[:, :, :], 0.0).then_inc(pool_const, 1)
            pool.wait_ge(pool_const, 8)
            nc.gpsimd.affine_select(out=ident[:, :], in_=ident[:, :], compare_op=ALU.not_equal, fill=1.0, base=0,
                                    pattern=[[-1, P]], channel_multiplier=1).then_inc(pool_const, 1)
            nc.gpsimd.affine_select(out=tri[:, :], in_=tri[:, :], compare_op=ALU.is_ge, fill=0.0, base=0,
                                    pattern=[[1, P]], channel_multiplier=-1).then_inc(pool_const, 1)
            nc.gpsimd.affine_select(out=mask_qk[:, :], in_=mask_qk[:, :], compare_op=ALU.is_ge, fill=MASKED, base=0,
                                    pattern=[[-1, P]], channel_multiplier=1).then_inc(pool_const, 1)
            nc.gpsimd.affine_select(out=mask_kq[:, :], in_=mask_kq[:, :], compare_op=ALU.is_ge, fill=MASKED, base=0,
                                    pattern=[[1, P]], channel_multiplier=-1).then_inc(pool_const, 1)
            nc.gpsimd.affine_select(out=bdmask[:, :, :], in_=bdmask[:, :, :], compare_op=ALU.is_ge, fill=0.0, base=0,
                                    pattern=[[-D, HH8], [0, VW]], channel_multiplier=1).then_inc(pool_const, 1)
            pool.wait_ge(pool_const, 13)
            nc.gpsimd.affine_select(out=bdmask[:, :, :], in_=bdmask[:, :, :], compare_op=ALU.is_ge, fill=0.0,
                                    base=D - 1, pattern=[[D, HH8], [0, VW]], channel_multiplier=-1).then_inc(pool_const, 1)
            pool.wait_ge(c_in, 64)
            pool.wait_ge(pool_const, 14)

            for name in PER:
                nc.gpsimd.sem_inc(s[name], 1)
            nc.gpsimd.drain().then_inc(primed, 1)

            def rstd_of(st, it):
                pool.wait_ge(s["ve"], due("ve", it, st + 1))
                nc.gpsimd.tensor_tensor(rstd[:, :], ve[:, :], halfc[:, :], ALU.pow).then_inc(s["rstd"], 1)

            def ffn(f, it):
                st = 1 + 2 * f
                rstd_of(st, it)
                pool.wait_ge(s["xn"], due("xn", it, NT * (st + 1)))
                nc.gpsimd.tensor_tensor(xs[st][:, :, :], xs[st][:, :, :],
                                        b2bc[:, :].rearrange("p (a f) -> p a f", a=1).broadcast_to([P, NT, H]),
                                        ALU.add).then_inc(s["xb"], 1)
                for m in range(0, FT, 2):
                    pool.wait_ge(s["hh"], due("hh", it, FT * f + m + 1))
                    nc.gpsimd.tensor_tensor(hl[:, m, :], hf[:, m % 2, :], hh[:, m, :],
                                            ALU.subtract).then_inc(s["hl_pool"], 1)

            with pool.Fori(0, B) as it:
                rstd_of(0, it)
                for t in range(4):
                    pool.wait_ge(s["sh"], due("sh", it, t + 1))
                    pool.wait_ge(s["sq"], due("sq", it, t + 1))
                    nc.gpsimd.tensor_tensor(stl[:, t, :], sqb[:, t, :], sth[:, t, :], ALU.subtract).then_inc(s["sl"], 1)
                for n in range(6):
                    pool.wait_ge(s["bh"], due("bh", it, n + 1))
                    nc.gpsimd.tensor_tensor(bsl[:, n, :], bf[:, n % 2, :], bsh[:, n, :],
                                            ALU.subtract).then_inc(s["bl"], 1)
                for h in range(0, NH, 2):
                    pool.wait_ge(s["ah"], due("ah", it, h + 1))
                    nc.gpsimd.tensor_tensor(big_l[:, h, :], am[:, h % 2, :], big_h[:, h, :],
                                            ALU.subtract).then_inc(s["al_pool"], 1)
                ffn(0, it)
                rstd_of(2, it)
                for t in range(4):
                    pool.wait_ge(s["t12"], due("t12", it, 2 * t + 2))
                    nc.gpsimd.tensor_tensor(sqb[:, t, :], t12[:, 0, :], t12[:, 1, :], ALU.add).then_inc(s["y"], 1)
                for h in range(NH):
                    for n in range(2):
                        a, b = S2_COL[n], S2_COL[n + 1]
                        pool.wait_ge(s["phi"], due("phi", it, 3 * h + n + 1))
                        nc.gpsimd.tensor_tensor(pl[:, h % 2, a:b], pf[:, h % 2, a:b], ph[:, h % 2, a:b],
                                                ALU.subtract).then_inc(s["plo_pool"], 1)
                ffn(1, it)

        @block.scalar
        def _(act):
            act.wait_ge(g_in, 16)
            nc.scalar.activation(gates[:, 1, :], gates[:, 0, :], ACT.Exp, scale=-1.0).then_inc(act_setup, 1)
            act.wait_ge(w_in, 16 * (NMAT + 2))
            for n in range(2):
                nc.scalar.activation(f_tmp[:, n * NFW:(n + 1) * NFW], f_stage[:, n * NFW:(n + 1) * NFW], ACT.Abs,
                                     accum_out=small[:, n:n + 1]).then_inc(act_setup, 1)
            act.wait_ge(dve_setup, DVE_SETUP)
            act.wait_ge(primed, 1)

            def turned(st, it):
                for k in range(KH):
                    act.wait_ge(s["xt"], due("xt", it, 2 * st + k + 1))
                    nc.scalar.activation(xh[:, k, :], ring(("T", st, k))[:, :], ACT.Copy).then_inc(s["xh"], 1)

            def values(st, it):
                n = st
                for j in range(2):
                    act.wait_ge(s["v"], due("v", it, n + j + 1))
                    nc.scalar.activation(
                        vp[:, 2 * j:2 * j + 2, :, 0:D],
                        ring(("V", st, j))[:, :].rearrange("p (c h d) -> p c h d", c=2, d=D),
                        ACT.Copy, scale=VS / WS).then_inc(s["vh"], 1)

            def heads_out(st, it):
                for half in range(KH):
                    act.wait_ge(s["ot"], due("ot", it, st + half + 1))
                    nc.scalar.activation(oth[:, half, :], ring(("OT", st, half))[:, :], ACT.Copy).then_inc(s["oh"], 1)

            def ffn(f, it):
                st = 1 + 2 * f
                turned(st, it)
                for m in range(FT):
                    act.wait_ge(s["up"], due("up", it, FT * f + m + 1))
                    if m >= 2:
                        if m % 2 == 0:
                            act.wait_ge(s["hl_pool"], due("hl_pool", it, (FT * f + m) // 2))
                        else:
                            act.wait_ge(s["hl_dve"], due("hl_dve", it, (FT * f + m - 1) // 2))
                    nc.scalar.activation(hf[:, m % 2, :], ring(("UP", st, m))[:, :], ACT.Relu,
                                         bias=b1c[:, m:m + 1]).then_inc(s["hf"], 1)

            with act.Fori(0, B) as it:
                turned(0, it)
                for t in range(4):
                    act.wait_ge(s["proj"], due("proj", it, t + 1))
                    if t == 0:
                        act.wait_ge(s["plo_pool"], due("plo_pool", it, 0))
                        act.wait_ge(s["plo_dve"], due("plo_dve", it, 0))
                    nc.scalar.activation(ebuf[:, t, :], ring(("PA", t))[:, :], ACT.Exp, scale=1 / WS).then_inc(s["e"], 1)
                    if t >= 1:
                        act.wait_ge(s["sq"], due("sq", it, t))
                        if t == 1:
                            act.wait_ge(s["a"], due("a", it, 0))
                        nc.scalar.activation(sth[:, t - 1, :], sqb[:, t - 1, :], ACT.Copy).then_inc(s["sh"], 1)
                act.wait_ge(s["sq"], due("sq", it, 4))
                nc.scalar.activation(sth[:, 3, :], sqb[:, 3, :], ACT.Copy).then_inc(s["sh"], 1)
                values(0, it)
                for c in range(NT - 1):
                    act.wait_ge(s["sk"], due("sk", it, c + 1))
                    nc.scalar.activation(skt[:, c, :, :].rearrange("p a b -> p (a b)"),
                                         ring(("SK", c))[:, :].bitcast(F16)[:, 0:4 * P], ACT.Copy).then_inc(s["skt"], 1)
                act.wait_ge(s["rdif"], due("rdif", it, 1))
                nc.scalar.activation(wexp[:, :, :, :], wdif[:, :, :, :], ACT.Exp, scale=1.0 / S).then_inc(s["rexp"], 1)
                for n in range(6):
                    act.wait_ge(s["bf"], due("bf", it, n + 1))
                    nc.scalar.activation(bsh[:, n, :], bf[:, n % 2, :], ACT.Copy).then_inc(s["bh"], 1)
                for h in range(NH):
                    act.wait_ge(s["am"], due("am", it, h + 1))
                    nc.scalar.activation(big_h[:, h, :], am[:, h % 2, :], ACT.Copy).then_inc(s["ah"], 1)
                heads_out(0, it)
                ffn(0, it)
                turned(2, it)
                for t in range(4):
                    act.wait_ge(s["y"], due("y", it, t + 1))
                    nc.scalar.activation(sth[:, t, :], sqb[:, t, :], ACT.Copy).then_inc(s["sh"], 1)
                values(2, it)
                for h in range(NH):
                    if h % NT == 0:
                        g = h // NT
                        act.wait_ge(s["nm"], due("nm", it, g + 1))
                        if g >= 2:
                            act.wait_ge(s["s2"], due("s2", it, 12 * (g - 1)))
                        nc.scalar.activation(nmt[:, g % 2, :], ring(("NM", g))[:, :].bitcast(BF16)[:, 0:P],
                                             ACT.Copy).then_inc(s["nmt"], 1)
                    if h >= 2:
                        act.wait_ge(s["plo_pool"], due("plo_pool", it, 2 * (h - 1)))
                        act.wait_ge(s["plo_dve"], due("plo_dve", it, h - 1))
                    for n in range(3):
                        w = [512, 512, 256][n]
                        act.wait_ge(s["s2"], due("s2", it, 3 * h + n + 1))
                        nc.scalar.activation(pf[:, h % 2, S2_COL[n]:S2_COL[n] + w], wide[n][:, 0:w], ACT.Exp,
                                             scale=D ** -0.5 / RS ** 2).then_inc(s["pexp"], 1)
                    for n in range(3):
                        w = [512, 512, 256][n]
                        act.wait_ge(s["pexp"], due("pexp", it, 3 * h + n + 1))
                        if h >= 2:
                            act.wait_ge(s["pv"], due("pv", it, h - 1))
                        nc.scalar.activation(ph[:, h % 2, S2_COL[n]:S2_COL[n] + w], pf[:, h % 2, S2_COL[n]:S2_COL[n] + w],
                                             ACT.Copy).then_inc(s["phi"], 1)
                heads_out(2, it)
                ffn(1, it)
                act.wait_ge(s["xffn"], due("xffn", it, 4))
                act.dma_start(x_out[bass.ds(it, 1)].rearrange("o p j f -> p (o j) f"), xs[4][:, :, :]).then_inc(s["store"], 16)
            act.wait_ge(s["store"], 16 * B + 1)

        @block.vector
        def _(dve):
            chain = [0]

            def link(ins):
                chain[0] += 1
                ins.then_inc(dve_setup, 1)
                dve.wait_ge(dve_setup, chain[0])

            V = nc.vector
            link(V.memset(onesf[:, :], 1.0))
            link(V.memset(vp[:, :, :, 2 * D:VW], 1.0))
            dve.wait_ge(w_in, 16 * (NMAT + 2))
            for stage, at, n in ((w_stage_a, 0, 8), (w_stage_b, 8, 2)):
                cols = n * KH * H
                hi = wh[:, at:at + n, :, :].rearrange("p n k f -> p (n k f)")
                lo = wl[:, at:at + n, :, :].rearrange("p n k f -> p (n k f)")
                link(V.tensor_scalar(hi, stage[:, 0:cols], WS, None, ALU.mult))
                link(V.scalar_tensor_tensor(lo, stage[:, 0:cols], WS, hi, ALU.mult, ALU.subtract))
            link(V.memset(qst[64:STK, :, :], 0.0))
            link(V.memset(kst[64:STK, :, :], 0.0))
            dve.wait_ge(act_setup, 3)
            link(V.tensor_scalar(gates[:, 1, :], gates[:, 1, :], 1.0, None, ALU.add))
            link(V.reciprocal(gates[:, 2, :], gates[:, 1, :]))
            for half in range(KH):
                link(V.tensor_scalar(wc[:, half, M, :], gates[:, 2, half * HH8:(half + 1) * HH8], -1.0, 1.0,
                                     ALU.mult, ALU.add))
            link(V.tensor_scalar(gates[:, 3, :], gates[:, 2, :], VS, None, ALU.mult))
            dve.wait_ge(pe_setup, 1)
            link(V.tensor_scalar(small[:, 2:4], work[0][:, 0:2], 1.0 / (H * FF), Q_EPS, ALU.mult, ALU.add))
            link(V.tensor_scalar(small[:, 4:6], small[:, 2:4], 0.5, None, ALU.mult))
            link(V.tensor_scalar(small[:, 6:8], small[:, 2:4], -0.5, None, ALU.mult))
            for n, w in enumerate((w1q[:, :, :].rearrange("p a b -> p (a b)"), w2q[:, :, :].rearrange("p a b -> p (a b)"))):
                stage = f_stage[:, n * NFW:(n + 1) * NFW]
                below = f_tmp[:, n * NFW:(n + 1) * NFW]
                link(V.tensor_scalar(below, stage, small[:, 6 + n:7 + n], None, ALU.is_lt))
                if n == 0:
                    link(V.scalar_tensor_tensor(w, stage, small[:, 4 + n:5 + n], below, ALU.is_gt, ALU.subtract))
                else:
                    link(V.scalar_tensor_tensor(w, stage, small[:, 4 + n:5 + n], below, ALU.is_gt, ALU.subtract))
            dve.wait_ge(pool_const, 14)
            link(V.tensor_copy(identh[:, :], ident[:, :]))
            link(V.tensor_copy(identb[:, :], ident[:, :]))
            G = NH * NT
            link(V.tensor_tensor(sel[:, :, :],
                                 ident[:, 0:G].rearrange("p (g o) -> p g o", o=1).broadcast_to([P, G, P]),
                                 ident[:, G:2 * G].rearrange("p (g o) -> p g o", o=1).broadcast_to([P, G, P]), ALU.add))
            dve.wait_ge(m_in, 16 * NH)
            bm_all = bm[:, :, :, :, :].rearrange("p a m h e -> p (a m h e)")
            bmh_all = bmh[:, :, :, :, :].rearrange("p a m h e -> p (a m h e)")
            bml_all = bml[:, :, :, :, :].rearrange("p a m h e -> p (a m h e)")
            link(V.tensor_copy(bmh_all, bm_all))
            V.tensor_tensor(bml_all, bm_all, bmh_all, ALU.subtract).then_inc(dve_setup, 1)
            chain[0] += 1
            assert chain[0] == DVE_SETUP, chain[0]
            dve.wait_ge(primed, 1)

            def norm(st, it):
                X = xs[st]
                for j in range(NT):
                    if j == 0:
                        if st == 0:
                            dve.wait_ge(s["xin"], due("xin", it, 16))
                        elif st % 2:
                            dve.wait_ge(s["xres"], due("xres", it, st + 1))
                        else:
                            dve.wait_ge(s["xffn"], due("xffn", it, st))
                    V.bn_stats(stats[:, j, :], X[:, j, :]).then_inc(s["bn"], 1)
                dve.wait_ge(s["bn"], due("bn", it, NT * (st + 1)))
                V.memset(tick[:, :], 0.0).then_inc(s["tick"], 1)
                for j in range(NT):
                    V.bn_aggr(mv[:, j, :], stats[:, j, :]).then_inc(s["mv"], 1)
                dve.wait_ge(s["mv"], due("mv", it, NT * (st + 1)))
                V.tensor_scalar(ve[:, :], mv[:, :, 1], LN_EPS, None, ALU.add).then_inc(s["ve"], 1)
                dve.wait_ge(s["rstd"], due("rstd", it, st + 1))
                for j in range(NT):
                    V.tensor_scalar(xn[:, j, :], X[:, j, :], mv[:, j, 0:1], rstd[:, j:j + 1],
                                    ALU.subtract, ALU.mult).then_inc(s["xn"], 1)
                for k in range(KH):
                    dve.wait_ge(s["xh"], due("xh", it, 2 * st + k + 1))
                    V.tensor_tensor(xlo[:, k, :], ring(("T", st, k))[:, :], xh[:, k, :],
                                    ALU.subtract).then_inc(s["xl"], 1)

            def values(st, it):
                for j in range(2):
                    dve.wait_ge(s["vh"], due("vh", it, st + j + 1))
                    for c in range(2):
                        ins = V.scalar_tensor_tensor(
                            vp[:, 2 * j + c, :, D:2 * D],
                            ring(("V", st, j))[:, c * H:(c + 1) * H].rearrange("p (h d) -> p h d", d=D),
                            VS / WS, vp[:, 2 * j + c, :, 0:D], ALU.mult, ALU.subtract)
                    ins.then_inc(s["vl"], 1)

            def project_out(st, it):
                for half in range(KH):
                    dve.wait_ge(s["oh"], due("oh", it, st + half + 1))
                    V.tensor_tensor(otl[:, half, :], ring(("OT", st, half))[:, :], oth[:, half, :],
                                    ALU.subtract).then_inc(s["ol"], 1)
                for j in range(2):
                    dve.wait_ge(s["wo"], due("wo", it, st + j + 1))
                    two = slice(2 * j, 2 * j + 2)
                    V.scalar_tensor_tensor(xs[st + 1][:, two, :],
                                           ring(("WO", st, j))[:, :].rearrange("p (a f) -> p a f", a=2),
                                           1 / (WS * VS), xs[st][:, two, :], ALU.mult, ALU.add).then_inc(s["xres"], 1)

            def ffn(f, it):
                st = 1 + 2 * f
                norm(st, it)
                for m in range(FT):
                    dve.wait_ge(s["hf"], due("hf", it, FT * f + m + 1))
                    V.tensor_copy(hh[:, m, :], hf[:, m % 2, :]).then_inc(s["hh"], 1)
                    if m % 2:
                        dve.wait_ge(s["hh"], due("hh", it, FT * f + m + 1))
                        V.tensor_tensor(hl[:, m, :], hf[:, m % 2, :], hh[:, m, :],
                                        ALU.subtract).then_inc(s["hl_dve"], 1)
                dve.wait_ge(s["xb"], due("xb", it, f + 1))
                for j in range(2):
                    dve.wait_ge(s["dn"], due("dn", it, 2 * f + j + 1))
                    if f == 1 and j == 0:
                        dve.wait_ge(s["store"], due("store", it, 0))
                    two = slice(2 * j, 2 * j + 2)
                    V.tensor_tensor(xs[st + 1][:, two, :],
                                    ring(("DN", st, j))[:, :].rearrange("p (a f) -> p a f", a=2),
                                    xs[st][:, two, :], ALU.add).then_inc(s["xffn"], 1)

            def causal(h, it):
                dve.wait_ge(s["a"], due("a", it, h + 1))
                if h >= 2:
                    if h % 2 == 0:
                        dve.wait_ge(s["al_pool"], due("al_pool", it, h // 2))
                    else:
                        dve.wait_ge(s["al_dve"], due("al_dve", it, (h - 1) // 2))
                V.scalar_tensor_tensor(am[:, h % 2, :].rearrange("p (c s) -> p c s", c=NT),
                                       sc[h % 2][:, :].rearrange("p (c s) -> p c s", c=NT), AS,
                                       tri[:, :].rearrange("p (c s) -> p c s", c=1).broadcast_to([P, NT, P]),
                                       ALU.mult, ALU.mult).then_inc(s["am"], 1)
                if h != HH8 and h >= 1 and (h - 1) % 2:
                    low(h - 1, it)

            def low(h, it):
                dve.wait_ge(s["ah"], due("ah", it, h + 1))
                V.tensor_tensor(big_l[:, h, :], am[:, h % 2, :], big_h[:, h, :],
                                ALU.subtract).then_inc(s["al_dve"], 1)

            def combine(n, it):
                half, r = n // NT, n % 2
                dve.wait_ge(s["om"], due("om", it, n + 1))
                local = wide[0][:, 0:HH8 * VW].rearrange("p (h w) -> p h w", w=VW)
                for k in range(2):
                    pair = wide[1 + k][:, 0:2 * HH8 * MW].rearrange("p (m h w) -> p m h w", m=2, w=MW)
                    V.tensor_scalar(den[:, r, 2 * k:2 * k + 2, :], pair[:, :, :, D], MEM_EPS, None,
                                    ALU.max).then_inc(s["clip"], 1)
                V.tensor_scalar(den[:, r, M, :], local[:, :, 2 * D], MEM_EPS * AS, None, ALU.max).then_inc(s["clip"], 1)
                dve.wait_ge(s["clip"], due("clip", it, 3 * n + 3))
                V.reciprocal(drec[:, r, :, :], den[:, r, :, :]).then_inc(s["rec"], 1)
                dve.wait_ge(s["rec"], due("rec", it, n + 1))
                V.tensor_tensor(coef[:, r, :, :], drec[:, r, :, :], wc[:, half, :, :], ALU.mult).then_inc(s["coef"], 1)
                dve.wait_ge(s["coef"], due("coef", it, n + 1))
                if n >= 2:
                    pass
                for k in range(2):
                    pair = wide[1 + k][:, 0:2 * HH8 * MW].rearrange("p (m w) -> p m w", w=MW)
                    V.tensor_tensor(t6[:, r, 2 * k:2 * k + 2, :].rearrange("p m (h d) -> p (m h) d", d=D),
                                    pair[:, :, 0:D],
                                    coef[:, r, 2 * k:2 * k + 2, :].rearrange("p m (h o) -> p (m h) o", o=1)
                                    .broadcast_to([P, 2 * HH8, D]), ALU.mult).then_inc(s["t6"], 1)
                V.tensor_tensor(t6[:, r, M:M + 2, :].rearrange("p t (h d) -> p t h d", d=D),
                                local[:, :, 0:2 * D].rearrange("p h (t d) -> p t h d", t=2),
                                coef[:, r, M:M + 1, :].rearrange("p t (h o) -> p t h o", o=1)
                                .broadcast_to([P, 2, HH8, D]), ALU.mult).then_inc(s["t6"], 1)

            def head_out(pair, it):
                r = pair % 2
                dve.wait_ge(s["pv"], due("pv", it, 2 * pair + 2))
                ps = ring(("PV", pair))[:, 0:2 * NT * VW].rearrange("p (a i w) -> p a i w", a=2, w=VW)
                V.reciprocal(prec[:, r, :, :], ps[:, :, :, 2 * D]).then_inc(s["prec"], 1)
                dve.wait_ge(s["prec"], due("prec", it, pair + 1))
                for a in range(2):
                    V.tensor_tensor(tbuf[:, :, :, 2 * pair + a, :],
                                    ps[:, a, :, 0:2 * D].rearrange("p i (t d) -> p i t d", t=2),
                                    prec[:, r, a, :].rearrange("p (i t o) -> p i t o", t=1, o=1)
                                    .broadcast_to([P, NT, 2, D]), ALU.mult).then_inc(s["tb"], 1)

            with dve.Fori(0, B) as it:
                norm(0, it)
                for t in range(4):
                    dve.wait_ge(s["e"], due("e", it, t + 1))
                    V.tensor_scalar(rbuf[:, t % 2, :], ring(("PA", t))[:, :], 1 / WS, 0.0,
                                    ALU.mult, ALU.max).then_inc(s["r"], 1)
                    dve.wait_ge(s["r"], due("r", it, t + 1))
                    if t == 0:
                        dve.wait_ge(s["ot"], due("ot", it, 0))
                    V.scalar_tensor_tensor(sqb[:, t, :], ebuf[:, t, :], 1.0, rbuf[:, t % 2, :], ALU.min, ALU.add,
                                           accum_out=ssum[:, t // 2:t // 2 + 1] if t % 2 == 0 else None
                                           ).then_inc(s["sq"], 1)
                dve.wait_ge(s["sq"], due("sq", it, 4))
                dve.wait_ge(s["rm"], due("rm", it, 0))
                for half in range(KH):
                    V.tensor_scalar(ssb[:, half, :], onesf[:, :], ssum[:, half:half + 1], None,
                                    ALU.mult).then_inc(s["ssb"], 1)
                values(0, it)
                dve.wait_ge(s["rm"], due("rm", it, 1))
                rm = ring(("RM",))[:, 0:KH * M * HH8].rearrange("p (a m h) -> p a m h", a=KH, m=M)
                V.tensor_reduce(wmax[:, :].rearrange("p (a h) -> p a h", a=KH), rm.rearrange("p a m h -> p a h m"),
                                AX, ALU.max).then_inc(s["rmax"], 1)
                dve.wait_ge(s["rmax"], due("rmax", it, 1))
                V.tensor_tensor(wdif[:, :, :, :], rm, wmax[:, :].rearrange("p (a m h) -> p a m h", a=KH, m=1)
                                .broadcast_to([P, KH, M, HH8]), ALU.subtract).then_inc(s["rdif"], 1)
                dve.wait_ge(s["rexp"], due("rexp", it, 1))
                V.tensor_reduce(wsum[:, :].rearrange("p (a h) -> p a h", a=KH),
                                wexp[:, :, :, :].rearrange("p a m h -> p a h m"), AX, ALU.add).then_inc(s["rsum"], 1)
                dve.wait_ge(s["rsum"], due("rsum", it, 1))
                V.reciprocal(wrec[:, :], wsum[:, :]).then_inc(s["rrec"], 1)
                dve.wait_ge(s["rrec"], due("rrec", it, 1))
                V.tensor_tensor(wnum[:, :, :, :], wexp[:, :, :, :],
                                wrec[:, :].rearrange("p (a m h) -> p a m h", a=KH, m=1)
                                .broadcast_to([P, KH, M, HH8]), ALU.mult).then_inc(s["rcoef"], 1)
                dve.wait_ge(s["rcoef"], due("rcoef", it, 1))
                V.tensor_tensor(wc[:, :, 0:M, :], wnum[:, :, :, :],
                                gates[:, 3, :].rearrange("p (a m h) -> p a m h", a=KH, m=1)
                                .broadcast_to([P, KH, M, HH8]), ALU.mult).then_inc(s["rcoef"], 1)
                dve.wait_ge(s["rcoef"], due("rcoef", it, 2))
                for n in range(6):
                    dve.wait_ge(s["st"], due("st", it, n + 1))
                    if n >= 2:
                        dve.wait_ge(s["bl"], due("bl", it, n - 1))
                    V.scalar_tensor_tensor(bf[:, n % 2, :], ring(("ST", n))[:, 0:HH8 * VW], AS,
                                           bdmask[:, :, :].rearrange("p h w -> p (h w)"),
                                           ALU.mult, ALU.mult).then_inc(s["bf"], 1)
                for h in range(HH8):
                    causal(h, it)
                low(HH8 - 1, it)
                for c in range(NT):
                    combine(c, it)
                    causal(HH8 + 2 * c, it)
                    causal(HH8 + 2 * c + 1, it)
                low(NH - 1, it)
                for c in range(NT):
                    combine(NT + c, it)
                project_out(0, it)
                ffn(0, it)
                norm(2, it)
                for t in range(4):
                    for r in range(2):
                        dve.wait_ge(s["pr"], due("pr", it, 2 * t + r + 1))
                        if t >= 1 and r == 0:
                            dve.wait_ge(s["y"], due("y", it, t))
                        V.scalar_tensor_tensor(t12[:, r, :], ring(("PB", t, r))[:, :], RS / WS,
                                               (cost, sint)[r][:, :], ALU.mult, ALU.mult).then_inc(s["t12"], 1)
                    if t >= 1:
                        dve.wait_ge(s["sh"], due("sh", it, 4 + t))
                        V.tensor_tensor(stl[:, t - 1, :], sqb[:, t - 1, :], sth[:, t - 1, :],
                                        ALU.subtract).then_inc(s["sl"], 1)
                dve.wait_ge(s["sh"], due("sh", it, 8))
                V.tensor_tensor(stl[:, 3, :], sqb[:, 3, :], sth[:, 3, :], ALU.subtract).then_inc(s["sl"], 1)
                values(2, it)
                for n in range(NH + 7):
                    if n < NH:
                        for i in range(NT):
                            g = NT * n + i
                            dve.wait_ge(s["s1"], due("s1", it, g + 1))
                            V.tensor_reduce(mxs[:, g:g + 1], sc[i % 2][:, 0:(i + 1) * P], AX, ALU.max).then_inc(s["mx"], 1)
                        if n % NT == NT - 1:
                            q = n // NT
                            gs = slice(16 * q, 16 * q + 16)
                            dve.wait_ge(s["mx"], due("mx", it, 16 * (q + 1)))
                            V.tensor_scalar(nt[:, 0, gs], mxs[:, gs], -1.0, None, ALU.mult).then_inc(s["nh"], 1)
                            dve.wait_ge(s["nh"], due("nh", it, q + 1))
                            V.scalar_tensor_tensor(nt[:, 1, gs], mxs[:, gs], -1.0, nt[:, 0, gs],
                                                   ALU.mult, ALU.subtract).then_inc(s["nl"], 1)
                    if 4 <= n < NH + 4:
                        h = n - 4
                        dve.wait_ge(s["phi"], due("phi", it, 3 * h + 3))
                        V.tensor_tensor(pl[:, h % 2, 1024:1280], pf[:, h % 2, 1024:1280], ph[:, h % 2, 1024:1280],
                                        ALU.subtract).then_inc(s["plo_dve"], 1)
                    if n >= 7 and (n - 7) % 2 == 0:
                        head_out((n - 7) // 2, it)
                project_out(2, it)
                ffn(1, it)

        @block.tensor
        def _(pe):
            T = nc.tensor
            pe.wait_ge(act_setup, 3)
            pe.wait_ge(dve_setup, 1)
            T.matmul(work[0][:, 0:2], onesf[:, :], small[:, 0:2], start=True, stop=True).then_inc(pe_setup, 1)
            pe.wait_ge(dve_setup, DVE_SETUP)
            pe.wait_ge(primed, 1)

            def take(job, it):
                n = WORK_AT[job]
                if n >= NWORK:
                    _, name, count = WORK[n - NWORK]
                    pe.wait_ge(s[name], due(name, it, count))
                else:
                    at = (n % NWORK) + (len(WORK) // NWORK) * NWORK
                    if at >= len(WORK):
                        at -= NWORK
                    name = WORK[at][1]
                    pe.wait_ge(s[name], due(name, it, 0))
                return ring(job)

            def turn(st, it):
                banks = [take(("T", st, k), it) for k in range(KH)]
                for j in range(NT):
                    pe.wait_ge(s["xn"], due("xn", it, NT * st + j + 1))
                    for k in range(KH):
                        ins = T.transpose(banks[k][:, j * P:(j + 1) * P], xn[:, j, k * P:(k + 1) * P], ident[:, :])
                        if j == NT - 1:
                            ins.then_inc(s["xt"], 1)

            def project(job, mat, m, name, it):
                bank = take(job, it)
                n = 0
                for w, a in ((wh, xh), (wl, xh), (wh, xlo)):
                    for k in range(KH):
                        ins = T.matmul(bank[:, :], w[:, mat, k, m * P:(m + 1) * P], a[:, k, :],
                                       start=(n == 0), stop=(n == 5))
                        n += 1
                ins.then_inc(s[name], 1)

            def rows(job, a_parts, mat, name, it):
                bank = take(job, it)
                j2 = job[-1]
                for a in range(2):
                    n = 0
                    cols = slice((2 * j2 + a) * P, (2 * j2 + a + 1) * P)
                    for w, part in ((wh, 0), (wl, 0), (wh, 1)):
                        for k in range(KH):
                            ins = T.matmul(bank[:, a * H:(a + 1) * H], a_parts[part][:, k, cols], w[:, mat, k, :],
                                           start=(n == 0), stop=(n == 5))
                            n += 1
                ins.then_inc(s[name], 1)

            def project_out(st, mat, it):
                pe.wait_ge(s["ol"], due("ol", it, st + 2))
                for j in range(2):
                    rows(("WO", st, j), (oth, otl), mat, "wo", it)

            def ffn(f, it):
                st = 1 + 2 * f
                turn(st, it)
                pe.wait_ge(s["xl"], due("xl", it, 2 * st + 2))
                for m in range(FT):
                    bank = take(("UP", st, m), it)
                    for n, (a, k) in enumerate(((xh, 0), (xh, 1), (xlo, 0), (xlo, 1))):
                        ins = T.matmul(bank[:, :], w1q[:, k, m * P:(m + 1) * P], a[:, k, :], start=(n == 0), stop=(n == 3))
                    ins.then_inc(s["up"], 1)
                pe.wait_ge(s["hl_pool"], due("hl_pool", it, FT // 2 * (f + 1)))
                pe.wait_ge(s["hl_dve"], due("hl_dve", it, FT // 2 * (f + 1)))
                for j2 in range(2):
                    bank = take(("DN", st, j2), it)
                    for a in range(2):
                        cols = slice((2 * j2 + a) * P, (2 * j2 + a + 1) * P)
                        for m in range(FT):
                            for part in (hh, hl):
                                ins = T.matmul(bank[:, a * H:(a + 1) * H], part[:, m, cols], w2q[:, m, :],
                                               start=(m == 0 and part is hh), stop=(m == FT - 1 and part is hl))
                    ins.then_inc(s["dn"], 1)

            def products(h, it):
                pe.wait_ge(landed[h], it * STACK_PER + STACK_PER // 2)
                if h >= 2:
                    pe.wait_ge(s["am"], due("am", it, h - 1))
                for c in range(NT):
                    cols = slice(c * P, (c + 1) * P)
                    ins = T.matmul(sc[h % 2][:, cols], kst[0:STK, h, cols], qst[0:STK, h, cols], start=True, stop=True)
                ins.then_inc(s["a"], 1)

            def outputs(n, it):
                half, c = divmod(n, NT)
                cols = slice(c * P, (c + 1) * P)
                if c == 0:
                    pe.wait_ge(s["al_pool"], due("al_pool", it, HH8 // 2 * (half + 1)))
                    pe.wait_ge(s["al_dve"], due("al_dve", it, HH8 // 2 * (half + 1)))
                if n >= 1:
                    pe.wait_ge(s["t6"], due("t6", it, 3 * n))
                local = wide[0]
                qh, ql = sth[:, 2 * half, cols], stl[:, 2 * half, cols]
                if c:
                    k = 3 * half + c - 1
                    if c == 1:
                        pe.wait_ge(s["bl"], due("bl", it, 3 * half + 3))
                    for m, (a, b) in enumerate(((qh, bsh), (ql, bsh), (qh, bsl))):
                        T.matmul(local[:, 0:HH8 * VW], a, b[:, k, :], start=(m == 0), stop=(m == 2), skip_group_check=True)
                for h in range(HH8):
                    hh_ = half * HH8 + h
                    for part in (big_h, big_l):
                        T.matmul(local[:, h * VW:(h + 1) * VW], part[:, hh_, cols], vp[:, c, hh_, :],
                                 start=(c == 0 and part is big_h), stop=(part is big_l), skip_group_check=True)
                for k in range(2):
                    for m, (a, b) in enumerate(((qh, bmh), (ql, bmh), (qh, bml))):
                        ins = T.matmul(wide[1 + k][:, 0:2 * HH8 * MW], a,
                                       b[:, half, 2 * k:2 * k + 2, :, :].rearrange("p m h w -> p (m h w)"),
                                       start=(m == 0), stop=(m == 2))
                ins.then_inc(s["om"], 1)

            def turn_back(n, it):
                half, c = divmod(n, NT)
                bank = take(("OT", 0, half), it) if c == 0 else ring(("OT", 0, half))
                pe.wait_ge(s["t6"], due("t6", it, 3 * n + 3))
                for t in range(M + 2):
                    ins = T.matmul(bank[:, c * P:(c + 1) * P], t6[:, n % 2, t, :], ident[:, :], is_transpose=True,
                                   start=(t == 0), stop=(t == M + 1))
                if c == NT - 1:
                    ins.then_inc(s["ot"], 1)

            def scores(h, it):
                pe.wait_ge(landed[h], it * STACK_PER + STACK_PER)
                for i in range(NT):
                    g = NT * h + i
                    if g >= 2:
                        pe.wait_ge(s["mx"], due("mx", it, g - 1))
                    bank = sc[i % 2]
                    T.matmul(bank[:, 0:(i + 1) * P], qst[0:STK, h, i * P:(i + 1) * P], kst[0:STK, h, 0:(i + 1) * P],
                             start=True, stop=True)
                    T.matmul(bank[:, i * P:(i + 1) * P], identb[:, :], mask_qk[:, :], start=False, stop=True,
                             skip_group_check=True).then_inc(s["s1"], 1)

            def shifted(h, it):
                if h % NT == 0:
                    pe.wait_ge(s["nmt"], due("nmt", it, h // NT + 1))
                for n, tiles in enumerate(S2_TILES):
                    if h >= 1:
                        pe.wait_ge(s["pexp"], due("pexp", it, 3 * (h - 1) + n + 1))
                    for kt in tiles:
                        at = KT_AT[kt] - S2_COL[n]
                        w = (NT - kt) * P
                        T.matmul(wide[n][:, at:at + w], kst[0:STK, h, kt * P:(kt + 1) * P], qst[0:STK, h, kt * P:S],
                                 start=True, stop=True)
                        T.matmul(wide[n][:, at:at + P], identb[:, :], mask_kq[:, :], start=False, stop=True,
                                 skip_group_check=True)
                        for i in range(kt, NT):
                            a = at + (i - kt) * P
                            ins = T.matmul(wide[n][:, a:a + P], sel[:, NT * h + i, :], nmt[:, (h // NT) % 2, :],
                                           start=False, stop=True, skip_group_check=True)
                    ins.then_inc(s["s2"], 1)

            def weighted(h, it):
                bank = take(("PV", h // 2), it) if h % 2 == 0 else ring(("PV", h // 2))
                pe.wait_ge(s["plo_pool"], due("plo_pool", it, 2 * h + 2))
                pe.wait_ge(s["plo_dve"], due("plo_dve", it, h + 1))
                for i in range(NT):
                    at = ((h % 2) * NT + i) * VW
                    for kt in range(i + 1):
                        p0 = KT_AT[kt] + (i - kt) * P
                        for part in (ph, pl):
                            ins = T.matmul(bank[:, at:at + VW], part[:, h % 2, p0:p0 + P], vp[:, kt, h, :],
                                           start=(kt == 0 and part is ph), stop=(kt == i and part is pl),
                                           skip_group_check=True)
                ins.then_inc(s["pv"], 1)

            with pe.Fori(0, B) as it:
                turn(0, it)
                pe.wait_ge(s["xl"], due("xl", it, 2))
                for t, (mat, m) in enumerate(((AQ, 0), (AK, 0), (AQ, 1), (AK, 1))):
                    project(("PA", t), mat, m, "proj", it)
                for j in range(2):
                    rows(("V", 0, j), (xh, xlo), AV, "v", it)
                pe.wait_ge(s["sl"], due("sl", it, 4))
                for c in range(NT - 1):
                    bank = take(("SK", c), it)
                    cols = slice(c * P, (c + 1) * P)
                    for n, (part, half) in enumerate(((sth, 0), (stl, 0), (sth, 1), (stl, 1))):
                        ins = T.transpose(bank[:, :].bitcast(F16)[:, n * P:(n + 1) * P], part[:, 2 * half + 1, cols],
                                          identh[:, :])
                    ins.then_inc(s["sk"], 1)
                bank = take(("RM",), it)
                pe.wait_ge(s["ssb"], due("ssb", it, 2))
                for half in range(KH):
                    ins = T.matmul(bank[:, half * M * HH8:(half + 1) * M * HH8], ssb[:, half, :],
                                   bm[:, half, :, :, D].rearrange("p m h -> p m h"), start=True, stop=True)
                ins.then_inc(s["rm"], 1)
                pe.wait_ge(s["vl"], due("vl", it, 2))
                pe.wait_ge(s["skt"], due("skt", it, NT - 1))
                for n in range(6):
                    half, c = divmod(n, 3)
                    bank = take(("ST", n), it)
                    for cc in range(c + 1):
                        for part in range(2):
                            ins = T.matmul(bank[:, 0:HH8 * VW], skt[:, cc, 2 * half + part, :],
                                           vp[:, cc, half * HH8:(half + 1) * HH8, :].rearrange("p h w -> p (h w)"),
                                           start=(cc == 0 and part == 0), stop=(cc == c and part == 1))
                    ins.then_inc(s["st"], 1)
                for h in range(HH8):
                    products(h, it)
                for c in range(NT):
                    outputs(c, it)
                    products(HH8 + 2 * c, it)
                    products(HH8 + 2 * c + 1, it)
                    turn_back(c, it)
                for c in range(NT):
                    outputs(NT + c, it)
                    turn_back(NT + c, it)
                project_out(0, AO, it)
                ffn(0, it)
                turn(2, it)
                pe.wait_ge(s["xl"], due("xl", it, 6))
                for t, (m, a, b) in enumerate(((0, BQ, BQR), (0, BK, BKR), (1, BQ, BQR), (1, BK, BKR))):
                    project(("PB", t, 0), a, m, "pr", it)
                    project(("PB", t, 1), b, m, "pr", it)
                for j in range(2):
                    rows(("V", 2, j), (xh, xlo), BV, "v", it)
                pe.wait_ge(s["vl"], due("vl", it, 4))
                for n in range(NH + 5):
                    if n < NH:
                        scores(n, it)
                    if n >= 4 and n % 4 == 0 and n < NH + 4:
                        q = n // 4 - 1
                        bank = take(("NM", q), it)
                        pe.wait_ge(s["nl"], due("nl", it, q + 1))
                        T.transpose(bank[:, :].bitcast(BF16)[:, 0:P], nt[:, :, :].rearrange("p a g -> p (a g)"),
                                    identb[:, :]).then_inc(s["nm"], 1)
                    if 4 <= n < NH + 4:
                        shifted(n - 4, it)
                    if n >= 5:
                        weighted(n - 5, it)
                pe.wait_ge(s["tb"], due("tb", it, NH))
                for half in range(KH):
                    bank = take(("OT", 2, half), it)
                    for i in range(NT):
                        for t in range(2):
                            ins = T.matmul(bank[:, i * P:(i + 1) * P],
                                           tbuf[:, i, t, half * HH8:(half + 1) * HH8, :].rearrange("p h d -> p (h d)"),
                                           ident[:, :], is_transpose=True, start=(t == 0), stop=(t == 1))
                    ins.then_inc(s["ot"], 1)
                project_out(2, BO, it)
                ffn(1, it)


def kernel(**inputs):
    import numpy as _np
    import concourse.bacc as _bacc
    from concourse import mybir as _mybir
    from concourse.bass_utils import run_bass_kernel_spmd as _run

    a = {k: _np.asarray(v) for k, v in inputs.items()}
    pairs = _np.arange(H) ^ 1
    mats = [a["L0_attn_a_w_q"], a["L0_attn_a_w_k"], a["L0_attn_a_w_v"], a["L0_attn_a_w_o"],
            a["L0_attn_b_W_Q"], a["L0_attn_b_W_K"], a["L0_attn_b_W_V"], a["L0_attn_b_W_O"],
            a["L0_attn_b_W_Q"][pairs], a["L0_attn_b_W_K"][pairs]]
    f32 = _np.float32
    inv = (f32(THETA) ** (f32(-2.0) * _np.arange(D // 2, dtype=f32) / f32(D))).astype(f32)
    ang = (_np.arange(S, dtype=f32)[:, None] * inv).astype(f32)
    of_row = (_np.arange(P) % D) // 2
    sign = _np.where(_np.arange(P) % 2 == 0, -1.0, 1.0).astype(f32)
    cos = _np.cos(ang)[:, of_row].T
    sin = _np.sin(ang)[:, of_row].T * sign[:, None]
    arrays = {
        "x": a["L0_attn_a_hidden_states"].reshape(B * S, H),
        "wall": _np.stack([m.T for m in mats]),
        "mem": _np.concatenate([a["L0_attn_a_memories"], a["L0_attn_a_memory_norms"][..., None]],
                               axis=-1).transpose(1, 2, 0, 3),
        "gate": a["L0_attn_a_gate"].reshape(1, NH),
        "w1t": a["L0_ffn_W1"].T,
        "b1t": a["L0_ffn_b1"].reshape(FT, P).T,
        "w2t": a["L0_ffn_W2"].T,
        "b2": a["L0_ffn_b2"].reshape(1, H),
        "cos": cos,
        "sin": sin,
    }
    arrays = {k: _np.ascontiguousarray(v) for k, v in arrays.items()}
    nc = _bacc.Bacc("TRN2", target_bir_lowering=False, num_devices=1)
    args = [nc.dram_tensor(k, v.shape, _mybir.dt.from_np(v.dtype), kind="ExternalInput").ap() for k, v in arrays.items()]
    out = nc.dram_tensor("out", (B * S, H), _mybir.dt.float32, kind="ExternalOutput").ap()
    build(nc, *args, out)
    r = _run(nc, [arrays], core_ids=[0])
    return r.results[0]["out"].reshape(B, S, H)
```

```python
from contextlib import ExitStack

import numpy as np

import concourse.bass as bass
from concourse import mybir

F32 = mybir.dt.float32
F16 = mybir.dt.float16
BF16 = mybir.dt.bfloat16
ALU = mybir.AluOpType
ACT = mybir.ActivationFunctionType
AX = mybir.AxisListType.X

P = 128
B, S, H, NH, M = 16, 512, 256, 16, 4
D = H // NH
FF = 4 * H
KH = H // P
HH8 = NH // KH
NT = S // P
FT = FF // P
LN_EPS = 1e-5
MEM_EPS = 1e-6
Q_EPS = 1e-5
THETA = 10000.0

WS = 128.0
VS = 8.0
AS = 2.0 ** -6
RS = 16.0
SHIFT = 1024.0
MASKED = -1e30
VW = 2 * D + 1
MW = D + 1
PARTS = 4 * D
STK = 96
MAXROW = 96
LAG = 5
AQ, AK, AV, AO, BQ, BK, BV, BO, BQR, BKR = range(10)
NMAT = 10

NORM = dict(bn=8, tick=2, ptick=2, mv=8, ve=2, rstd=2, xn=8, xt=4, xh=4, xl=4)
OUTS = dict(v=2, vh=2, vl=2, sh=4, sl=4, bounced=64, wo=2, xres=2)
FFN = dict(up=8, hf=8, hh=8, hl_pool=4, hl_dve=4, xb=1, dn=2, xffn=2)
PER1 = dict(
    NORM, **OUTS, **FFN, xin=16, proj=4, e=4, r=4, sq=4, sk=3, skt=3,
    ssb=2, rm=1, rmax=1, rdif=1, rexp=1, rsum=1, rrec=1, rcoef=2,
    st=6, bf=6, bh=6, bl=6, a=16, am=16, ah=16, al_pool=8, al_dve=8,
    om=24, clip=24, rec=8, coef=8, t6=24, ot=8, oh=8, ol=8,
)
PER2 = dict(
    NORM, **OUTS, **FFN, pr=8, t12=8, y=4, s1=64, mx=64, nh=4, nl=4, nm=4, nmt=4, mrow=128, s2=48, pexp=48,
    phi=48, plo_pool=32, plo_dve=16, pv=16, prec=16, tb=16, ot=2, oh=2, ol=2, store=16,
)
LANDED = 2 * 4 * 16

def mark1(kind, n=0):
    return {"T": 0, "PA": 3 + 2 * n, "V": 12 + 2 * n, "SK": 17, "RM": 18, "ST": 19 + n, "N": 26 + 4.8 * n,
            "WO": 70 + 3 * n, "FT": 76, "UP": 79 + 1.2 * n, "DN": 90 + 5 * n, "END": 99}[kind]


def mark2(kind, n=0):
    return {"T": 0.5, "PB": 2.5 + 3 * n, "V": 15 + 2 * n, "N": 20 + 2.3 * n, "OT": 72 + n, "WO": 75 + 2 * n,
            "FT": 79, "UP": 82 + n, "DN": 90.5 + 5 * n, "END": 99.5}[kind]


def jobs1():
    jobs = [(("T", 0, k), "xl", k + 1) for k in range(KH)]
    jobs += [(("PA", t), "r", t + 1) for t in range(4)]
    jobs += [(("V", j), "vl", j + 1) for j in range(2)]
    jobs += [(("SK", c), "skt", c + 1) for c in range(NT - 1)]
    jobs += [(("RM",), "rdif", 1)]
    jobs += [(("ST", n), "bf", n + 1) for n in range(6)]
    for n in range(-1, 9):
        if n + 1 < 8:
            jobs += [(("PR", n + 1, k), "am", 2 * (n + 1) + k + 1) for k in range(2)]
        if 0 <= n < 8:
            jobs += [(("LO", n), "t6", 3 * n + 3)]
            jobs += [(("ME", n, k), "t6", 3 * n + k + 1) for k in range(2)]
        if 0 <= n - 1 < 8:
            jobs += [(("OT", n - 1), "ol", n)]
    return jobs + tail_jobs()


def tail_jobs():
    jobs = [(("WO", j), "xres", j + 1) for j in range(2)]
    jobs += [(("T", 1, k), "xl", KH + k + 1) for k in range(KH)]
    jobs += [(("UP", m), "hf", m + 1) for m in range(FT)]
    jobs += [(("DN", j), "xffn", j + 1) for j in range(2)]
    return jobs


def jobs2():
    jobs = [(("T", 0, k), "xl", k + 1) for k in range(KH)]
    jobs += [(("PB", t, r), "t12", 2 * t + r + 1) for t in range(4) for r in range(2)]
    jobs += [(("V", j), "vl", j + 1) for j in range(2)]
    for n in range(NH + LAG + 1):
        if n < NH:
            jobs += [(("S1", n, i), "mx", NT * n + i + 1) for i in range(NT)]
        if n >= 4 and n % 4 == 0 and n < NH + 4:
            jobs += [(("NM", n // 4 - 1), "nmt", n // 4)]
        if LAG <= n < NH + LAG:
            jobs += [(("S2", n - LAG, k), "pexp", 3 * (n - LAG) + k + 1) for k in range(3)]
        h = n - LAG - 1
        if h >= 0:
            jobs += [(("PV", h), "tb", h + 1)]
    jobs += [(("OT", half), "ol", half + 1) for half in range(KH)]
    return jobs + tail_jobs()


S2_TILES = [[0], [1, 3], [2]]
S2_COL = [0, 512, 1024]
S2_W = [512, 512, 256]
KT_AT = {0: 0, 1: 512, 3: 512 + 384, 2: 1024}


class Lane:

    def __init__(self, n, per, jobs, banks, sem):
        self.n, self.per, self.jobs, self.banks = n, per, jobs, banks
        self.at = {job: k for k, (job, _, _) in enumerate(jobs)}
        self.s = {name: sem(f"{name}_{n}") for name in per}


def due(L, name, turn, n):
    return turn * L.per[name] + n + 1


def bank_of(L, job):
    return L.banks[L.at[job] % len(L.banks)]


def in_order(a, b):
    pa, pb = next(a), next(b)
    while pa is not None or pb is not None:
        if pb is None or (pa is not None and pa <= pb):
            pa = next(a, None)
        else:
            pb = next(b, None)


def alone(a):
    for _ in a:
        pass


def build(nc, x, wall, mem, gate, w1t, b1t, w2t, b2, cos, sin, out):
    with ExitStack() as ctx:
        def sb(name, shape, dt=F32):
            return ctx.enter_context(nc.sbuf_tensor(name, shape, dt))

        def sem(name):
            return ctx.enter_context(nc.semaphore(name))

        wh = sb("wh", [P, NMAT, KH, H], F16)
        wl = sb("wl", [P, NMAT, KH, H], F16)
        w1q = sb("w1q", [P, KH, FF], F16)
        w2q = sb("w2q", [P, FT, H], F16)
        b1c = sb("b1c", [P, FT])
        b2bc = sb("b2bc", [P, H])
        cost = sb("cost", [P, S])
        sint = sb("sint", [P, S])
        ident = sb("ident", [P, P])
        identh = sb("identh", [P, P], F16)
        identb = sb("identb", [P, P], BF16)
        onesf = sb("onesf", [P, P])
        tri = sb("tri", [P, P])
        mask_qk = sb("mask_qk", [P, P], BF16)
        mask_kq = sb("mask_kq", [P, P], BF16)
        bdmask = sb("bdmask", [P, HH8, VW])
        bmh = sb("bmh", [P, KH, M, HH8, MW], F16)
        bml = sb("bml", [P, KH, M, HH8, MW], F16)
        bnorm = sb("bnorm", [P, KH, M, HH8])
        gates = sb("gates", [P, 4, NH])
        small = sb("small", [P, 16])
        halfc = sb("halfc", [P, NT])
        xa = sb("xa", [P, NT, H])
        xb = sb("xb", [P, NT, H])
        xc = sb("xc", [P, NT, H])

        banks = [ctx.enter_context(nc.psum_tensor(f"bank{n}", [P, 512], F32)) for n in range(8)]
        L1 = Lane(1, PER1, jobs1(), banks[0:4], sem)
        L2 = Lane(2, PER2, jobs2(), banks[4:8], sem)
        for L, parts in ((L1, 4 * S), (L2, 5 * S)):
            def own(name, shape, dt=F32):
                return sb(f"{name}_{L.n}", shape, dt)

            L.stats = own("stats", [P, NT, 6])
            L.tick = own("tick", [P, 1])
            L.ptick = own("ptick", [P, 1])
            L.mv = own("mv", [P, NT, 2])
            L.ve = own("ve", [P, NT])
            L.rstd = own("rstd", [P, NT])
            L.xh = own("xh", [P, KH, S], F16)
            L.xlo = own("xlo", [P, KH, S], F16)
            L.qst = own("qst", [P, NH, S], F16)
            L.kst = own("kst", [P, NH, S], F16)
            L.vp = own("vp", [P, NT, NH, VW], F16)
            L.oth, L.otl = L.xh, L.xlo
            L.place1 = own("place1", [P, parts])
            L.place2 = own("place2", [P, 2 * parts], F16)
            L.place3 = own("place3", [P, 4, S])
            L.place4 = own("place4", [P, 2, S])
            split = L.place1[:, 0:4 * S].bitcast(F16).rearrange("p (r t s) -> p r t s", r=2, t=4)
            L.sth, L.stl = split[:, 0], split[:, 1]
            L.hh = L.place1[:, 0:FT * S // 2].bitcast(F16).rearrange("p (m s) -> p m s", s=S)
            L.hl = L.place2[:, 0:FT * S].rearrange("p (m s) -> p m s", s=S)
            L.sq = L.place3
            L.xn = L.place4[:, :, :].rearrange("p a (b f) -> p (a b) f", f=H)
            L.hf = L.place4
        s1, s2 = L1.s, L2.s
        skt_at = L1.place3[:, :, :].rearrange("p a s -> p (a s)")[:, 0:(NT - 1) * 2 * P]
        skt = skt_at.bitcast(F16).rearrange("p (c a s) -> p c a s", c=NT - 1, a=4)
        ssum = sb("ssum", [P, KH])
        wmax = sb("wmax", [P, NH])
        wdif = sb("wdif", [P, KH, M, HH8])
        wexp = sb("wexp", [P, KH, M, HH8])
        wsum = sb("wsum", [P, NH])
        wrec = sb("wrec", [P, NH])
        wnum = sb("wnum", [P, KH, M, HH8])
        wc = sb("wc", [P, KH, M + 1, HH8])
        bf_from = (NT - 1) * 2 * P
        bf = L1.place3[:, :, :].rearrange("p a s -> p (a s)")[:, bf_from:bf_from + 2 * HH8 * VW]
        bf = bf.rearrange("p (r w) -> p r w", r=2)
        bsh = L1.place4[:, :, :].rearrange("p a s -> p (a s)")[:, 0:3 * HH8 * VW]
        bsh = bsh.bitcast(F16).rearrange("p (n w) -> p n w", n=6)
        bsl = sb("bsl", [P, 6, HH8 * VW], F16)
        am = sb("am", [P, 2, S])
        ebuf = L1.place4
        rbuf = am
        ssb = am[:, 0, 0:KH * P].rearrange("p (a s) -> p a s", a=KH)
        alp = L1.place2[:, 0:4 * S].rearrange("p (r k s) -> p r k s", r=2, k=2)
        ahp = L1.place2[:, 4 * S:8 * S].rearrange("p (r k s) -> p r k s", r=2, k=2)
        den = sb("den", [P, 2, M + 1, HH8])
        drec = sb("drec", [P, 2, M + 1, HH8])
        coef = sb("coef", [P, 2, M + 1, HH8])
        t6 = L1.place3[:, 0:3, :].rearrange("p a s -> p (a s)").rearrange("p (r t s) -> p r t s", r=2, t=M + 2)
        t12 = L2.place4
        pf = L2.place1[:, :].rearrange("p (r n) -> p r n", r=2)
        ph = L2.place2[:, 0:5 * S].rearrange("p (r n) -> p r n", r=2)
        pl = L2.place2[:, 5 * S:10 * S].rearrange("p (r n) -> p r n", r=2)
        tbuf = L2.place3[:, :, :].rearrange("p a s -> p (a s)").rearrange("p (i t h d) -> p i t h d", i=NT, t=2, h=NH)
        nt = sb("nt", [P, 2, NH * NT], F16)
        nmt = sb("nmt", [P, 2, P], F16)
        mxs = sb("mxs", [P, NH * NT])
        prec = sb("prec", [P, 2, NT])

        scratch = nc.dram_tensor("scratch", (2, KH, 2, P, 2, S), F16, kind="Internal").ap()
        for L in (L1, L2):
            L.landed = [sem(f"landed{half}_{L.n}") for half in range(KH)]
            L.scratch = scratch[L.n - 1]

        w_in = sem("w_in")
        f_in = sem("f_in")
        c_in = sem("c_in")
        g_in = sem("g_in")
        m_in = sem("m_in")
        pool_const = sem("pool_const")
        dve_setup = sem("dve_setup")
        act_setup = sem("act_setup")
        pe_setup = sem("pe_setup")
        primed = sem("primed")
        DVE_SETUP = 28
        block = ctx.enter_context(nc.Block())

        x_in, x_out = (t.rearrange("(b j p) f -> b p j f", b=B, p=P) for t in (x, out))

        def sequence(of, t):
            if isinstance(t, int):
                return of[t]
            return of[bass.ds(t, 1)].rearrange("o p j f -> p (o j) f")

        w_stage = [L1.qst, L1.kst]
        w_stage = [t[:, :, :].rearrange("p a b -> p (a b)").bitcast(F32) for t in w_stage]
        f_stage = L2.qst[:, :, :].rearrange("p a b -> p (a b)").bitcast(F32)
        f_tmp = L2.kst[:, :, :].rearrange("p a b -> p (a b)")
        bm_all = L2.place3[:, :, :].rearrange("p a s -> p (a s)")[:, 0:KH * M * HH8 * MW]
        bm = bm_all.rearrange("p (a m h e) -> p a m h e", a=KH, m=M, h=HH8)
        NFW = KH * FF

        @block.sync
        def _(sp):
            sp.dma_start(gates[:, 0, :], gate.broadcast_to([P, NH])).then_inc(g_in, 16)
            sp.dma_start(f_stage[:, 0:NFW].rearrange("p (k f) -> p k f", k=KH),
                         w1t.rearrange("(k p) f -> p k f", p=P)).then_inc(f_in, 16)
            sp.dma_start(f_stage[:, NFW:2 * NFW].rearrange("p (k f) -> p k f", k=FT),
                         w2t.rearrange("(k p) f -> p k f", p=P)).then_inc(f_in, 16)
            wv = wall.rearrange("n (k p) f -> p n k f", p=P)
            for n in range(NMAT):
                at = (n % 8) * KH * H
                sp.dma_start(w_stage[n // 8][:, at:at + KH * H].rearrange("p (k f) -> p k f", k=KH),
                             wv[:, n]).then_inc(w_in, 16)
            sp.dma_start(b1c[:, :], b1t).then_inc(c_in, 16)
            sp.dma_start(b2bc[:, :], b2.broadcast_to([P, H])).then_inc(c_in, 16)
            sp.dma_start(cost[:, :], cos).then_inc(c_in, 16)
            sp.dma_start(sint[:, :], sin).then_inc(c_in, 16)
            sp.wait_ge(pool_const, 1)
            for half in range(KH):
                for h in range(HH8):
                    sp.dma_start(bm[h * D:(h + 1) * D, half, :, h, :], mem[half * HH8 + h]).then_inc(m_in, 16)
            sp.wait_ge(dve_setup, DVE_SETUP)
            sp.wait_ge(primed, 1)

            def stack(L, half, t):
                s = L.s
                if half == 0:
                    sp.wait_ge(s["xt"], due(L, "xt", t, 2))
                sp.wait_ge(s["sh"], due(L, "sh", t, 2 * half + 2))
                sp.wait_ge(s["sl"], due(L, "sl", t, 2 * half + 2))
                for part, src in enumerate((L.sth, L.stl)):
                    sp.dma_start(L.scratch[half, part], src[:, 2 * half:2 * half + 2, :]).then_inc(s["bounced"], 16)
                sp.wait_ge(s["bounced"], due(L, "bounced", t, 32 * (half + 1)))
                heads = slice(half * HH8, (half + 1) * HH8)
                for k, (q_part, k_part) in enumerate(((0, 0), (0, 1), (1, 0), (1, 1))):
                    to = slice(k * D, (k + 1) * D)
                    for dst, part, which in ((L.qst, q_part, 0), (L.kst, k_part, 1)):
                        sp.dma_start(dst[to, heads, :], L.scratch[half, part, :, which, :]
                                     .rearrange("(h d) s -> d h s", d=D)).then_inc(L.landed[half], 16)

            def lane1(t):
                yield mark1("T")
                sp.wait_ge(s1["xffn"], due(L1, "xffn", t, 0))
                sp.dma_start(xa[:, :, :], sequence(x_in, t)).then_inc(s1["xin"], 16)
                for half in range(KH):
                    yield mark1("PA", 2 * half + 1.5)
                    stack(L1, half, t)
                yield None

            def lane2(t):
                for half in range(KH):
                    yield mark2("PB", 2 * half + 1.5)
                    stack(L2, half, t)
                for g in range(NH // NT):
                    yield mark2("N", 4 * g + 4.5)
                    sp.wait_ge(s2["nmt"], due(L2, "nmt", t, g + 1))
                    for part in range(2):
                        at = part * NH * NT + 16 * g
                        sp.dma_start(L2.qst[MAXROW + part:MAXROW + part + 1, NT * g:NT * g + NT, :],
                                     nmt[at:at + 16, g % 2, :]).then_inc(s2["mrow"], 16)
                yield None

            alone(lane1(0))
            with sp.Fori(1, B) as it:
                in_order(lane1(it), lane2(it - 1))
            alone(lane2(B - 1))

        @block.gpsimd
        def _(pool):
            G = nc.gpsimd
            G.memset(bm_all, 0.0).then_inc(pool_const, 1)
            G.memset(ident[:, :], 0.0).then_inc(pool_const, 1)
            G.memset(tri[:, :], 1.0).then_inc(pool_const, 1)
            G.memset(mask_qk[:, :], 0.0).then_inc(pool_const, 1)
            G.memset(mask_kq[:, :], 0.0).then_inc(pool_const, 1)
            G.memset(bdmask[:, :, :], 1.0).then_inc(pool_const, 1)
            G.memset(halfc[:, :], -0.5).then_inc(pool_const, 1)
            G.memset(nt[:, :, :], 0.0).then_inc(pool_const, 1)
            pool.wait_ge(pool_const, 8)
            G.affine_select(out=ident[:, :], in_=ident[:, :], compare_op=ALU.not_equal, fill=1.0, base=0,
                            pattern=[[-1, P]], channel_multiplier=1).then_inc(pool_const, 1)
            G.affine_select(out=tri[:, :], in_=tri[:, :], compare_op=ALU.is_ge, fill=0.0, base=0,
                            pattern=[[1, P]], channel_multiplier=-1).then_inc(pool_const, 1)
            G.affine_select(out=mask_qk[:, :], in_=mask_qk[:, :], compare_op=ALU.is_ge, fill=MASKED, base=0,
                            pattern=[[-1, P]], channel_multiplier=1).then_inc(pool_const, 1)
            G.affine_select(out=mask_kq[:, :], in_=mask_kq[:, :], compare_op=ALU.is_ge, fill=MASKED, base=0,
                            pattern=[[1, P]], channel_multiplier=-1).then_inc(pool_const, 1)
            G.affine_select(out=bdmask[:, :, :], in_=bdmask[:, :, :], compare_op=ALU.is_ge, fill=0.0, base=0,
                            pattern=[[-D, HH8], [0, VW]], channel_multiplier=1).then_inc(pool_const, 1)
            pool.wait_ge(pool_const, 13)
            G.affine_select(out=bdmask[:, :, :], in_=bdmask[:, :, :], compare_op=ALU.is_ge, fill=0.0,
                            base=D - 1, pattern=[[D, HH8], [0, VW]], channel_multiplier=-1).then_inc(pool_const, 1)
            pool.wait_ge(c_in, 64)
            pool.wait_ge(pool_const, 14)
            pool.wait_ge(dve_setup, DVE_SETUP)
            for L in (L1, L2):
                for name in L.per:
                    G.sem_inc(L.s[name], 1)
            G.drain().then_inc(primed, 1)

            def norm(L, u, X, t):
                s = L.s
                pool.wait_ge(s["ve"], due(L, "ve", t, u + 1))
                G.tensor_tensor(L.rstd[:, :], L.ve[:, :], halfc[:, :], ALU.pow).then_inc(s["rstd"], 1)
                pool.wait_ge(s["rstd"], due(L, "rstd", t, u + 1))
                G.tensor_tensor(L.ptick[:, :], halfc[:, 0:1], halfc[:, 0:1], ALU.mult).then_inc(s["ptick"], 1)
                for j in range(NT):
                    G.tensor_scalar(L.xn[:, j, :], X[:, j, :], L.mv[:, j, 0:1], L.rstd[:, j:j + 1],
                                    ALU.subtract, ALU.mult).then_inc(s["xn"], 1)

            def ffn(L, X, mark, t):
                s = L.s
                yield mark("FT")
                norm(L, 1, X, t)
                yield mark("UP")
                pool.wait_ge(s["xn"], due(L, "xn", t, 2 * NT))
                G.tensor_tensor(X[:, :, :], X[:, :, :],
                                b2bc[:, :].rearrange("p (a f) -> p a f", a=1).broadcast_to([P, NT, H]),
                                ALU.add).then_inc(s["xb"], 1)
                for m in range(0, FT, 2):
                    yield mark("UP", m)
                    pool.wait_ge(s["hh"], due(L, "hh", t, m + 1))
                    G.tensor_tensor(L.hl[:, m, :], L.hf[:, 0, :], L.hh[:, m, :], ALU.subtract).then_inc(s["hl_pool"], 1)

            def lane1(t):
                s = s1
                yield mark1("T")
                norm(L1, 0, xa, t)
                for q in range(4):
                    yield mark1("PA", q + 1)
                    pool.wait_ge(s["sh"], due(L1, "sh", t, q + 1))
                    G.tensor_tensor(L1.stl[:, q, :], L1.sq[:, q, :], L1.sth[:, q, :], ALU.subtract).then_inc(s["sl"], 1)
                for n in range(6):
                    yield mark1("ST", n)
                    pool.wait_ge(s["bh"], due(L1, "bh", t, n + 1))
                    G.tensor_tensor(bsl[:, n, :], bf[:, n % 2, :], bsh[:, n, :], ALU.subtract).then_inc(s["bl"], 1)
                for n in range(8):
                    yield mark1("N", n)
                    pool.wait_ge(s["ah"], due(L1, "ah", t, 2 * n + 1))
                    if n >= 2:
                        pool.wait_ge(s["om"], due(L1, "om", t, 3 * (n - 1)))
                    G.tensor_tensor(alp[:, n % 2, 0, :], am[:, 0, :], ahp[:, n % 2, 0, :],
                                    ALU.subtract).then_inc(s["al_pool"], 1)
                yield from ffn(L1, xa, mark1, t)
                yield None

            def lane2(t):
                s = s2
                yield mark2("T")
                norm(L2, 0, xb, t)
                for q in range(4):
                    yield mark2("PB", q)
                    pool.wait_ge(s["t12"], due(L2, "t12", t, 2 * q + 2))
                    G.tensor_tensor(L2.sq[:, q, :], t12[:, 0, :], t12[:, 1, :], ALU.add).then_inc(s["y"], 1)
                for h in range(NH):
                    yield mark2("N", h + LAG)
                    for n in range(2):
                        a, b = S2_COL[n], S2_COL[n + 1]
                        pool.wait_ge(s["phi"], due(L2, "phi", t, 3 * h + n + 1))
                        G.tensor_tensor(pl[:, h % 2, a:b], pf[:, h % 2, a:b], ph[:, h % 2, a:b],
                                        ALU.subtract).then_inc(s["plo_pool"], 1)
                yield from ffn(L2, xc, mark2, t)
                yield None

            alone(lane1(0))
            with pool.Fori(1, B) as it:
                in_order(lane1(it), lane2(it - 1))
            alone(lane2(B - 1))

        @block.scalar
        def _(act):
            A = nc.scalar
            act.wait_ge(g_in, 16)
            A.activation(gates[:, 1, :], gates[:, 0, :], ACT.Exp, scale=-1.0).then_inc(act_setup, 1)
            act.wait_ge(f_in, 32)
            for n in range(2):
                A.activation(f_tmp[:, n * NFW:(n + 1) * NFW], f_stage[:, n * NFW:(n + 1) * NFW], ACT.Abs,
                             accum_out=small[:, n:n + 1]).then_inc(act_setup, 1)
            act.wait_ge(dve_setup, DVE_SETUP)
            act.wait_ge(primed, 1)

            def turned(L, u, t):
                s = L.s
                for k in range(KH):
                    act.wait_ge(s["xt"], due(L, "xt", t, 2 * u + k + 1))
                    A.activation(L.xh[:, k, :], bank_of(L, ("T", u, k))[:, :], ACT.Copy).then_inc(s["xh"], 1)

            def values(L, j, t):
                act.wait_ge(L.s["v"], due(L, "v", t, j + 1))
                A.activation(L.vp[:, 2 * j:2 * j + 2, :, 0:D],
                             bank_of(L, ("V", j))[:, :].rearrange("p (c h d) -> p c h d", c=2, d=D),
                             ACT.Copy, scale=VS / WS).then_inc(L.s["vh"], 1)

            def ffn(L, mark, t):
                s = L.s
                yield mark("FT")
                turned(L, 1, t)
                for m in range(FT):
                    yield mark("UP", m)
                    act.wait_ge(s["up"], due(L, "up", t, m + 1))
                    if m >= 2:
                        name = "hl_dve" if m % 2 else "hl_pool"
                        act.wait_ge(s[name], due(L, name, t, m // 2))
                    A.activation(L.hf[:, m % 2, :], bank_of(L, ("UP", m))[:, :], ACT.Relu,
                                 bias=b1c[:, m:m + 1]).then_inc(s["hf"], 1)
                    act.wait_ge(s["hf"], due(L, "hf", t, m + 1))
                    A.activation(L.hh[:, m, :], L.hf[:, m % 2, :], ACT.Copy).then_inc(s["hh"], 1)

            def lane1(t):
                s = s1
                yield mark1("T")
                turned(L1, 0, t)
                for q in range(4):
                    yield mark1("PA", q)
                    act.wait_ge(s["proj"], due(L1, "proj", t, q + 1))
                    if q >= 2:
                        act.wait_ge(s["sq"], due(L1, "sq", t, q - 1))
                    A.activation(ebuf[:, q % 2, :], bank_of(L1, ("PA", q))[:, :], ACT.Exp,
                                 scale=1 / WS).then_inc(s["e"], 1)
                    if q >= 1:
                        act.wait_ge(s["sq"], due(L1, "sq", t, q))
                        A.activation(L1.sth[:, q - 1, :], L1.sq[:, q - 1, :], ACT.Copy).then_inc(s["sh"], 1)
                yield mark1("PA", 4)
                act.wait_ge(s["sq"], due(L1, "sq", t, 4))
                A.activation(L1.sth[:, 3, :], L1.sq[:, 3, :], ACT.Copy).then_inc(s["sh"], 1)
                for j in range(2):
                    yield mark1("V", j)
                    values(L1, j, t)
                for c in range(NT - 1):
                    yield mark1("SK")
                    act.wait_ge(s["sk"], due(L1, "sk", t, c + 1))
                    A.activation(skt[:, c, :, :].rearrange("p a b -> p (a b)"),
                                 bank_of(L1, ("SK", c))[:, :].bitcast(F16)[:, 0:4 * P], ACT.Copy).then_inc(s["skt"], 1)
                yield mark1("RM")
                act.wait_ge(s["rdif"], due(L1, "rdif", t, 1))
                A.activation(wexp[:, :, :, :], wdif[:, :, :, :], ACT.Exp, scale=1.0 / S).then_inc(s["rexp"], 1)
                for n in range(6):
                    yield mark1("ST", n)
                    act.wait_ge(s["bf"], due(L1, "bf", t, n + 1))
                    A.activation(bsh[:, n, :], bf[:, n % 2, :], ACT.Copy).then_inc(s["bh"], 1)
                for n in range(10):
                    yield mark1("N", n)
                    if n < 8:
                        for k in range(2):
                            act.wait_ge(s["am"], due(L1, "am", t, 2 * n + k + 1))
                            if n >= 2 and k == 0:
                                act.wait_ge(s["om"], due(L1, "om", t, 3 * (n - 1)))
                            A.activation(ahp[:, n % 2, k, :], am[:, k, :], ACT.Copy).then_inc(s["ah"], 1)
                    if n >= 2:
                        half, c = divmod(n - 2, NT)
                        act.wait_ge(s["ot"], due(L1, "ot", t, n - 1))
                        A.activation(L1.oth[:, half, c * P:(c + 1) * P], bank_of(L1, ("OT", n - 2))[:, 0:P],
                                     ACT.Copy).then_inc(s["oh"], 1)
                yield from ffn(L1, mark1, t)
                yield None

            def lane2(t):
                s = s2
                yield mark2("T")
                turned(L2, 0, t)
                for q in range(4):
                    yield mark2("PB", q + 0.5)
                    act.wait_ge(s["y"], due(L2, "y", t, q + 1))
                    A.activation(L2.sth[:, q, :], L2.sq[:, q, :], ACT.Copy).then_inc(s["sh"], 1)
                for j in range(2):
                    yield mark2("V", j)
                    values(L2, j, t)
                for n in range(4, NH + LAG):
                    yield mark2("N", n)
                    if n % NT == 0 and n < NH + NT:
                        g = n // NT - 1
                        act.wait_ge(s["nm"], due(L2, "nm", t, g + 1))
                        if g >= 2:
                            act.wait_ge(s["mrow"], due(L2, "mrow", t, 32 * (g - 1)))
                        A.activation(nmt[:, g % 2, :], bank_of(L2, ("NM", g))[:, :].bitcast(F16)[:, 0:P],
                                     ACT.Copy).then_inc(s["nmt"], 1)
                    h = n - LAG
                    if h < 0:
                        continue
                    if h >= 2:
                        act.wait_ge(s["plo_pool"], due(L2, "plo_pool", t, 2 * (h - 1)))
                        act.wait_ge(s["plo_dve"], due(L2, "plo_dve", t, h - 1))
                    for k in range(3):
                        act.wait_ge(s["s2"], due(L2, "s2", t, 3 * h + k + 1))
                        A.activation(pf[:, h % 2, S2_COL[k]:S2_COL[k] + S2_W[k]], bank_of(L2, ("S2", h, k))[:, 0:S2_W[k]],
                                     ACT.Exp, scale=D ** -0.5 / RS ** 2).then_inc(s["pexp"], 1)
                    for k in range(3):
                        at = slice(S2_COL[k], S2_COL[k] + S2_W[k])
                        act.wait_ge(s["pexp"], due(L2, "pexp", t, 3 * h + k + 1))
                        if h >= 2:
                            act.wait_ge(s["pv"], due(L2, "pv", t, h - 1))
                        A.activation(ph[:, h % 2, at], pf[:, h % 2, at], ACT.Copy).then_inc(s["phi"], 1)
                for half in range(KH):
                    yield mark2("OT", half)
                    act.wait_ge(s["ot"], due(L2, "ot", t, half + 1))
                    A.activation(L2.oth[:, half, :], bank_of(L2, ("OT", half))[:, :], ACT.Copy).then_inc(s["oh"], 1)
                yield from ffn(L2, mark2, t)
                yield mark2("END")
                act.wait_ge(s["xffn"], due(L2, "xffn", t, 2))
                act.dma_start(sequence(x_out, t), xc[:, :, :]).then_inc(s["store"], 16)
                yield None

            alone(lane1(0))
            with act.Fori(1, B) as it:
                in_order(lane1(it), lane2(it - 1))
            alone(lane2(B - 1))
            act.wait_ge(s2["store"], 16 * B + 1)

        @block.vector
        def _(dve):
            chain = [0]
            V = nc.vector

            def link(ins):
                chain[0] += 1
                ins.then_inc(dve_setup, 1)
                dve.wait_ge(dve_setup, chain[0])

            link(V.memset(onesf[:, :], 1.0))
            for L in (L1, L2):
                link(V.memset(L.vp[:, :, :, 2 * D:VW], 1.0))
            dve.wait_ge(w_in, 16 * NMAT)
            for stage, at, n in ((w_stage[0], 0, 8), (w_stage[1], 8, 2)):
                cols = n * KH * H
                hi = wh[:, at:at + n, :, :].rearrange("p n k f -> p (n k f)")
                lo = wl[:, at:at + n, :, :].rearrange("p n k f -> p (n k f)")
                link(V.tensor_scalar(hi, stage[:, 0:cols], WS, None, ALU.mult))
                link(V.scalar_tensor_tensor(lo, stage[:, 0:cols], WS, hi, ALU.mult, ALU.subtract))
            dve.wait_ge(act_setup, 3)
            link(V.tensor_scalar(gates[:, 1, :], gates[:, 1, :], 1.0, None, ALU.add))
            link(V.reciprocal(gates[:, 2, :], gates[:, 1, :]))
            link(V.tensor_scalar(wc[:, :, M, :], gates[:, 2, :].rearrange("p (a h) -> p a h", a=KH), -1.0, 1.0,
                                 ALU.mult, ALU.add))
            link(V.tensor_scalar(gates[:, 3, :], gates[:, 2, :], VS, None, ALU.mult))
            dve.wait_ge(pe_setup, 1)
            link(V.tensor_scalar(small[:, 2:4], banks[0][:, 0:2], 1.0 / (H * FF), Q_EPS, ALU.mult, ALU.add))
            link(V.tensor_scalar(small[:, 4:6], small[:, 2:4], 0.5, None, ALU.mult))
            link(V.tensor_scalar(small[:, 6:8], small[:, 2:4], -0.5, None, ALU.mult))
            for n, w in enumerate((w1q[:, :, :].rearrange("p a b -> p (a b)"), w2q[:, :, :].rearrange("p a b -> p (a b)"))):
                stage = f_stage[:, n * NFW:(n + 1) * NFW]
                below = f_tmp[:, n * NFW:(n + 1) * NFW]
                link(V.tensor_scalar(below, stage, small[:, 6 + n:7 + n], None, ALU.is_lt))
                link(V.scalar_tensor_tensor(w, stage, small[:, 4 + n:5 + n], below, ALU.is_gt, ALU.subtract))
            dve.wait_ge(pool_const, 14)
            link(V.tensor_copy(identh[:, :], ident[:, :]))
            link(V.tensor_copy(identb[:, :], ident[:, :]))
            for L in (L1, L2):
                for st in (L.qst, L.kst):
                    V.memset(st[PARTS:P, :, :], 0.0).then_inc(dve_setup, 1)
                    chain[0] += 1
            dve.wait_ge(dve_setup, chain[0])
            V.memset(L2.kst[MAXROW:MAXROW + 2, :, :], SHIFT).then_inc(dve_setup, 1)
            chain[0] += 1
            dve.wait_ge(m_in, 16 * NH)
            bmh_all = bmh[:, :, :, :, :].rearrange("p a m h e -> p (a m h e)")
            bml_all = bml[:, :, :, :, :].rearrange("p a m h e -> p (a m h e)")
            link(V.tensor_copy(bmh_all, bm_all))
            link(V.tensor_tensor(bml_all, bm_all, bmh_all, ALU.subtract))
            link(V.tensor_copy(bnorm[:, :, :, :].rearrange("p a m h -> p (a m h)"),
                               bm_all.rearrange("p (n e) -> p n e", e=MW)[:, :, D]))
            assert chain[0] == DVE_SETUP, chain[0]
            dve.wait_ge(primed, 1)

            def norm(L, u, X, t):
                s = L.s
                for j in range(NT):
                    V.bn_stats(L.stats[:, j, :], X[:, j, :]).then_inc(s["bn"], 1)
                dve.wait_ge(s["bn"], due(L, "bn", t, NT * (u + 1)))
                V.memset(L.tick[:, :], 0.0).then_inc(s["tick"], 1)
                for j in range(NT):
                    V.bn_aggr(L.mv[:, j, :], L.stats[:, j, :]).then_inc(s["mv"], 1)
                dve.wait_ge(s["mv"], due(L, "mv", t, NT * (u + 1)))
                V.tensor_scalar(L.ve[:, :], L.mv[:, :, 1], LN_EPS, None, ALU.add).then_inc(s["ve"], 1)

            def low_parts(L, u, t):
                s = L.s
                for k in range(KH):
                    dve.wait_ge(s["xh"], due(L, "xh", t, 2 * u + k + 1))
                    V.tensor_tensor(L.xlo[:, k, :], bank_of(L, ("T", u, k))[:, :], L.xh[:, k, :],
                                    ALU.subtract).then_inc(s["xl"], 1)

            def values(L, j, t):
                dve.wait_ge(L.s["vh"], due(L, "vh", t, j + 1))
                for c in range(2):
                    ins = V.scalar_tensor_tensor(
                        L.vp[:, 2 * j + c, :, D:2 * D],
                        bank_of(L, ("V", j))[:, c * H:(c + 1) * H].rearrange("p (h d) -> p h d", d=D),
                        VS / WS, L.vp[:, 2 * j + c, :, 0:D], ALU.mult, ALU.subtract)
                ins.then_inc(L.s["vl"], 1)

            def add_attention(L, j, X, Y, t):
                s = L.s
                dve.wait_ge(s["wo"], due(L, "wo", t, j + 1))
                two = slice(2 * j, 2 * j + 2)
                V.scalar_tensor_tensor(Y[:, two, :], bank_of(L, ("WO", j))[:, :].rearrange("p (a f) -> p a f", a=2),
                                       1 / (WS * VS), X[:, two, :], ALU.mult, ALU.add).then_inc(s["xres"], 1)

            def ffn(L, X, Y, mark, t):
                s = L.s
                yield mark("FT")
                dve.wait_ge(s["xres"], due(L, "xres", t, 2))
                norm(L, 1, X, t)
                low_parts(L, 1, t)
                for m in range(1, FT, 2):
                    yield mark("UP", m)
                    dve.wait_ge(s["hh"], due(L, "hh", t, m + 1))
                    V.tensor_tensor(L.hl[:, m, :], L.hf[:, 1, :], L.hh[:, m, :], ALU.subtract).then_inc(s["hl_dve"], 1)
                for j in range(2):
                    yield mark("DN", j)
                    if j == 0:
                        dve.wait_ge(s["xb"], due(L, "xb", t, 1))
                        if L is L1 and not (isinstance(t, int) and t == 0):
                            dve.wait_ge(s2["xres"], due(L2, "xres", t - 1, 2))
                    dve.wait_ge(s["dn"], due(L, "dn", t, j + 1))
                    two = slice(2 * j, 2 * j + 2)
                    V.tensor_tensor(Y[:, two, :], bank_of(L, ("DN", j))[:, :].rearrange("p (a f) -> p a f", a=2),
                                    X[:, two, :], ALU.add).then_inc(s["xffn"], 1)

            def causal(n, t):
                s = s1
                for k in range(2):
                    dve.wait_ge(s["a"], due(L1, "a", t, 2 * n + k + 1))
                    if n >= 1:
                        name = "al_dve" if k else "al_pool"
                        dve.wait_ge(s[name], due(L1, name, t, n))
                    V.scalar_tensor_tensor(am[:, k, :].rearrange("p (c s) -> p c s", c=NT),
                                           bank_of(L1, ("PR", n, k))[:, :].rearrange("p (c s) -> p c s", c=NT), AS,
                                           tri[:, :].rearrange("p (c s) -> p c s", c=1).broadcast_to([P, NT, P]),
                                           ALU.mult, ALU.mult).then_inc(s["am"], 1)

            def causal_low(n, t):
                s = s1
                dve.wait_ge(s["ah"], due(L1, "ah", t, 2 * n + 2))
                if n >= 2:
                    dve.wait_ge(s["om"], due(L1, "om", t, 3 * (n - 1)))
                V.tensor_tensor(alp[:, n % 2, 1, :], am[:, 1, :], ahp[:, n % 2, 1, :],
                                ALU.subtract).then_inc(s["al_dve"], 1)

            def combine(n, t):
                s = s1
                half, r = n // NT, n % 2
                local = bank_of(L1, ("LO", n))[:, 0:HH8 * VW].rearrange("p (h w) -> p h w", w=VW)
                pairs = [bank_of(L1, ("ME", n, k))[:, 0:2 * HH8 * MW] for k in range(2)]
                dve.wait_ge(s["om"], due(L1, "om", t, 3 * n + 1))
                V.tensor_scalar(den[:, r, M, :], local[:, :, 2 * D], MEM_EPS * AS, None, ALU.max).then_inc(s["clip"], 1)
                for k in range(2):
                    dve.wait_ge(s["om"], due(L1, "om", t, 3 * n + 2 + k))
                    V.tensor_scalar(den[:, r, 2 * k:2 * k + 2, :],
                                    pairs[k].rearrange("p (m h w) -> p m h w", m=2, w=MW)[:, :, :, D],
                                    MEM_EPS, None, ALU.max).then_inc(s["clip"], 1)
                dve.wait_ge(s["clip"], due(L1, "clip", t, 3 * n + 3))
                V.reciprocal(drec[:, r, :, :], den[:, r, :, :]).then_inc(s["rec"], 1)
                dve.wait_ge(s["rec"], due(L1, "rec", t, n + 1))
                V.tensor_tensor(coef[:, r, :, :], drec[:, r, :, :], wc[:, half, :, :], ALU.mult).then_inc(s["coef"], 1)
                dve.wait_ge(s["coef"], due(L1, "coef", t, n + 1))
                if n >= 2:
                    dve.wait_ge(s["ot"], due(L1, "ot", t, n - 1))
                for k in range(2):
                    V.tensor_tensor(t6[:, r, 2 * k:2 * k + 2, :].rearrange("p m (h d) -> p (m h) d", d=D),
                                    pairs[k].rearrange("p (m w) -> p m w", w=MW)[:, :, 0:D],
                                    coef[:, r, 2 * k:2 * k + 2, :].rearrange("p m (h o) -> p (m h) o", o=1)
                                    .broadcast_to([P, 2 * HH8, D]), ALU.mult).then_inc(s["t6"], 1)
                V.tensor_tensor(t6[:, r, M:M + 2, :].rearrange("p t (h d) -> p t h d", d=D),
                                local[:, :, 0:2 * D].rearrange("p h (t d) -> p t h d", t=2),
                                coef[:, r, M:M + 1, :].rearrange("p t (h o) -> p t h o", o=1)
                                .broadcast_to([P, 2, HH8, D]), ALU.mult).then_inc(s["t6"], 1)

            def heads_low(L, job, n, at, t):
                s = L.s
                dve.wait_ge(s["oh"], due(L, "oh", t, n + 1))
                half, cols = at
                V.tensor_tensor(L.otl[:, half, cols], bank_of(L, job)[:, 0:cols.stop - cols.start], L.oth[:, half, cols],
                                ALU.subtract).then_inc(s["ol"], 1)

            def memory_weights(t):
                s = s1
                dve.wait_ge(s["rm"], due(L1, "rm", t, 1))
                rm = bank_of(L1, ("RM",))[:, 0:KH * M * HH8].rearrange("p (a m h) -> p a m h", a=KH, m=M)
                V.tensor_reduce(wmax[:, :].rearrange("p (a h) -> p a h", a=KH), rm.rearrange("p a m h -> p a h m"),
                                AX, ALU.max).then_inc(s["rmax"], 1)
                dve.wait_ge(s["rmax"], due(L1, "rmax", t, 1))
                V.tensor_tensor(wdif[:, :, :, :], rm, wmax[:, :].rearrange("p (a m h) -> p a m h", a=KH, m=1)
                                .broadcast_to([P, KH, M, HH8]), ALU.subtract).then_inc(s["rdif"], 1)

            def memory_weights_end(t):
                s = s1
                dve.wait_ge(s["rexp"], due(L1, "rexp", t, 1))
                V.tensor_reduce(wsum[:, :].rearrange("p (a h) -> p a h", a=KH),
                                wexp[:, :, :, :].rearrange("p a m h -> p a h m"), AX, ALU.add).then_inc(s["rsum"], 1)
                dve.wait_ge(s["rsum"], due(L1, "rsum", t, 1))
                V.reciprocal(wrec[:, :], wsum[:, :]).then_inc(s["rrec"], 1)
                dve.wait_ge(s["rrec"], due(L1, "rrec", t, 1))
                V.tensor_tensor(wnum[:, :, :, :], wexp[:, :, :, :],
                                wrec[:, :].rearrange("p (a m h) -> p a m h", a=KH, m=1)
                                .broadcast_to([P, KH, M, HH8]), ALU.mult).then_inc(s["rcoef"], 1)
                dve.wait_ge(s["rcoef"], due(L1, "rcoef", t, 1))
                V.tensor_tensor(wc[:, :, 0:M, :], wnum[:, :, :, :],
                                gates[:, 3, :].rearrange("p (a m h) -> p a m h", a=KH, m=1)
                                .broadcast_to([P, KH, M, HH8]), ALU.mult).then_inc(s["rcoef"], 1)
                dve.wait_ge(s["rcoef"], due(L1, "rcoef", t, 2))

            def lane1(t):
                s = s1
                yield mark1("T")
                dve.wait_ge(s["xin"], due(L1, "xin", t, 16))
                norm(L1, 0, xa, t)
                low_parts(L1, 0, t)
                for q in range(4):
                    yield mark1("PA", q)
                    dve.wait_ge(s["e"], due(L1, "e", t, q + 1))
                    V.tensor_scalar(rbuf[:, q % 2, :], bank_of(L1, ("PA", q))[:, :], 1 / WS, 0.0,
                                    ALU.mult, ALU.max).then_inc(s["r"], 1)
                    dve.wait_ge(s["r"], due(L1, "r", t, q + 1))
                    V.scalar_tensor_tensor(L1.sq[:, q, :], ebuf[:, q % 2, :], 1.0, rbuf[:, q % 2, :], ALU.min, ALU.add,
                                           accum_out=ssum[:, q // 2:q // 2 + 1] if q % 2 == 0 else None
                                           ).then_inc(s["sq"], 1)
                yield mark1("PA", 4)
                dve.wait_ge(s["sq"], due(L1, "sq", t, 4))
                for half in range(KH):
                    V.tensor_scalar(ssb[:, half, :], onesf[:, :], ssum[:, half:half + 1], None,
                                    ALU.mult).then_inc(s["ssb"], 1)
                for j in range(2):
                    yield mark1("V", j)
                    values(L1, j, t)
                yield mark1("RM")
                memory_weights(t)
                for n in range(6):
                    yield mark1("ST", n)
                    dve.wait_ge(s["st"], due(L1, "st", t, n + 1))
                    if n >= 2:
                        dve.wait_ge(s["bl"], due(L1, "bl", t, n - 1))
                    V.scalar_tensor_tensor(bf[:, n % 2, :], bank_of(L1, ("ST", n))[:, 0:HH8 * VW], AS,
                                           bdmask[:, :, :].rearrange("p h w -> p (h w)"),
                                           ALU.mult, ALU.mult).then_inc(s["bf"], 1)
                memory_weights_end(t)
                for n in range(11):
                    yield mark1("N", n)
                    if n < 8:
                        causal(n, t)
                    if 1 <= n < 9:
                        combine(n - 1, t)
                    if n < 8:
                        causal_low(n, t)
                    if 2 <= n < 10:
                        half, c = divmod(n - 2, NT)
                        heads_low(L1, ("OT", n - 2), n - 2, (half, slice(c * P, (c + 1) * P)), t)
                for j in range(2):
                    yield mark1("WO", j)
                    add_attention(L1, j, xa, xa, t)
                yield from ffn(L1, xa, xb, mark1, t)
                yield None

            def head_out(h, t):
                s = s2
                dve.wait_ge(s["pv"], due(L2, "pv", t, h + 1))
                ps = bank_of(L2, ("PV", h))[:, 0:NT * VW].rearrange("p (i w) -> p i w", w=VW)
                V.reciprocal(prec[:, h % 2, :], ps[:, :, 2 * D]).then_inc(s["prec"], 1)
                dve.wait_ge(s["prec"], due(L2, "prec", t, h + 1))
                V.tensor_tensor(tbuf[:, :, :, h, :], ps[:, :, 0:2 * D].rearrange("p i (t d) -> p i t d", t=2),
                                prec[:, h % 2, :].rearrange("p (i t o) -> p i t o", t=1, o=1)
                                .broadcast_to([P, NT, 2, D]), ALU.mult).then_inc(s["tb"], 1)

            def lane2(t):
                s = s2
                yield mark2("T")
                dve.wait_ge(s1["xffn"], due(L1, "xffn", t, 2))
                norm(L2, 0, xb, t)
                low_parts(L2, 0, t)
                for q in range(4):
                    yield mark2("PB", q)
                    for r in range(2):
                        dve.wait_ge(s["pr"], due(L2, "pr", t, 2 * q + r + 1))
                        if q >= 1 and r == 0:
                            dve.wait_ge(s["y"], due(L2, "y", t, q))
                        V.scalar_tensor_tensor(t12[:, r, :], bank_of(L2, ("PB", q, r))[:, :], RS / WS,
                                               (cost, sint)[r][:, :], ALU.mult, ALU.mult).then_inc(s["t12"], 1)
                    if q >= 1:
                        dve.wait_ge(s["sh"], due(L2, "sh", t, q))
                        V.tensor_tensor(L2.stl[:, q - 1, :], L2.sq[:, q - 1, :], L2.sth[:, q - 1, :],
                                        ALU.subtract).then_inc(s["sl"], 1)
                yield mark2("PB", 4)
                dve.wait_ge(s["sh"], due(L2, "sh", t, 4))
                V.tensor_tensor(L2.stl[:, 3, :], L2.sq[:, 3, :], L2.sth[:, 3, :], ALU.subtract).then_inc(s["sl"], 1)
                for j in range(2):
                    yield mark2("V", j)
                    values(L2, j, t)
                for n in range(NH + LAG + 1 + 1):
                    yield mark2("N", n)
                    h = n - LAG
                    if h >= 2:
                        head_out(h - 2, t)
                    if n < NH:
                        for i in range(NT):
                            g = NT * n + i
                            dve.wait_ge(s["s1"], due(L2, "s1", t, g + 1))
                            V.tensor_reduce(mxs[:, g:g + 1], bank_of(L2, ("S1", n, i))[:, 0:(i + 1) * P], AX,
                                            ALU.max).then_inc(s["mx"], 1)
                        if n % NT == NT - 1:
                            q = n // NT
                            gs = slice(16 * q, 16 * q + 16)
                            dve.wait_ge(s["mx"], due(L2, "mx", t, 16 * (q + 1)))
                            dve.wait_ge(s["nm"], due(L2, "nm", t, q))
                            V.tensor_scalar(nt[:, 0, gs], mxs[:, gs], -1.0 / SHIFT, None, ALU.mult).then_inc(s["nh"], 1)
                            dve.wait_ge(s["nh"], due(L2, "nh", t, q + 1))
                            V.scalar_tensor_tensor(nt[:, 1, gs], mxs[:, gs], -1.0 / SHIFT, nt[:, 0, gs],
                                                   ALU.mult, ALU.subtract).then_inc(s["nl"], 1)
                    if 0 <= h < NH:
                        if h >= 2:
                            dve.wait_ge(s["pv"], due(L2, "pv", t, h - 1))
                        dve.wait_ge(s["phi"], due(L2, "phi", t, 3 * h + 3))
                        V.tensor_tensor(pl[:, h % 2, 1024:1280], pf[:, h % 2, 1024:1280], ph[:, h % 2, 1024:1280],
                                        ALU.subtract).then_inc(s["plo_dve"], 1)
                for half in range(KH):
                    yield mark2("OT", half)
                    heads_low(L2, ("OT", half), half, (half, slice(0, S)), t)
                for j in range(2):
                    yield mark2("WO", j)
                    if j == 0:
                        dve.wait_ge(s["store"], due(L2, "store", t, 0))
                    add_attention(L2, j, xb, xc, t)
                yield from ffn(L2, xc, xc, mark2, t)
                yield None

            alone(lane1(0))
            with dve.Fori(1, B) as it:
                in_order(lane1(it), lane2(it - 1))
            alone(lane2(B - 1))

        @block.tensor
        def _(pe):
            T = nc.tensor
            pe.wait_ge(act_setup, 3)
            pe.wait_ge(dve_setup, 1)
            T.matmul(banks[0][:, 0:2], onesf[:, :], small[:, 0:2], start=True, stop=True).then_inc(pe_setup, 1)
            pe.wait_ge(dve_setup, DVE_SETUP)
            pe.wait_ge(primed, 1)

            def take(L, job, t):
                n, ring = L.at[job], len(L.banks)
                if n >= ring:
                    _, name, count = L.jobs[n - ring]
                    pe.wait_ge(L.s[name], due(L, name, t, count))
                else:
                    last = max(k for k in range(len(L.jobs)) if k % ring == n)
                    name = L.jobs[last][1]
                    pe.wait_ge(L.s[name], due(L, name, t, 0))
                return bank_of(L, job)

            def turn(L, u, t):
                s = L.s
                into = [take(L, ("T", u, k), t) for k in range(KH)]
                for j in range(NT):
                    pe.wait_ge(s["xn"], due(L, "xn", t, NT * u + j + 1))
                    for k in range(KH):
                        ins = T.transpose(into[k][:, j * P:(j + 1) * P], L.xn[:, j, k * P:(k + 1) * P], ident[:, :])
                        if j == NT - 1:
                            ins.then_inc(s["xt"], 1)

            def project(L, job, mat, m, name, t):
                into = take(L, job, t)
                n = 0
                for w, a in ((wh, L.xh), (wl, L.xh), (wh, L.xlo)):
                    for k in range(KH):
                        ins = T.matmul(into[:, :], w[:, mat, k, m * P:(m + 1) * P], a[:, k, :],
                                       start=(n == 0), stop=(n == 5))
                        n += 1
                ins.then_inc(L.s[name], 1)

            def rows(L, job, high, low, mat, name, t):
                into = take(L, job, t)
                for a in range(2):
                    n = 0
                    cols = slice((2 * job[-1] + a) * P, (2 * job[-1] + a + 1) * P)
                    for w, part in ((wh, high), (wl, high), (wh, low)):
                        for k in range(KH):
                            ins = T.matmul(into[:, a * H:(a + 1) * H], part[:, k, cols], w[:, mat, k, :],
                                           start=(n == 0), stop=(n == 5))
                            n += 1
                ins.then_inc(L.s[name], 1)

            def project_out(L, mat, mark, t):
                s = L.s
                for j in range(2):
                    yield mark("WO", j)
                    if j == 0:
                        pe.wait_ge(s["ol"], due(L, "ol", t, L.per["ol"]))
                    rows(L, ("WO", j), L.oth, L.otl, mat, "wo", t)

            def ffn(L, mark, t):
                s = L.s
                yield mark("FT")
                turn(L, 1, t)
                for m in range(FT):
                    yield mark("UP", m)
                    if m == 0:
                        pe.wait_ge(s["xl"], due(L, "xl", t, 4))
                    into = take(L, ("UP", m), t)
                    for n, (a, k) in enumerate(((L.xh, 0), (L.xh, 1), (L.xlo, 0), (L.xlo, 1))):
                        ins = T.matmul(into[:, :], w1q[:, k, m * P:(m + 1) * P], a[:, k, :], start=(n == 0), stop=(n == 3))
                    ins.then_inc(s["up"], 1)
                for j2 in range(2):
                    yield mark("DN", j2)
                    into = take(L, ("DN", j2), t)
                    for a in range(2):
                        cols = slice((2 * j2 + a) * P, (2 * j2 + a + 1) * P)
                        for m in range(FT):
                            if j2 == 0 and a == 0:
                                pe.wait_ge(s["hh"], due(L, "hh", t, m + 1))
                                name = "hl_dve" if m % 2 else "hl_pool"
                                pe.wait_ge(s[name], due(L, name, t, m // 2 + 1))
                            for part in (L.hh, L.hl):
                                ins = T.matmul(into[:, a * H:(a + 1) * H], part[:, m, cols], w2q[:, m, :],
                                               start=(m == 0 and part is L.hh), stop=(m == FT - 1 and part is L.hl))
                    ins.then_inc(s["dn"], 1)

            def stacks_landed(L, half, t):
                pe.wait_ge(L.landed[half], (t + 1) * LANDED)

            def products(n, t):
                half, c = divmod(n, NT)
                cols = slice(c * P, (c + 1) * P)
                if c == 0:
                    stacks_landed(L1, half, t)
                for k in range(2):
                    into = take(L1, ("PR", n, k), t)
                    for h4 in range(4):
                        h = half * HH8 + 4 * k + h4
                        ins = T.matmul(into[:, h4 * P:(h4 + 1) * P], L1.kst[0:STK, h, cols], L1.qst[0:STK, h, cols],
                                       start=True, stop=True)
                    ins.then_inc(s1["a"], 1)

            def outputs(n, t):
                s = s1
                half, c = divmod(n, NT)
                cols = slice(c * P, (c + 1) * P)
                qh, ql = L1.sth[:, 2 * half, cols], L1.stl[:, 2 * half, cols]
                local = take(L1, ("LO", n), t)
                if c:
                    state = 3 * half + c - 1
                    for m, (a, b) in enumerate(((qh, bsh), (ql, bsh), (qh, bsl))):
                        T.matmul(local[:, 0:HH8 * VW], a, b[:, state, :], start=(m == 0), stop=(m == 2),
                                 skip_group_check=True)
                pe.wait_ge(s["al_pool"], due(L1, "al_pool", t, n + 1))
                pe.wait_ge(s["al_dve"], due(L1, "al_dve", t, n + 1))
                for h in range(HH8):
                    for part in (ahp, alp):
                        ins = T.matmul(local[:, h * VW:(h + 1) * VW], part[:, n % 2, h // 4, (h % 4) * P:(h % 4 + 1) * P],
                                       L1.vp[:, c, half * HH8 + h, :],
                                       start=(c == 0 and part is ahp), stop=(part is alp), skip_group_check=True)
                ins.then_inc(s["om"], 1)
                for k in range(2):
                    into = take(L1, ("ME", n, k), t)
                    for m, (a, b) in enumerate(((qh, bmh), (ql, bmh), (qh, bml))):
                        ins = T.matmul(into[:, 0:2 * HH8 * MW], a,
                                       b[:, half, 2 * k:2 * k + 2, :, :].rearrange("p m h w -> p (m h w)"),
                                       start=(m == 0), stop=(m == 2))
                    ins.then_inc(s["om"], 1)

            def turn_back(n, t):
                into = take(L1, ("OT", n), t)
                pe.wait_ge(s1["t6"], due(L1, "t6", t, 3 * n + 3))
                for k in range(M + 2):
                    ins = T.matmul(into[:, 0:P], t6[:, n % 2, k, :], ident[:, :], is_transpose=True,
                                   start=(k == 0), stop=(k == M + 1))
                ins.then_inc(s1["ot"], 1)

            def lane1(t):
                s = s1
                yield mark1("T")
                turn(L1, 0, t)
                for q, (mat, m) in enumerate(((AQ, 0), (AK, 0), (AQ, 1), (AK, 1))):
                    yield mark1("PA", q)
                    if q == 0:
                        pe.wait_ge(s["xl"], due(L1, "xl", t, 2))
                    project(L1, ("PA", q), mat, m, "proj", t)
                for j in range(2):
                    yield mark1("V", j)
                    rows(L1, ("V", j), L1.xh, L1.xlo, AV, "v", t)
                for c in range(NT - 1):
                    yield mark1("SK")
                    if c == 0:
                        pe.wait_ge(s["sl"], due(L1, "sl", t, 4))
                    into = take(L1, ("SK", c), t)
                    cols = slice(c * P, (c + 1) * P)
                    for n, (part, half) in enumerate(((L1.sth, 0), (L1.stl, 0), (L1.sth, 1), (L1.stl, 1))):
                        ins = T.transpose(into[:, :].bitcast(F16)[:, n * P:(n + 1) * P], part[:, 2 * half + 1, cols],
                                          identh[:, :])
                    ins.then_inc(s["sk"], 1)
                yield mark1("RM")
                into = take(L1, ("RM",), t)
                pe.wait_ge(s["ssb"], due(L1, "ssb", t, 2))
                for half in range(KH):
                    ins = T.matmul(into[:, half * M * HH8:(half + 1) * M * HH8], ssb[:, half, :],
                                   bnorm[:, half, :, :].rearrange("p m h -> p (m h)"), start=True, stop=True)
                ins.then_inc(s["rm"], 1)
                for n in range(6):
                    yield mark1("ST", n)
                    if n == 0:
                        pe.wait_ge(s["vl"], due(L1, "vl", t, 2))
                        pe.wait_ge(s["skt"], due(L1, "skt", t, NT - 1))
                    half, c = divmod(n, 3)
                    into = take(L1, ("ST", n), t)
                    for cc in range(c + 1):
                        for part in range(2):
                            ins = T.matmul(into[:, 0:HH8 * VW], skt[:, cc, 2 * half + part, :],
                                           L1.vp[:, cc, half * HH8:(half + 1) * HH8, :].rearrange("p h w -> p (h w)"),
                                           start=(cc == 0 and part == 0), stop=(cc == c and part == 1))
                    ins.then_inc(s["st"], 1)
                for n in range(10):
                    yield mark1("N", n)
                    if n < 8:
                        products(n, t)
                    if n == 1:
                        pe.wait_ge(s["bl"], due(L1, "bl", t, 6))
                    if 1 <= n < 9:
                        outputs(n - 1, t)
                    if n >= 2:
                        turn_back(n - 2, t)
                yield from project_out(L1, AO, mark1, t)
                yield from ffn(L1, mark1, t)
                yield None

            def scores(h, t):
                if h % HH8 == 0:
                    stacks_landed(L2, h // HH8, t)
                for i in range(NT):
                    into = take(L2, ("S1", h, i), t)
                    T.matmul(into[:, 0:(i + 1) * P], L2.qst[0:STK, h, i * P:(i + 1) * P],
                             L2.kst[0:STK, h, 0:(i + 1) * P], start=True, stop=True)
                    T.matmul(into[:, i * P:(i + 1) * P], identb[:, :], mask_qk[:, :], start=False, stop=True,
                             skip_group_check=True).then_inc(s2["s1"], 1)

            def shifted(h, t):
                if h % NT == 0:
                    pe.wait_ge(s2["mrow"], due(L2, "mrow", t, 32 * (h // NT + 1)))
                for n, tiles in enumerate(S2_TILES):
                    into = take(L2, ("S2", h, n), t)
                    for kt in tiles:
                        at = KT_AT[kt] - S2_COL[n]
                        T.matmul(into[:, at:at + (NT - kt) * P], L2.kst[:, h, kt * P:(kt + 1) * P],
                                 L2.qst[:, h, kt * P:S], start=True, stop=True)
                        ins = T.matmul(into[:, at:at + P], identb[:, :], mask_kq[:, :], start=False, stop=True,
                                       skip_group_check=True)
                    ins.then_inc(s2["s2"], 1)

            def weighted(h, t):
                into = take(L2, ("PV", h), t)
                pe.wait_ge(s2["plo_pool"], due(L2, "plo_pool", t, 2 * h + 2))
                pe.wait_ge(s2["plo_dve"], due(L2, "plo_dve", t, h + 1))
                for i in range(NT):
                    at = i * VW
                    for kt in range(i + 1):
                        p0 = KT_AT[kt] + (i - kt) * P
                        for part in (ph, pl):
                            ins = T.matmul(into[:, at:at + VW], part[:, h % 2, p0:p0 + P], L2.vp[:, kt, h, :],
                                           start=(kt == 0 and part is ph), stop=(kt == i and part is pl),
                                           skip_group_check=True)
                ins.then_inc(s2["pv"], 1)

            def lane2(t):
                s = s2
                yield mark2("T")
                turn(L2, 0, t)
                for q, (m, a, b) in enumerate(((0, BQ, BQR), (0, BK, BKR), (1, BQ, BQR), (1, BK, BKR))):
                    yield mark2("PB", q)
                    if q == 0:
                        pe.wait_ge(s["xl"], due(L2, "xl", t, 2))
                    project(L2, ("PB", q, 0), a, m, "pr", t)
                    project(L2, ("PB", q, 1), b, m, "pr", t)
                for j in range(2):
                    yield mark2("V", j)
                    rows(L2, ("V", j), L2.xh, L2.xlo, BV, "v", t)
                for n in range(NH + LAG + 1):
                    yield mark2("N", n)
                    if n < NH:
                        scores(n, t)
                    if n >= 4 and n % 4 == 0 and n < NH + 4:
                        q = n // 4 - 1
                        into = take(L2, ("NM", q), t)
                        pe.wait_ge(s["nl"], due(L2, "nl", t, q + 1))
                        T.transpose(into[:, :].bitcast(F16)[:, 0:P], nt[:, :, :].rearrange("p a g -> p (a g)"),
                                    identh[:, :]).then_inc(s["nm"], 1)
                    if LAG <= n < NH + LAG:
                        shifted(n - LAG, t)
                    if n > LAG:
                        if n == LAG + 1:
                            pe.wait_ge(s["vl"], due(L2, "vl", t, 2))
                        weighted(n - LAG - 1, t)
                for half in range(KH):
                    yield mark2("OT", half)
                    pe.wait_ge(s["tb"], due(L2, "tb", t, NH))
                    into = take(L2, ("OT", half), t)
                    for i in range(NT):
                        for k in range(2):
                            ins = T.matmul(into[:, i * P:(i + 1) * P],
                                           tbuf[:, i, k, half * HH8:(half + 1) * HH8, :].rearrange("p h d -> p (h d)"),
                                           ident[:, :], is_transpose=True, start=(k == 0), stop=(k == 1))
                    ins.then_inc(s["ot"], 1)
                yield from project_out(L2, BO, mark2, t)
                yield from ffn(L2, mark2, t)
                yield None

            alone(lane1(0))
            with pe.Fori(1, B) as it:
                in_order(lane1(it), lane2(it - 1))
            alone(lane2(B - 1))


def kernel(**inputs):
    import numpy as _np
    import concourse.bacc as _bacc
    from concourse import mybir as _mybir
    from concourse.bass_utils import run_bass_kernel_spmd as _run

    a = {k: _np.asarray(v) for k, v in inputs.items()}
    pairs = _np.arange(H) ^ 1
    mats = [a["L0_attn_a_w_q"], a["L0_attn_a_w_k"], a["L0_attn_a_w_v"], a["L0_attn_a_w_o"],
            a["L0_attn_b_W_Q"], a["L0_attn_b_W_K"], a["L0_attn_b_W_V"], a["L0_attn_b_W_O"],
            a["L0_attn_b_W_Q"][pairs], a["L0_attn_b_W_K"][pairs]]
    f32 = _np.float32
    inv = (f32(THETA) ** (f32(-2.0) * _np.arange(D // 2, dtype=f32) / f32(D))).astype(f32)
    ang = (_np.arange(S, dtype=f32)[:, None] * inv).astype(f32)
    of_row = (_np.arange(P) % D) // 2
    sign = _np.where(_np.arange(P) % 2 == 0, -1.0, 1.0).astype(f32)
    cos = _np.cos(ang)[:, of_row].T
    sin = _np.sin(ang)[:, of_row].T * sign[:, None]
    arrays = {
        "x": a["L0_attn_a_hidden_states"].reshape(B * S, H),
        "wall": _np.stack([m.T for m in mats]),
        "mem": _np.concatenate([a["L0_attn_a_memories"], a["L0_attn_a_memory_norms"][..., None]],
                               axis=-1).transpose(1, 2, 0, 3),
        "gate": a["L0_attn_a_gate"].reshape(1, NH),
        "w1t": a["L0_ffn_W1"].T,
        "b1t": a["L0_ffn_b1"].reshape(FT, P).T,
        "w2t": a["L0_ffn_W2"].T,
        "b2": a["L0_ffn_b2"].reshape(1, H),
        "cos": cos,
        "sin": sin,
    }
    arrays = {k: _np.ascontiguousarray(v) for k, v in arrays.items()}
    nc = _bacc.Bacc("TRN2", target_bir_lowering=False, num_devices=1)
    args = [nc.dram_tensor(k, v.shape, _mybir.dt.from_np(v.dtype), kind="ExternalInput").ap() for k, v in arrays.items()]
    out = nc.dram_tensor("out", (B * S, H), _mybir.dt.float32, kind="ExternalOutput").ap()
    build(nc, *args, out)
    r = _run(nc, [arrays], core_ids=[0])
    return r.results[0]["out"].reshape(B, S, H)
```

```python
from contextlib import ExitStack

import numpy as np

import concourse.bass as bass
from concourse import mybir

F32 = mybir.dt.float32
F16 = mybir.dt.float16
BF16 = mybir.dt.bfloat16
ALU = mybir.AluOpType
ACT = mybir.ActivationFunctionType
AX = mybir.AxisListType.X

P = 128
B, S, H, NH, M = 16, 512, 256, 16, 4
D = H // NH
FF = 4 * H
KH = H // P
HH8 = NH // KH
NT = S // P
FT = FF // P
LN_EPS = 1e-5
MEM_EPS = 1e-6
Q_EPS = 1e-5
THETA = 10000.0

WS = 128.0
VS = 8.0
AS = 2.0 ** -6
RS = 16.0
SHIFT = 1024.0
MASKED = -1e30
VW = 2 * D + 1
MW = D + 1
PARTS = 4 * D
STK = 96
MAXROW = 96
LAG = 5
PV_LAG = LAG + 2
RING = 3
AQ, AK, AV, AO, BQ, BK, BV, BO, BQR, BKR = range(10)
NMAT = 10

NORM = dict(bn=8, tick=2, mv=8, ve=2, rstd=2, shift=2, xn=8, xt=4, xh=4, xl=4)
OUTS = dict(v=2, vh=2, vl=2, sh=4, sl=4, bounced=64, wo=2, xres=2)
FFN = dict(up=8, hf=8, hh=8, hl_pool=4, hl_dve=4, xb=1, dn=2, xffn=2)
PER1 = dict(
    NORM, **OUTS, **FFN, xin=16, proj=4, e=4, r=4, sq=4, sk=3, skt=3,
    ssb=2, rm=1, rmax=1, rdif=1, rexp=1, rsum=1, rrec=1, rcoef=2,
    st=6, bf=6, bh=6, bl=6, a=16, am=16, ah=16, al_pool=8, al_dve=8,
    om=24, clip=24, rec=8, coef=8, t6=24, ot=8, oh=8, ol=8,
)
PER2 = dict(
    NORM, **OUTS, **FFN, pr=8, t12=8, y=4, s1=48, mx=64, nh=4, nl=4, nm=4, nmt=4, mrow=128, s2=48, pexp=48,
    phi=32, phi_dve=16, plo_pool=32, plo_dve=16, pv=16, prec=16, tb=16, ot=2, oh=2, ol=2, store=16, handed=16,
)
LANDED = 2 * 4 * 16

CUT = 7


MARKS = {
    1: {
        "sync": {
            "T": [48],
            "PA": [58.7, 60.7],
        },
        "pool": {
            "T": [51.3],
            "PA": [58.7, 58.7, 59.8, 60.7, 61.5],
            "ST": [64.3, 64.7, 65.4, 65.8, 66.8, 67.5],
            "N": [69.6, 72.6, 77.4, 83.3, 89.5, 94.2, 98.7, 103.2],
            "FT": [116],
            "XB": [120.3],
            "UP": [123.3, 123.3, 125.3, 125.3, 127.1, 127.1, 129],
        },
        "act": {
            "T": [52],
            "TT": [52.6],
            "PA": [55.9, 57.4, 58.5, 59.2, 60.5],
            "V": [61.4, 61.7],
            "SK": [62.5],
            "RM": [63.7],
            "ST": [64, 64.3, 65.1, 65.5, 66.3, 67],
            "N": [68.8, 71.8, 76.9, 82.9, 89.1, 93.7, 98.2, 102.8, 108.7, 111.3],
            "NT": [71.8, 76.9, 80.2, 86, 90.5, 95.1, 99.6, 104.2, 108.4, 111],
            "FT": [117.8],
            "FTT": [119.6],
            "UP": [122.3, 123.5, 124.4, 125.2, 126.2, 127, 128, 128.8],
        },
        "dve": {
            "T": [50],
            "TR": [51.9],
            "TT": [54],
            "PA": [56.9, 58.4, 59.4, 60.2, 61.1],
            "V": [61.8, 62.2],
            "RM": [63.4],
            "ST": [63.7, 64, 64.8, 65.2, 65.9, 66.5],
            "N": [68, 71, 75.8, 81.8, 88, 92.6, 97.1, 101.7, 106.9, 111.3],
            "NC": [70.2, 72.4, 77.6, 83.8, 89.6, 94.2, 98.7, 103.3, 107.2, 111.6],
            "NL": [70.2, 75.5, 80.9, 87.1, 91.7, 96.2, 99.6, 105.3, 109.8, 111.3],
            "WO": [113.8, 115.1],
            "FT": [115.5],
            "FTR": [117.7],
            "FTT": [120.1],
            "UP": [124.4, 124.4, 124.4, 126.1, 126.1, 128, 128, 129.8],
            "DN": [132.8, 135.3],
        },
        "pe": {
            "TT": [52.8],
            "PA": [54.8, 56.4, 57.9, 58.9],
            "V": [60, 60.8],
            "SK": [62.5],
            "RM": [63.3],
            "ST": [63.8, 63.9, 64.2, 64.6, 64.7, 65],
            "N": [66.3, 67.8, 74.1, 82.4, 88.6, 93.2, 97.7, 102.2, 106.8, 111.3],
            "NT": [66.5, 73.1, 78.6, 84.8, 89.5, 94.1, 98.6, 103.2, 107.4, 110],
            "NO": [66.8, 71.4, 76.1, 82.3, 88.1, 92.9, 97.2, 101.7, 105.8, 110.3],
            "NA": [71.4, 71.4, 76.9, 83.1, 88.5, 92.9, 97.5, 102.1, 106.5],
            "WO": [112.3, 114],
            "FTT": [118.7],
            "UP": [121.3, 122.5, 123.6, 124.5, 125.1, 125.7, 126.3, 126.9],
            "DN": [127.5, 132.9],
            "DM": [127.5, 127.6, 127.8, 127.9, 128.3, 128.8, 130.1, 130.6],
        },
    },
    2: {
        "sync": {
            "PB": [18.5, 21.8],
            "N": [32.2, 40.9, 49.2, 57.6],
        },
        "pool": {
            "T": [1.9],
            "PB": [12.4, 14.9, 17.3, 19.8],
            "N": [36.2, 38.2, 40.1, 42.1, 44.7, 46.5, 48.4, 50.8, 53, 54.8, 56.8, 58.8, 61.6, 63.5, 65.4, 67.2],
            "FT": [78.7],
            "XB": [81],
            "UP": [86.5, 86.5, 88.5, 88.5, 90.4, 90.4, 92.2],
        },
        "act": {
            "T": [2],
            "TT": [5.9],
            "PB": [13.6, 16.1, 18.5, 20.9],
            "V": [21.4, 21.8],
            "N": [31.9, 31.9, 31.9, 31.9, 31.9, 34.7, 36.8, 38.7, 40.6, 43.3, 45.2, 47, 48.9, 51.6, 53.5, 55.3,
                 57.3, 60.2, 62.1, 64, 65.8],
            "NS": [34.7, 34.7, 34.7, 34.7, 34.7, 34.7, 36.8, 38.7, 40.7, 43.3, 45.2, 47, 49.4, 51.6, 53.5, 55.3,
                 57.4, 60.2, 62.1, 64, 65.8],
            "NX": [35.7, 35.7, 35.7, 35.7, 35.7, 35.7, 37.7, 39.6, 41.6, 44.2, 46, 47.9, 50.3, 52.5, 54.3, 56.3,
                 58.3, 61.1, 63, 64.9, 66.7],
            "OT": [69.3, 70.5],
            "FT": [79.5],
            "FTT": [81.4],
            "UP": [84.9, 86.1, 87, 87.8, 88.8, 89.7, 90.7, 92.1],
            "END": [103],
        },
        "dve": {
            "T": [0],
            "TR": [2.8],
            "TT": [6.5],
            "PB": [9.5, 13.7, 16.1, 18.6, 21.5],
            "PL": [14.8, 14.8, 18.2, 20.6],
            "V": [22, 22.6],
            "N": [26.6, 27.8, 28.9, 30.1, 31.5, 32.7, 35.9, 37.5, 39.3, 41.5, 44, 46, 48.1, 50.3, 52.4, 54.5, 56.5,
                 58, 61.2, 62.7, 64.4, 66.3, 68.1, 69.5],
            "NL": [28.1, 29.2, 30.4, 31.8, 33, 36.2, 37.3, 39.3, 41.1, 43.3, 45.7, 48.1, 49.6, 51.8, 53.8, 56.2,
                 57.4, 59.4, 62.3, 64.1, 66, 67.9, 69.5, 71.8],
            "OT": [69.8, 70.9],
            "WO": [75.4, 76.7],
            "FT": [77.2],
            "FTR": [79.4],
            "FTT": [81.8],
            "UP": [87.6, 87.6, 87.6, 89.4, 89.4, 91.2, 91.2, 93.1],
            "DN": [96.7, 99.3],
        },
        "pe": {
            "TT": [4.3],
            "PB": [7.1, 11.6, 14.1, 16.4],
            "V": [18.6, 19.8],
            "N": [26, 27.1, 28.2, 29.3, 30.2, 32.1, 35.3, 37.2, 39.2, 41.4, 43.8, 45.9, 48, 50.2, 52.2, 54.3, 56.4,
                 59.6, 61.1, 62.6, 64.5, 67.1, 69],
            "NS": [27.1, 28.2, 29.3, 30.2, 31.7, 34.2, 36.4, 37.9, 39.9, 42.9, 44.5, 46.5, 48.5, 51.2, 52.8, 54.9,
                 56.4, 59.6, 61.1, 62.6, 64.5, 67.1, 69],
            "NP": [27.1, 28.2, 29.3, 30.2, 32.1, 35.3, 37.2, 38.8, 41, 43.5, 45.5, 47.6, 49.8, 51.9, 54, 56, 57.5,
                 60.7, 62.2, 63.7, 65.2, 67.1, 69],
            "OT": [68, 69.2],
            "WO": [73.5, 75.2],
            "FTT": [80.1],
            "UP": [84.2, 85.4, 86.5, 87.4, 88, 88.6, 89.2, 89.8],
            "DM": [91, 91.2, 91.3, 91.5, 91.9, 92.4, 93.7, 94.2],
            "DN": [92.4, 97.9],
        },
    },
}


def marks(lane, engine):
    return lambda kind, n=0: MARKS[lane][engine][kind][n]


def back(part):
    for mark in part:
        yield None if mark is None else mark - 100


S1_TILES = [[0, 2], [1], [3]]
S1_DONE = [2, 3, 4]
Q_AT = {0: 0, 2: P, 1: 0, 3: 0}
S2_TILES = [[0], [1, 3], [2]]
S2_COL = [0, 512, 1024]
S2_W = [512, 512, 256]
KT_AT = {0: 0, 1: 512, 3: 512 + 384, 2: 1024}


def jobs1():
    jobs = [(("T", 0, k), "xl", k + 1) for k in range(KH)]
    jobs += [(("PA", t), "r", t + 1) for t in range(4)]
    jobs += [(("V", j), "vl", j + 1) for j in range(2)]
    jobs += [(("SK", c), "skt", c + 1) for c in range(NT - 1)]
    jobs += [(("RM",), "rdif", 1)]
    jobs += [(("ST", n), "bf", n + 1) for n in range(6)]
    for n in range(-1, 9):
        if n + 1 < 8:
            jobs += [(("PR", n + 1, k), "am", 2 * (n + 1) + k + 1) for k in range(2)]
        if 0 <= n < 8:
            jobs += [(("LO", n), "t6", 3 * n + 3)]
            jobs += [(("ME", n, k), "t6", 3 * n + k + 1) for k in range(2)]
        if 0 <= n - 1 < 8:
            jobs += [(("OT", n - 1), "ol", n)]
    return jobs + tail_jobs()


def tail_jobs():
    jobs = [(("WO", j), "xres", j + 1) for j in range(2)]
    jobs += [(("T", 1, k), "xl", KH + k + 1) for k in range(KH)]
    jobs += [(("UP", m), "hf", m + 1) for m in range(FT)]
    jobs += [(("DN", j), "xffn", j + 1) for j in range(2)]
    return jobs


def jobs2():
    jobs = [(("T", 0, k), "xl", k + 1) for k in range(KH)]
    jobs += [(("PB", t, r), "t12", 2 * t + r + 1) for t in range(4) for r in range(2)]
    jobs += [(("V", j), "vl", j + 1) for j in range(2)]
    for n in range(NH + PV_LAG):
        if n < NH:
            jobs += [(("S1", n, k), "mx", NT * n + S1_DONE[k]) for k in range(3)]
        if n >= 4 and n % 4 == 0 and n < NH + 4:
            jobs += [(("NM", n // 4 - 1), "nmt", n // 4)]
        if LAG <= n < NH + LAG:
            jobs += [(("S2", n - LAG, k), "pexp", 3 * (n - LAG) + k + 1) for k in range(3)]
        h = n - PV_LAG
        if h >= 0:
            jobs += [(("PV", h), "tb", h + 1)]
    jobs += [(("OT", half), "ol", half + 1) for half in range(KH)]
    return jobs + tail_jobs()


class Lane:

    def __init__(self, n, per, jobs, banks, sem):
        self.n, self.per, self.jobs, self.banks = n, per, jobs, banks
        self.at = {job: k for k, (job, _, _) in enumerate(jobs)}
        self.s = {name: sem(f"{name}_{n}") for name in per}


def due(L, name, turn, n):
    return turn * L.per[name] + n + 1


def bank_of(L, job):
    return L.banks[L.at[job] % len(L.banks)]


def in_order(a, b):
    pa, pb = next(a), next(b)
    while pa is not None or pb is not None:
        if pb is None or (pa is not None and pa <= pb):
            pa = next(a, None)
        else:
            pb = next(b, None)


def after(a, b):
    for part in (a, b):
        for mark in part:
            if mark is not None:
                yield mark
    yield None


def alone(a):
    for _ in a:
        pass


def build(nc, x, wall, mem, gate, w1t, b1t, w2t, b2, cos, sin, out):
    with ExitStack() as ctx:
        def sb(name, shape, dt=F32):
            return ctx.enter_context(nc.sbuf_tensor(name, shape, dt))

        def sem(name):
            return ctx.enter_context(nc.semaphore(name))

        wh = sb("wh", [P, NMAT, KH, H], F16)
        wl = sb("wl", [P, NMAT, KH, H], F16)
        w1q = sb("w1q", [P, KH, FF], F16)
        w2q = sb("w2q", [P, FT, H], F16)
        b1c = sb("b1c", [P, FT])
        b2bc = sb("b2bc", [P, H])
        cost = sb("cost", [P, S])
        sint = sb("sint", [P, S])
        ident = sb("ident", [P, P])
        identh = sb("identh", [P, P], F16)
        identb = sb("identb", [P, P], BF16)
        onesf = sb("onesf", [P, P])
        tri = sb("tri", [P, P])
        mask_qk = sb("mask_qk", [P, P], BF16)
        mask_kq = sb("mask_kq", [P, P], BF16)
        bdmask = sb("bdmask", [P, HH8, VW])
        bmh = sb("bmh", [P, KH, M, HH8, MW], F16)
        bml = sb("bml", [P, KH, M, HH8, MW], F16)
        bnorm = sb("bnorm", [P, KH, M, HH8])
        gates = sb("gates", [P, 4, NH])
        small = sb("small", [P, 16])
        halfc = sb("halfc", [P, NT])
        xa = sb("xa", [P, NT, H])
        xb = sb("xb", [P, NT, H])
        xc = sb("xc", [P, NT, H])

        banks = [ctx.enter_context(nc.psum_tensor(f"bank{n}", [P, 512], F32)) for n in range(8)]
        L1 = Lane(1, PER1, jobs1(), banks[0:4], sem)
        L2 = Lane(2, PER2, jobs2(), banks[4:8], sem)
        for L, parts in ((L1, 4 * S), (L2, 5 * S)):
            def own(name, shape, dt=F32):
                return sb(f"{name}_{L.n}", shape, dt)

            L.stats = own("stats", [P, NT, 6])
            L.tick = own("tick", [P, 1])
            L.mv = own("mv", [P, NT, 2])
            L.ve = own("ve", [P, NT])
            L.rstd = own("rstd", [P, NT])
            L.shift = own("shift", [P, NT])
            L.xh = own("xh", [P, KH, S], F16)
            L.xlo = own("xlo", [P, KH, S], F16)
            L.qst = own("qst", [P, NH, S], F16)
            L.kst = own("kst", [P, NH, S], F16)
            L.vp = own("vp", [P, NT, NH, VW], F16)
            L.oth, L.otl = L.xh, L.xlo
            L.place1 = own("place1", [P, parts])
            L.place2 = own("place2", [P, 2 * parts], F16)
            L.place3 = own("place3", [P, 4, S])
            L.place4 = own("place4", [P, 2, S])
            split = L.place1[:, 0:4 * S].bitcast(F16).rearrange("p (r t s) -> p r t s", r=2, t=4)
            L.sth, L.stl = split[:, 0], split[:, 1]
            L.hh = L.place1[:, 0:FT * S // 2].bitcast(F16).rearrange("p (m s) -> p m s", s=S)
            L.hl = L.place2[:, 0:FT * S].rearrange("p (m s) -> p m s", s=S)
            L.sq = L.place3
            L.xn = L.place4[:, :, :].rearrange("p a (b f) -> p (a b) f", f=H)
            L.hf = L.place4
        s1, s2 = L1.s, L2.s
        skt_at = L1.place3[:, :, :].rearrange("p a s -> p (a s)")[:, 0:(NT - 1) * 2 * P]
        skt = skt_at.bitcast(F16).rearrange("p (c a s) -> p c a s", c=NT - 1, a=4)
        ssum = sb("ssum", [P, KH])
        wmax = sb("wmax", [P, NH])
        wdif = sb("wdif", [P, KH, M, HH8])
        wexp = sb("wexp", [P, KH, M, HH8])
        wsum = sb("wsum", [P, NH])
        wrec = sb("wrec", [P, NH])
        wnum = sb("wnum", [P, KH, M, HH8])
        wc = sb("wc", [P, KH, M + 1, HH8])
        bf_from = (NT - 1) * 2 * P
        bf = L1.place3[:, :, :].rearrange("p a s -> p (a s)")[:, bf_from:bf_from + 2 * HH8 * VW]
        bf = bf.rearrange("p (r w) -> p r w", r=2)
        bsh = L1.place4[:, :, :].rearrange("p a s -> p (a s)")[:, 0:3 * HH8 * VW]
        bsh = bsh.bitcast(F16).rearrange("p (n w) -> p n w", n=6)
        bsl = sb("bsl", [P, 6, HH8 * VW], F16)
        am = sb("am", [P, 2, S])
        ebuf = L1.place4
        rbuf = am
        ssb = am[:, 0, 0:KH * P].rearrange("p (a s) -> p a s", a=KH)
        alp = L1.place2[:, 0:4 * S].rearrange("p (r k s) -> p r k s", r=2, k=2)
        ahp = L1.place2[:, 4 * S:8 * S].rearrange("p (r k s) -> p r k s", r=2, k=2)
        den = sb("den", [P, 2, M + 1, HH8])
        drec = sb("drec", [P, 2, M + 1, HH8])
        coef = sb("coef", [P, 2, M + 1, HH8])
        t6 = L1.place3[:, 0:3, :].rearrange("p a s -> p (a s)").rearrange("p (r t s) -> p r t s", r=2, t=M + 2)
        t12 = L2.place4
        pf = L2.place1[:, :].rearrange("p (r n) -> p r n", r=2)
        wide = S2_COL[-1] + S2_W[-1]
        in_place = [L2.place2[:, n * wide:(n + 1) * wide] for n in range(4)]
        low3 = L2.place4[:, :, :].rearrange("p a s -> p (a s)")[:, 0:wide // 2].bitcast(F16)
        ph = in_place[0:2] + [sb("high3", [P, wide], F16)[:, :]]
        pl = in_place[2:4] + [low3]
        tbuf = L2.place3[:, :, :].rearrange("p a s -> p (a s)").rearrange("p (i t h d) -> p i t h d", i=NT, t=2, h=NH)
        nt = sb("nt", [P, 2, NH * NT], F16)
        nmt = sb("nmt", [P, 2, P], F16)
        mxs = sb("mxs", [P, NH * NT])
        prec = sb("prec", [P, 2, NT])

        scratch = nc.dram_tensor("scratch", (2, KH, 2, P, 2, S), F16, kind="Internal").ap()
        for L in (L1, L2):
            L.landed = [sem(f"landed{half}_{L.n}") for half in range(KH)]
            L.scratch = scratch[L.n - 1]

        w_in = sem("w_in")
        f_in = sem("f_in")
        c_in = sem("c_in")
        g_in = sem("g_in")
        m_in = sem("m_in")
        pool_const = sem("pool_const")
        dve_setup = sem("dve_setup")
        act_setup = sem("act_setup")
        pe_setup = sem("pe_setup")
        primed = sem("primed")
        DVE_SETUP = 26
        SPLIT = 7
        block = ctx.enter_context(nc.Block())

        x_in, x_out = (t.rearrange("(b j p) f -> b p j f", b=B, p=P) for t in (x, out))

        def sequence(of, t):
            if isinstance(t, int):
                return of[t]
            return of[bass.ds(t, 1)].rearrange("o p j f -> p (o j) f")

        w_stage = [L1.qst, L1.kst]
        w_stage = [t[:, :, :].rearrange("p a b -> p (a b)").bitcast(F32) for t in w_stage]
        f_stage = L2.qst[:, :, :].rearrange("p a b -> p (a b)").bitcast(F32)
        f_tmp = L2.kst[:, :, :].rearrange("p a b -> p (a b)")
        bm_all = L2.place3[:, :, :].rearrange("p a s -> p (a s)")[:, 0:KH * M * HH8 * MW]
        bm = bm_all.rearrange("p (a m h e) -> p a m h e", a=KH, m=M, h=HH8)
        NFW = KH * FF

        @block.sync
        def _(sp):
            at1, at2 = marks(1, "sync"), marks(2, "sync")
            sp.dma_start(gates[:, 0, :], gate.broadcast_to([P, NH])).then_inc(g_in, 16)
            sp.dma_start(f_stage[:, 0:NFW].rearrange("p (k f) -> p k f", k=KH),
                         w1t.rearrange("(k p) f -> p k f", p=P)).then_inc(f_in, 16)
            sp.dma_start(f_stage[:, NFW:2 * NFW].rearrange("p (k f) -> p k f", k=FT),
                         w2t.rearrange("(k p) f -> p k f", p=P)).then_inc(f_in, 16)
            wv = wall.rearrange("n (k p) f -> p n k f", p=P)
            for n in range(NMAT):
                at = (n % 8) * KH * H
                sp.dma_start(w_stage[n // 8][:, at:at + KH * H].rearrange("p (k f) -> p k f", k=KH),
                             wv[:, n]).then_inc(w_in, 16)
            sp.dma_start(b1c[:, :], b1t).then_inc(c_in, 16)
            sp.dma_start(b2bc[:, :], b2.broadcast_to([P, H])).then_inc(c_in, 16)
            sp.dma_start(cost[:, :], cos).then_inc(c_in, 16)
            sp.dma_start(sint[:, :], sin).then_inc(c_in, 16)
            sp.wait_ge(pool_const, 1)
            for half in range(KH):
                for h in range(HH8):
                    sp.dma_start(bm[h * D:(h + 1) * D, half, :, h, :], mem[half * HH8 + h]).then_inc(m_in, 16)
            sp.wait_ge(primed, 1)

            def stack(L, half, t):
                s = L.s
                if half == 0:
                    sp.wait_ge(s["xt"], due(L, "xt", t, 2))
                sp.wait_ge(s["sh"], due(L, "sh", t, 2 * half + 2))
                sp.wait_ge(s["sl"], due(L, "sl", t, 2 * half + 2))
                for part, src in enumerate((L.sth, L.stl)):
                    sp.dma_start(L.scratch[half, part], src[:, 2 * half:2 * half + 2, :]).then_inc(s["bounced"], 16)
                sp.wait_ge(s["bounced"], due(L, "bounced", t, 32 * (half + 1)))
                heads = slice(half * HH8, (half + 1) * HH8)
                for k, (q_part, k_part) in enumerate(((0, 0), (0, 1), (1, 0), (1, 1))):
                    to = slice(k * D, (k + 1) * D)
                    for dst, part, which in ((L.qst, q_part, 0), (L.kst, k_part, 1)):
                        sp.dma_start(dst[to, heads, :], L.scratch[half, part, :, which, :]
                                     .rearrange("(h d) s -> d h s", d=D)).then_inc(L.landed[half], 16)

            def lane1_start(t):
                yield at1("T")
                sp.wait_ge(s1["xffn"], due(L1, "xffn", t, 0))
                sp.dma_start(xa[:, :, :], sequence(x_in, t)).then_inc(s1["xin"], 16)
                for half in range(KH):
                    yield at1("PA", half)
                    stack(L1, half, t)
                yield None

            def lane1_end(t):
                yield None

            def lane2(t):
                for half in range(KH):
                    yield at2("PB", half)
                    stack(L2, half, t)
                for g in range(NH // NT):
                    yield at2("N", g)
                    sp.wait_ge(s2["nmt"], due(L2, "nmt", t, g + 1))
                    for part in range(2):
                        at = part * NH * NT + 16 * g
                        sp.dma_start(L2.qst[MAXROW + part:MAXROW + part + 1, NT * g:NT * g + NT, :],
                                     nmt[at:at + 16, g % 2, :]).then_inc(s2["mrow"], 16)
                yield None

            alone(lane1_start(0))
            alone(lane1_end(0))
            alone(lane1_start(1))
            with sp.Fori(1, B - 1) as it:
                in_order(lane2(it - 1), after(back(lane1_end(it)), lane1_start(it + 1)))
            in_order(lane2(B - 2), back(lane1_end(B - 1)))
            alone(lane2(B - 1))

        @block.gpsimd
        def _(pool):
            at1, at2 = marks(1, "pool"), marks(2, "pool")
            G = nc.gpsimd
            G.memset(bm_all, 0.0).then_inc(pool_const, 1)
            G.memset(ident[:, :], 0.0).then_inc(pool_const, 1)
            G.memset(tri[:, :], 1.0).then_inc(pool_const, 1)
            G.memset(mask_qk[:, :], 0.0).then_inc(pool_const, 1)
            G.memset(mask_kq[:, :], 0.0).then_inc(pool_const, 1)
            G.memset(bdmask[:, :, :], 1.0).then_inc(pool_const, 1)
            G.memset(nt[:, :, :], 0.0).then_inc(pool_const, 1)
            G.memset(halfc[:, :], -0.5).then_inc(pool_const, 1)
            pool.wait_ge(pool_const, 8)
            G.affine_select(out=ident[:, :], in_=ident[:, :], compare_op=ALU.not_equal, fill=1.0, base=0,
                            pattern=[[-1, P]], channel_multiplier=1).then_inc(pool_const, 1)
            G.affine_select(out=tri[:, :], in_=tri[:, :], compare_op=ALU.is_ge, fill=0.0, base=0,
                            pattern=[[1, P]], channel_multiplier=-1).then_inc(pool_const, 1)
            G.affine_select(out=mask_qk[:, :], in_=mask_qk[:, :], compare_op=ALU.is_ge, fill=MASKED, base=0,
                            pattern=[[-1, P]], channel_multiplier=1).then_inc(pool_const, 1)
            G.affine_select(out=mask_kq[:, :], in_=mask_kq[:, :], compare_op=ALU.is_ge, fill=MASKED, base=0,
                            pattern=[[1, P]], channel_multiplier=-1).then_inc(pool_const, 1)
            G.affine_select(out=bdmask[:, :, :], in_=bdmask[:, :, :], compare_op=ALU.is_ge, fill=0.0, base=0,
                            pattern=[[-D, HH8], [0, VW]], channel_multiplier=1).then_inc(pool_const, 1)
            pool.wait_ge(pool_const, 13)
            G.affine_select(out=bdmask[:, :, :], in_=bdmask[:, :, :], compare_op=ALU.is_ge, fill=0.0,
                            base=D - 1, pattern=[[D, HH8], [0, VW]], channel_multiplier=-1).then_inc(pool_const, 1)
            pool.wait_ge(c_in, 64)
            pool.wait_ge(pool_const, 14)
            for L in (L1, L2):
                for name in L.per:
                    G.sem_inc(L.s[name], 1)
            G.drain().then_inc(primed, 1)
            pool.wait_ge(dve_setup, SPLIT)
            for st in (L1.qst, L1.kst):
                G.memset(st[PARTS:P, :, :].rearrange("p a s -> p (a s)").bitcast(F32), 0.0).then_inc(pool_const, 1)
            pool.wait_ge(dve_setup, DVE_SETUP)

            def norm(L, u, t):
                s = L.s
                pool.wait_ge(s["ve"], due(L, "ve", t, u + 1))
                G.tensor_tensor(L.rstd[:, :], L.ve[:, :], halfc[:, :], ALU.pow).then_inc(s["rstd"], 1)

            def ffn(L, X, mark, t):
                s = L.s
                yield mark("FT")
                norm(L, 1, t)
                yield mark("XB")
                pool.wait_ge(s["xn"], due(L, "xn", t, 2 * NT))
                G.tensor_tensor(X[:, :, :], X[:, :, :],
                                b2bc[:, :].rearrange("p (a f) -> p a f", a=1).broadcast_to([P, NT, H]),
                                ALU.add).then_inc(s["xb"], 1)
                for m in range(0, FT, 2):
                    yield mark("UP", m)
                    pool.wait_ge(s["hh"], due(L, "hh", t, m + 1))
                    G.tensor_tensor(L.hl[:, m, :], L.hf[:, 0, :], L.hh[:, m, :], ALU.subtract).then_inc(s["hl_pool"], 1)

            def causal_low(n, t):
                s = s1
                pool.wait_ge(s["ah"], due(L1, "ah", t, 2 * n + 1))
                if n >= 2:
                    pool.wait_ge(s["om"], due(L1, "om", t, 3 * (n - 1)))
                G.tensor_tensor(alp[:, n % 2, 0, :], am[:, 0, :], ahp[:, n % 2, 0, :],
                                ALU.subtract).then_inc(s["al_pool"], 1)

            def lane1_start(t):
                s = s1
                yield at1("T")
                norm(L1, 0, t)
                for q in range(4):
                    yield at1("PA", q + 1)
                    pool.wait_ge(s["sh"], due(L1, "sh", t, q + 1))
                    G.tensor_tensor(L1.stl[:, q, :], L1.sq[:, q, :], L1.sth[:, q, :], ALU.subtract).then_inc(s["sl"], 1)
                for n in range(6):
                    yield at1("ST", n)
                    pool.wait_ge(s["bh"], due(L1, "bh", t, n + 1))
                    G.tensor_tensor(bsl[:, n, :], bf[:, n % 2, :], bsh[:, n, :], ALU.subtract).then_inc(s["bl"], 1)
                for n in range(CUT):
                    yield at1("N", n)
                    causal_low(n, t)
                yield None

            def lane1_end(t):
                for n in range(CUT, 8):
                    yield at1("N", n)
                    causal_low(n, t)
                yield from ffn(L1, xa, at1, t)
                yield None

            def lane2(t):
                s = s2
                yield at2("T")
                norm(L2, 0, t)
                for q in range(4):
                    yield at2("PB", q)
                    pool.wait_ge(s["t12"], due(L2, "t12", t, 2 * q + 2))
                    G.tensor_tensor(L2.sq[:, q, :], t12[:, 0, :], t12[:, 1, :], ALU.add).then_inc(s["y"], 1)
                for h in range(NH):
                    yield at2("N", h)
                    for n in range(2):
                        a, b = S2_COL[n], S2_COL[n + 1]
                        pool.wait_ge(s["phi"], due(L2, "phi", t, 2 * h + n + 1))
                        G.tensor_tensor(pl[h % RING][:, a:b], pf[:, h % 2, a:b], ph[h % RING][:, a:b],
                                        ALU.subtract).then_inc(s["plo_pool"], 1)
                yield from ffn(L2, xc, at2, t)
                yield None

            alone(lane1_start(0))
            alone(lane1_end(0))
            alone(lane1_start(1))
            with pool.Fori(1, B - 1) as it:
                in_order(lane2(it - 1), after(back(lane1_end(it)), lane1_start(it + 1)))
            in_order(lane2(B - 2), back(lane1_end(B - 1)))
            alone(lane2(B - 1))

        @block.scalar
        def _(act):
            at1, at2 = marks(1, "act"), marks(2, "act")
            A = nc.scalar
            act.wait_ge(g_in, 16)
            A.activation(gates[:, 1, :], gates[:, 0, :], ACT.Exp, scale=-1.0).then_inc(act_setup, 1)
            act.wait_ge(f_in, 32)
            for n in range(2):
                A.activation(f_tmp[:, n * NFW:(n + 1) * NFW], f_stage[:, n * NFW:(n + 1) * NFW], ACT.Abs,
                             accum_out=small[:, n:n + 1]).then_inc(act_setup, 1)
            act.wait_ge(dve_setup, DVE_SETUP)
            act.wait_ge(primed, 1)

            def normed(L, u, X, t):
                s = L.s
                act.wait_ge(s["shift"], due(L, "shift", t, u + 1))
                for j in range(NT):
                    A.activation(L.xn[:, j, :], X[:, j, :], ACT.Identity, bias=L.shift[:, j:j + 1],
                                 scale=L.rstd[:, j:j + 1]).then_inc(s["xn"], 1)

            def turned(L, u, t):
                s = L.s
                for k in range(KH):
                    act.wait_ge(s["xt"], due(L, "xt", t, 2 * u + k + 1))
                    A.activation(L.xh[:, k, :], bank_of(L, ("T", u, k))[:, :], ACT.Copy).then_inc(s["xh"], 1)

            def values(L, j, t):
                act.wait_ge(L.s["v"], due(L, "v", t, j + 1))
                A.activation(L.vp[:, 2 * j:2 * j + 2, :, 0:D],
                             bank_of(L, ("V", j))[:, :].rearrange("p (c h d) -> p c h d", c=2, d=D),
                             ACT.Copy, scale=VS / WS).then_inc(L.s["vh"], 1)

            def ffn(L, X, mark, t):
                s = L.s
                yield mark("FT")
                normed(L, 1, X, t)
                yield mark("FTT")
                turned(L, 1, t)
                for m in range(FT):
                    yield mark("UP", m)
                    act.wait_ge(s["up"], due(L, "up", t, m + 1))
                    if m >= 2:
                        name = "hl_dve" if m % 2 else "hl_pool"
                        act.wait_ge(s[name], due(L, name, t, m // 2))
                    A.activation(L.hf[:, m % 2, :], bank_of(L, ("UP", m))[:, :], ACT.Relu,
                                 bias=b1c[:, m:m + 1]).then_inc(s["hf"], 1)
                    act.wait_ge(s["hf"], due(L, "hf", t, m + 1))
                    A.activation(L.hh[:, m, :], L.hf[:, m % 2, :], ACT.Copy).then_inc(s["hh"], 1)

            def tiles(first, end, t):
                s = s1
                for n in range(first, end):
                    yield at1("N", n)
                    if n < 8:
                        for k in range(2):
                            act.wait_ge(s["am"], due(L1, "am", t, 2 * n + k + 1))
                            if n >= 2 and k == 0:
                                act.wait_ge(s["om"], due(L1, "om", t, 3 * (n - 1)))
                            A.activation(ahp[:, n % 2, k, :], am[:, k, :], ACT.Copy).then_inc(s["ah"], 1)
                    yield at1("NT", n)
                    if n >= 2:
                        half, c = divmod(n - 2, NT)
                        act.wait_ge(s["ot"], due(L1, "ot", t, n - 1))
                        A.activation(L1.oth[:, half, c * P:(c + 1) * P], bank_of(L1, ("OT", n - 2))[:, 0:P],
                                     ACT.Copy).then_inc(s["oh"], 1)

            def lane1_start(t):
                s = s1
                yield at1("T")
                normed(L1, 0, xa, t)
                yield at1("TT")
                turned(L1, 0, t)
                for q in range(4):
                    yield at1("PA", q)
                    act.wait_ge(s["proj"], due(L1, "proj", t, q + 1))
                    if q >= 2:
                        act.wait_ge(s["sq"], due(L1, "sq", t, q - 1))
                    A.activation(ebuf[:, q % 2, :], bank_of(L1, ("PA", q))[:, :], ACT.Exp,
                                 scale=1 / WS).then_inc(s["e"], 1)
                    if q >= 1:
                        act.wait_ge(s["sq"], due(L1, "sq", t, q))
                        A.activation(L1.sth[:, q - 1, :], L1.sq[:, q - 1, :], ACT.Copy).then_inc(s["sh"], 1)
                yield at1("PA", 4)
                act.wait_ge(s["sq"], due(L1, "sq", t, 4))
                A.activation(L1.sth[:, 3, :], L1.sq[:, 3, :], ACT.Copy).then_inc(s["sh"], 1)
                for j in range(2):
                    yield at1("V", j)
                    values(L1, j, t)
                for c in range(NT - 1):
                    yield at1("SK")
                    act.wait_ge(s["sk"], due(L1, "sk", t, c + 1))
                    A.activation(skt[:, c, :, :].rearrange("p a b -> p (a b)"),
                                 bank_of(L1, ("SK", c))[:, :].bitcast(F16)[:, 0:4 * P], ACT.Copy).then_inc(s["skt"], 1)
                yield at1("RM")
                act.wait_ge(s["rdif"], due(L1, "rdif", t, 1))
                A.activation(wexp[:, :, :, :], wdif[:, :, :, :], ACT.Exp, scale=1.0 / S).then_inc(s["rexp"], 1)
                for n in range(6):
                    yield at1("ST", n)
                    act.wait_ge(s["bf"], due(L1, "bf", t, n + 1))
                    A.activation(bsh[:, n, :], bf[:, n % 2, :], ACT.Copy).then_inc(s["bh"], 1)
                yield from tiles(0, CUT, t)
                yield None

            def lane1_end(t):
                yield from tiles(CUT, 10, t)
                yield from ffn(L1, xa, at1, t)
                yield None

            def lane2(t):
                s = s2
                yield at2("T")
                act.wait_ge(s1["xffn"], due(L1, "xffn", t, 2))
                act.wait_ge(s["store"], due(L2, "store", t, 0))
                act.dma_start(xc[:, :, :], xb[:, :, :]).then_inc(s["handed"], 16)
                normed(L2, 0, xb, t)
                yield at2("TT")
                turned(L2, 0, t)
                for q in range(4):
                    yield at2("PB", q)
                    act.wait_ge(s["y"], due(L2, "y", t, q + 1))
                    A.activation(L2.sth[:, q, :], L2.sq[:, q, :], ACT.Copy).then_inc(s["sh"], 1)
                for j in range(2):
                    yield at2("V", j)
                    values(L2, j, t)
                for n in range(4, NH + LAG):
                    yield at2("N", n)
                    if n % NT == 0 and n < NH + NT:
                        g = n // NT - 1
                        act.wait_ge(s["nm"], due(L2, "nm", t, g + 1))
                        if g >= 2:
                            act.wait_ge(s["mrow"], due(L2, "mrow", t, 32 * (g - 1)))
                        A.activation(nmt[:, g % 2, :], bank_of(L2, ("NM", g))[:, :].bitcast(F16)[:, 0:P],
                                     ACT.Copy).then_inc(s["nmt"], 1)
                    yield at2("NS", n)
                    h = n - LAG
                    if h < 0:
                        continue
                    if h >= 2:
                        act.wait_ge(s["plo_pool"], due(L2, "plo_pool", t, 2 * (h - 1)))
                        act.wait_ge(s["plo_dve"], due(L2, "plo_dve", t, h - 1))
                    for k in range(3):
                        act.wait_ge(s["s2"], due(L2, "s2", t, 3 * h + k + 1))
                        A.activation(pf[:, h % 2, S2_COL[k]:S2_COL[k] + S2_W[k]], bank_of(L2, ("S2", h, k))[:, 0:S2_W[k]],
                                     ACT.Exp, scale=D ** -0.5 / RS ** 2).then_inc(s["pexp"], 1)
                    yield at2("NX", n)
                    for k in range(2):
                        at = slice(S2_COL[k], S2_COL[k] + S2_W[k])
                        act.wait_ge(s["pexp"], due(L2, "pexp", t, 3 * h + k + 1))
                        if h >= RING:
                            act.wait_ge(s["pv"], due(L2, "pv", t, h - RING + 1))
                        A.activation(ph[h % RING][:, at], pf[:, h % 2, at], ACT.Copy).then_inc(s["phi"], 1)
                for half in range(KH):
                    yield at2("OT", half)
                    act.wait_ge(s["ot"], due(L2, "ot", t, half + 1))
                    A.activation(L2.oth[:, half, :], bank_of(L2, ("OT", half))[:, :], ACT.Copy).then_inc(s["oh"], 1)
                yield from ffn(L2, xc, at2, t)
                yield at2("END")
                act.wait_ge(s["xffn"], due(L2, "xffn", t, 2))
                act.dma_start(sequence(x_out, t), xc[:, :, :]).then_inc(s["store"], 16)
                yield None

            alone(lane1_start(0))
            alone(lane1_end(0))
            alone(lane1_start(1))
            with act.Fori(1, B - 1) as it:
                in_order(lane2(it - 1), after(back(lane1_end(it)), lane1_start(it + 1)))
            in_order(lane2(B - 2), back(lane1_end(B - 1)))
            alone(lane2(B - 1))
            act.wait_ge(s2["store"], 16 * B + 1)

        @block.vector
        def _(dve):
            at1, at2 = marks(1, "dve"), marks(2, "dve")
            chain = [0]
            V = nc.vector

            def link(ins):
                chain[0] += 1
                ins.then_inc(dve_setup, 1)
                dve.wait_ge(dve_setup, chain[0])

            link(V.memset(onesf[:, :], 1.0))
            for L in (L1, L2):
                link(V.memset(L.vp[:, :, :, 2 * D:VW], 1.0))
            dve.wait_ge(w_in, 16 * NMAT)
            for stage, at, n in ((w_stage[0], 0, 8), (w_stage[1], 8, 2)):
                cols = n * KH * H
                hi = wh[:, at:at + n, :, :].rearrange("p n k f -> p (n k f)")
                lo = wl[:, at:at + n, :, :].rearrange("p n k f -> p (n k f)")
                link(V.tensor_scalar(hi, stage[:, 0:cols], WS, None, ALU.mult))
                link(V.scalar_tensor_tensor(lo, stage[:, 0:cols], WS, hi, ALU.mult, ALU.subtract))
            dve.wait_ge(act_setup, 3)
            link(V.tensor_scalar(gates[:, 1, :], gates[:, 1, :], 1.0, None, ALU.add))
            link(V.reciprocal(gates[:, 2, :], gates[:, 1, :]))
            link(V.tensor_scalar(wc[:, :, M, :], gates[:, 2, :].rearrange("p (a h) -> p a h", a=KH), -1.0, 1.0,
                                 ALU.mult, ALU.add))
            link(V.tensor_scalar(gates[:, 3, :], gates[:, 2, :], VS, None, ALU.mult))
            dve.wait_ge(pe_setup, 1)
            link(V.tensor_scalar(small[:, 2:4], banks[0][:, 0:2], 1.0 / (H * FF), Q_EPS, ALU.mult, ALU.add))
            link(V.tensor_scalar(small[:, 4:6], small[:, 2:4], 0.5, None, ALU.mult))
            link(V.tensor_scalar(small[:, 6:8], small[:, 2:4], -0.5, None, ALU.mult))
            for n, w in enumerate((w1q[:, :, :].rearrange("p a b -> p (a b)"), w2q[:, :, :].rearrange("p a b -> p (a b)"))):
                stage = f_stage[:, n * NFW:(n + 1) * NFW]
                below = f_tmp[:, n * NFW:(n + 1) * NFW]
                link(V.tensor_scalar(below, stage, small[:, 6 + n:7 + n], None, ALU.is_lt))
                link(V.scalar_tensor_tensor(w, stage, small[:, 4 + n:5 + n], below, ALU.is_gt, ALU.subtract))
            dve.wait_ge(pool_const, 14)
            link(V.tensor_copy(identh[:, :], ident[:, :]))
            link(V.tensor_copy(identb[:, :], ident[:, :]))
            for st in (L2.qst, L2.kst):
                V.memset(st[PARTS:P, :, :].rearrange("p a s -> p (a s)").bitcast(F32), 0.0).then_inc(dve_setup, 1)
                chain[0] += 1
            dve.wait_ge(dve_setup, chain[0])
            V.memset(L2.kst[MAXROW:MAXROW + 2, :, :], SHIFT).then_inc(dve_setup, 1)
            chain[0] += 1
            dve.wait_ge(m_in, 16 * NH)
            bmh_all = bmh[:, :, :, :, :].rearrange("p a m h e -> p (a m h e)")
            bml_all = bml[:, :, :, :, :].rearrange("p a m h e -> p (a m h e)")
            link(V.tensor_copy(bmh_all, bm_all))
            link(V.tensor_tensor(bml_all, bm_all, bmh_all, ALU.subtract))
            link(V.tensor_copy(bnorm[:, :, :, :].rearrange("p a m h -> p (a m h)"),
                               bm_all.rearrange("p (n e) -> p n e", e=MW)[:, :, D]))
            assert chain[0] == DVE_SETUP, chain[0]
            dve.wait_ge(pool_const, 16)
            dve.wait_ge(primed, 1)

            def norm(L, u, X, mark, kind, t):
                s = L.s
                for j in range(NT):
                    V.bn_stats(L.stats[:, j, :], X[:, j, :]).then_inc(s["bn"], 1)
                dve.wait_ge(s["bn"], due(L, "bn", t, NT * (u + 1)))
                V.memset(L.tick[:, :], 0.0).then_inc(s["tick"], 1)
                for j in range(NT):
                    V.bn_aggr(L.mv[:, j, :], L.stats[:, j, :]).then_inc(s["mv"], 1)
                dve.wait_ge(s["mv"], due(L, "mv", t, NT * (u + 1)))
                V.tensor_scalar(L.ve[:, :], L.mv[:, :, 1], LN_EPS, None, ALU.add).then_inc(s["ve"], 1)
                yield mark(kind)
                dve.wait_ge(s["rstd"], due(L, "rstd", t, u + 1))
                V.scalar_tensor_tensor(L.shift[:, :], L.mv[:, :, 0], -1.0, L.rstd[:, :],
                                       ALU.mult, ALU.mult).then_inc(s["shift"], 1)

            def low_parts(L, u, t):
                s = L.s
                for k in range(KH):
                    dve.wait_ge(s["xh"], due(L, "xh", t, 2 * u + k + 1))
                    V.tensor_tensor(L.xlo[:, k, :], bank_of(L, ("T", u, k))[:, :], L.xh[:, k, :],
                                    ALU.subtract).then_inc(s["xl"], 1)

            def values(L, j, t):
                dve.wait_ge(L.s["vh"], due(L, "vh", t, j + 1))
                for c in range(2):
                    ins = V.scalar_tensor_tensor(
                        L.vp[:, 2 * j + c, :, D:2 * D],
                        bank_of(L, ("V", j))[:, c * H:(c + 1) * H].rearrange("p (h d) -> p h d", d=D),
                        VS / WS, L.vp[:, 2 * j + c, :, 0:D], ALU.mult, ALU.subtract)
                ins.then_inc(L.s["vl"], 1)

            def add_attention(L, j, X, Y, t):
                s = L.s
                dve.wait_ge(s["wo"], due(L, "wo", t, j + 1))
                two = slice(2 * j, 2 * j + 2)
                V.scalar_tensor_tensor(Y[:, two, :], bank_of(L, ("WO", j))[:, :].rearrange("p (a f) -> p a f", a=2),
                                       1 / (WS * VS), X[:, two, :], ALU.mult, ALU.add).then_inc(s["xres"], 1)

            def ffn(L, X, Y, mark, t):
                s = L.s
                yield mark("FT")
                dve.wait_ge(s["xres"], due(L, "xres", t, 2))
                yield from norm(L, 1, X, mark, "FTR", t)
                yield mark("FTT")
                low_parts(L, 1, t)
                for m in range(1, FT, 2):
                    yield mark("UP", m)
                    dve.wait_ge(s["hh"], due(L, "hh", t, m + 1))
                    V.tensor_tensor(L.hl[:, m, :], L.hf[:, 1, :], L.hh[:, m, :], ALU.subtract).then_inc(s["hl_dve"], 1)
                for j in range(2):
                    yield mark("DN", j)
                    if j == 0:
                        dve.wait_ge(s["xb"], due(L, "xb", t, 1))
                        if L is L1 and not (isinstance(t, int) and t == 0):
                            dve.wait_ge(s2["xn"], due(L2, "xn", t - 1, NT))
                            dve.wait_ge(s2["handed"], due(L2, "handed", t - 1, 16))
                    dve.wait_ge(s["dn"], due(L, "dn", t, j + 1))
                    two = slice(2 * j, 2 * j + 2)
                    V.tensor_tensor(Y[:, two, :], bank_of(L, ("DN", j))[:, :].rearrange("p (a f) -> p a f", a=2),
                                    X[:, two, :], ALU.add).then_inc(s["xffn"], 1)

            def causal(n, t):
                s = s1
                for k in range(2):
                    dve.wait_ge(s["a"], due(L1, "a", t, 2 * n + k + 1))
                    if n >= 1:
                        name = "al_dve" if k else "al_pool"
                        dve.wait_ge(s[name], due(L1, name, t, n))
                    V.scalar_tensor_tensor(am[:, k, :].rearrange("p (c s) -> p c s", c=NT),
                                           bank_of(L1, ("PR", n, k))[:, :].rearrange("p (c s) -> p c s", c=NT), AS,
                                           tri[:, :].rearrange("p (c s) -> p c s", c=1).broadcast_to([P, NT, P]),
                                           ALU.mult, ALU.mult).then_inc(s["am"], 1)

            def causal_low(n, t):
                s = s1
                dve.wait_ge(s["ah"], due(L1, "ah", t, 2 * n + 2))
                if n >= 2:
                    dve.wait_ge(s["om"], due(L1, "om", t, 3 * (n - 1)))
                V.tensor_tensor(alp[:, n % 2, 1, :], am[:, 1, :], ahp[:, n % 2, 1, :],
                                ALU.subtract).then_inc(s["al_dve"], 1)

            def combine(n, t):
                s = s1
                half, r = n // NT, n % 2
                local = bank_of(L1, ("LO", n))[:, 0:HH8 * VW].rearrange("p (h w) -> p h w", w=VW)
                pairs = [bank_of(L1, ("ME", n, k))[:, 0:2 * HH8 * MW] for k in range(2)]
                dve.wait_ge(s["om"], due(L1, "om", t, 3 * n + 1))
                V.tensor_scalar(den[:, r, M, :], local[:, :, 2 * D], MEM_EPS * AS, None, ALU.max).then_inc(s["clip"], 1)
                for k in range(2):
                    dve.wait_ge(s["om"], due(L1, "om", t, 3 * n + 2 + k))
                    V.tensor_scalar(den[:, r, 2 * k:2 * k + 2, :],
                                    pairs[k].rearrange("p (m h w) -> p m h w", m=2, w=MW)[:, :, :, D],
                                    MEM_EPS, None, ALU.max).then_inc(s["clip"], 1)
                dve.wait_ge(s["clip"], due(L1, "clip", t, 3 * n + 3))
                V.reciprocal(drec[:, r, :, :], den[:, r, :, :]).then_inc(s["rec"], 1)
                dve.wait_ge(s["rec"], due(L1, "rec", t, n + 1))
                V.tensor_tensor(coef[:, r, :, :], drec[:, r, :, :], wc[:, half, :, :], ALU.mult).then_inc(s["coef"], 1)
                dve.wait_ge(s["coef"], due(L1, "coef", t, n + 1))
                if n >= 2:
                    dve.wait_ge(s["ot"], due(L1, "ot", t, n - 1))
                for k in range(2):
                    V.tensor_tensor(t6[:, r, 2 * k:2 * k + 2, :].rearrange("p m (h d) -> p (m h) d", d=D),
                                    pairs[k].rearrange("p (m w) -> p m w", w=MW)[:, :, 0:D],
                                    coef[:, r, 2 * k:2 * k + 2, :].rearrange("p m (h o) -> p (m h) o", o=1)
                                    .broadcast_to([P, 2 * HH8, D]), ALU.mult).then_inc(s["t6"], 1)
                V.tensor_tensor(t6[:, r, M:M + 2, :].rearrange("p t (h d) -> p t h d", d=D),
                                local[:, :, 0:2 * D].rearrange("p h (t d) -> p t h d", t=2),
                                coef[:, r, M:M + 1, :].rearrange("p t (h o) -> p t h o", o=1)
                                .broadcast_to([P, 2, HH8, D]), ALU.mult).then_inc(s["t6"], 1)

            def heads_low(L, job, n, at, t):
                s = L.s
                dve.wait_ge(s["oh"], due(L, "oh", t, n + 1))
                half, cols = at
                V.tensor_tensor(L.otl[:, half, cols], bank_of(L, job)[:, 0:cols.stop - cols.start], L.oth[:, half, cols],
                                ALU.subtract).then_inc(s["ol"], 1)

            def memory_weights(t):
                s = s1
                dve.wait_ge(s["rm"], due(L1, "rm", t, 1))
                rm = bank_of(L1, ("RM",))[:, 0:KH * M * HH8].rearrange("p (a m h) -> p a m h", a=KH, m=M)
                V.tensor_reduce(wmax[:, :].rearrange("p (a h) -> p a h", a=KH), rm.rearrange("p a m h -> p a h m"),
                                AX, ALU.max).then_inc(s["rmax"], 1)
                dve.wait_ge(s["rmax"], due(L1, "rmax", t, 1))
                V.tensor_tensor(wdif[:, :, :, :], rm, wmax[:, :].rearrange("p (a m h) -> p a m h", a=KH, m=1)
                                .broadcast_to([P, KH, M, HH8]), ALU.subtract).then_inc(s["rdif"], 1)

            def memory_weights_end(t):
                s = s1
                dve.wait_ge(s["rexp"], due(L1, "rexp", t, 1))
                V.tensor_reduce(wsum[:, :].rearrange("p (a h) -> p a h", a=KH),
                                wexp[:, :, :, :].rearrange("p a m h -> p a h m"), AX, ALU.add).then_inc(s["rsum"], 1)
                dve.wait_ge(s["rsum"], due(L1, "rsum", t, 1))
                V.reciprocal(wrec[:, :], wsum[:, :]).then_inc(s["rrec"], 1)
                dve.wait_ge(s["rrec"], due(L1, "rrec", t, 1))
                V.tensor_tensor(wnum[:, :, :, :], wexp[:, :, :, :],
                                wrec[:, :].rearrange("p (a m h) -> p a m h", a=KH, m=1)
                                .broadcast_to([P, KH, M, HH8]), ALU.mult).then_inc(s["rcoef"], 1)
                dve.wait_ge(s["rcoef"], due(L1, "rcoef", t, 1))
                V.tensor_tensor(wc[:, :, 0:M, :], wnum[:, :, :, :],
                                gates[:, 3, :].rearrange("p (a m h) -> p a m h", a=KH, m=1)
                                .broadcast_to([P, KH, M, HH8]), ALU.mult).then_inc(s["rcoef"], 1)
                dve.wait_ge(s["rcoef"], due(L1, "rcoef", t, 2))

            def tiles(first, end, t):
                for n in range(first, end):
                    yield at1("N", n)
                    if n < 8:
                        causal(n, t)
                    yield at1("NC", n)
                    if 1 <= n < 9:
                        combine(n - 1, t)
                    yield at1("NL", n)
                    if n < 8:
                        causal_low(n, t)
                    if 2 <= n < 10:
                        half, c = divmod(n - 2, NT)
                        heads_low(L1, ("OT", n - 2), n - 2, (half, slice(c * P, (c + 1) * P)), t)

            def lane1_start(t):
                s = s1
                yield at1("T")
                dve.wait_ge(s["xin"], due(L1, "xin", t, 16))
                yield from norm(L1, 0, xa, at1, "TR", t)
                yield at1("TT")
                low_parts(L1, 0, t)
                for q in range(4):
                    yield at1("PA", q)
                    dve.wait_ge(s["e"], due(L1, "e", t, q + 1))
                    V.tensor_scalar(rbuf[:, q % 2, :], bank_of(L1, ("PA", q))[:, :], 1 / WS, 0.0,
                                    ALU.mult, ALU.max).then_inc(s["r"], 1)
                    dve.wait_ge(s["r"], due(L1, "r", t, q + 1))
                    V.scalar_tensor_tensor(L1.sq[:, q, :], ebuf[:, q % 2, :], 1.0, rbuf[:, q % 2, :], ALU.min, ALU.add,
                                           accum_out=ssum[:, q // 2:q // 2 + 1] if q % 2 == 0 else None
                                           ).then_inc(s["sq"], 1)
                yield at1("PA", 4)
                dve.wait_ge(s["sq"], due(L1, "sq", t, 4))
                for half in range(KH):
                    V.tensor_scalar(ssb[:, half, :], onesf[:, :], ssum[:, half:half + 1], None,
                                    ALU.mult).then_inc(s["ssb"], 1)
                for j in range(2):
                    yield at1("V", j)
                    values(L1, j, t)
                yield at1("RM")
                memory_weights(t)
                for n in range(6):
                    yield at1("ST", n)
                    dve.wait_ge(s["st"], due(L1, "st", t, n + 1))
                    if n >= 2:
                        dve.wait_ge(s["bl"], due(L1, "bl", t, n - 1))
                    V.scalar_tensor_tensor(bf[:, n % 2, :], bank_of(L1, ("ST", n))[:, 0:HH8 * VW], AS,
                                           bdmask[:, :, :].rearrange("p h w -> p (h w)"),
                                           ALU.mult, ALU.mult).then_inc(s["bf"], 1)
                memory_weights_end(t)
                yield from tiles(0, CUT, t)
                yield None

            def lane1_end(t):
                yield from tiles(CUT, 10, t)
                for j in range(2):
                    yield at1("WO", j)
                    add_attention(L1, j, xa, xa, t)
                yield from ffn(L1, xa, xb, at1, t)
                yield None

            def head_out(h, t):
                s = s2
                dve.wait_ge(s["pv"], due(L2, "pv", t, h + 1))
                ps = bank_of(L2, ("PV", h))[:, 0:NT * VW].rearrange("p (i w) -> p i w", w=VW)
                V.reciprocal(prec[:, h % 2, :], ps[:, :, 2 * D]).then_inc(s["prec"], 1)
                dve.wait_ge(s["prec"], due(L2, "prec", t, h + 1))
                V.tensor_tensor(tbuf[:, :, :, h, :], ps[:, :, 0:2 * D].rearrange("p i (t d) -> p i t d", t=2),
                                prec[:, h % 2, :].rearrange("p (i t o) -> p i t o", t=1, o=1)
                                .broadcast_to([P, NT, 2, D]), ALU.mult).then_inc(s["tb"], 1)

            def lane2(t):
                s = s2
                yield at2("T")
                dve.wait_ge(s1["xffn"], due(L1, "xffn", t, 2))
                yield from norm(L2, 0, xb, at2, "TR", t)
                yield at2("TT")
                low_parts(L2, 0, t)
                for q in range(4):
                    yield at2("PB", q)
                    for r in range(2):
                        dve.wait_ge(s["pr"], due(L2, "pr", t, 2 * q + r + 1))
                        if q >= 1 and r == 0:
                            dve.wait_ge(s["y"], due(L2, "y", t, q))
                        V.scalar_tensor_tensor(t12[:, r, :], bank_of(L2, ("PB", q, r))[:, :], RS / WS,
                                               (cost, sint)[r][:, :], ALU.mult, ALU.mult).then_inc(s["t12"], 1)
                    if q >= 1:
                        yield at2("PL", q)
                        dve.wait_ge(s["sh"], due(L2, "sh", t, q))
                        V.tensor_tensor(L2.stl[:, q - 1, :], L2.sq[:, q - 1, :], L2.sth[:, q - 1, :],
                                        ALU.subtract).then_inc(s["sl"], 1)
                yield at2("PB", 4)
                dve.wait_ge(s["sh"], due(L2, "sh", t, 4))
                V.tensor_tensor(L2.stl[:, 3, :], L2.sq[:, 3, :], L2.sth[:, 3, :], ALU.subtract).then_inc(s["sl"], 1)
                for j in range(2):
                    yield at2("V", j)
                    values(L2, j, t)
                for n in range(NH + PV_LAG + 1):
                    yield at2("N", n)
                    if n > PV_LAG:
                        head_out(n - PV_LAG - 1, t)
                    if n < NH:
                        for k, tiles in enumerate(S1_TILES):
                            dve.wait_ge(s["s1"], due(L2, "s1", t, 3 * n + k + 1))
                            for i in tiles:
                                g = NT * n + i
                                V.tensor_reduce(mxs[:, g:g + 1],
                                                bank_of(L2, ("S1", n, k))[:, Q_AT[i]:Q_AT[i] + (i + 1) * P],
                                                AX, ALU.max).then_inc(s["mx"], 1)
                        if n % NT == NT - 1:
                            q = n // NT
                            gs = slice(16 * q, 16 * q + 16)
                            dve.wait_ge(s["mx"], due(L2, "mx", t, 16 * (q + 1)))
                            dve.wait_ge(s["nm"], due(L2, "nm", t, q))
                            V.tensor_scalar(nt[:, 0, gs], mxs[:, gs], -1.0 / SHIFT, None, ALU.mult).then_inc(s["nh"], 1)
                            dve.wait_ge(s["nh"], due(L2, "nh", t, q + 1))
                            V.scalar_tensor_tensor(nt[:, 1, gs], mxs[:, gs], -1.0 / SHIFT, nt[:, 0, gs],
                                                   ALU.mult, ALU.subtract).then_inc(s["nl"], 1)
                    yield at2("NL", n)
                    h = n - LAG - 1
                    if 0 <= h < NH:
                        last = slice(S2_COL[-1], wide)
                        if h >= RING:
                            dve.wait_ge(s["pv"], due(L2, "pv", t, h - RING + 1))
                        dve.wait_ge(s["pexp"], due(L2, "pexp", t, 3 * h + 3))
                        V.tensor_copy(ph[h % RING][:, last], pf[:, h % 2, last]).then_inc(s["phi_dve"], 1)
                        dve.wait_ge(s["phi_dve"], due(L2, "phi_dve", t, h + 1))
                        V.tensor_tensor(pl[h % RING][:, last], pf[:, h % 2, last], ph[h % RING][:, last],
                                        ALU.subtract).then_inc(s["plo_dve"], 1)
                for half in range(KH):
                    yield at2("OT", half)
                    heads_low(L2, ("OT", half), half, (half, slice(0, S)), t)
                for j in range(2):
                    yield at2("WO", j)
                    if j == 0:
                        dve.wait_ge(s["handed"], due(L2, "handed", t, 16))
                    add_attention(L2, j, xc, xc, t)
                yield from ffn(L2, xc, xc, at2, t)
                yield None

            alone(lane1_start(0))
            alone(lane1_end(0))
            alone(lane1_start(1))
            with dve.Fori(1, B - 1) as it:
                in_order(lane2(it - 1), after(back(lane1_end(it)), lane1_start(it + 1)))
            in_order(lane2(B - 2), back(lane1_end(B - 1)))
            alone(lane2(B - 1))

        @block.tensor
        def _(pe):
            at1, at2 = marks(1, "pe"), marks(2, "pe")
            T = nc.tensor
            pe.wait_ge(act_setup, 3)
            pe.wait_ge(dve_setup, 1)
            T.matmul(banks[0][:, 0:2], onesf[:, :], small[:, 0:2], start=True, stop=True).then_inc(pe_setup, 1)
            pe.wait_ge(dve_setup, DVE_SETUP)
            pe.wait_ge(pool_const, 16)
            pe.wait_ge(primed, 1)

            def take(L, job, t):
                n, ring = L.at[job], len(L.banks)
                if n >= ring:
                    _, name, count = L.jobs[n - ring]
                    pe.wait_ge(L.s[name], due(L, name, t, count))
                else:
                    last = max(k for k in range(len(L.jobs)) if k % ring == n)
                    name = L.jobs[last][1]
                    pe.wait_ge(L.s[name], due(L, name, t, 0))
                return bank_of(L, job)

            def turn(L, u, t):
                s = L.s
                into = [take(L, ("T", u, k), t) for k in range(KH)]
                for j in range(NT):
                    pe.wait_ge(s["xn"], due(L, "xn", t, NT * u + j + 1))
                    for k in range(KH):
                        ins = T.transpose(into[k][:, j * P:(j + 1) * P], L.xn[:, j, k * P:(k + 1) * P], ident[:, :])
                        if j == NT - 1:
                            ins.then_inc(s["xt"], 1)

            def project(L, job, mat, m, name, t):
                into = take(L, job, t)
                n = 0
                for w, a in ((wh, L.xh), (wl, L.xh), (wh, L.xlo)):
                    for k in range(KH):
                        ins = T.matmul(into[:, :], w[:, mat, k, m * P:(m + 1) * P], a[:, k, :],
                                       start=(n == 0), stop=(n == 5))
                        n += 1
                ins.then_inc(L.s[name], 1)

            def rows(L, job, high, low, mat, name, t):
                into = take(L, job, t)
                for a in range(2):
                    n = 0
                    cols = slice((2 * job[-1] + a) * P, (2 * job[-1] + a + 1) * P)
                    for w, part in ((wh, high), (wl, high), (wh, low)):
                        for k in range(KH):
                            ins = T.matmul(into[:, a * H:(a + 1) * H], part[:, k, cols], w[:, mat, k, :],
                                           start=(n == 0), stop=(n == 5))
                            n += 1
                ins.then_inc(L.s[name], 1)

            def project_out(L, mat, mark, t):
                s = L.s
                for j in range(2):
                    yield mark("WO", j)
                    if j == 0:
                        pe.wait_ge(s["ol"], due(L, "ol", t, L.per["ol"]))
                    rows(L, ("WO", j), L.oth, L.otl, mat, "wo", t)

            def ffn(L, mark, t):
                s = L.s
                yield mark("FTT")
                turn(L, 1, t)
                for m in range(FT):
                    yield mark("UP", m)
                    if m == 0:
                        pe.wait_ge(s["xl"], due(L, "xl", t, 4))
                    into = take(L, ("UP", m), t)
                    for n, (a, k) in enumerate(((L.xh, 0), (L.xh, 1), (L.xlo, 0), (L.xlo, 1))):
                        ins = T.matmul(into[:, :], w1q[:, k, m * P:(m + 1) * P], a[:, k, :], start=(n == 0), stop=(n == 3))
                    ins.then_inc(s["up"], 1)
                for j2 in range(2):
                    yield mark("DN", j2)
                    into = take(L, ("DN", j2), t)
                    for a in range(2):
                        cols = slice((2 * j2 + a) * P, (2 * j2 + a + 1) * P)
                        for m in range(FT):
                            if j2 == 0 and a == 0:
                                yield mark("DM", m)
                                pe.wait_ge(s["hh"], due(L, "hh", t, m + 1))
                                name = "hl_dve" if m % 2 else "hl_pool"
                                pe.wait_ge(s[name], due(L, name, t, m // 2 + 1))
                            for part in (L.hh, L.hl):
                                ins = T.matmul(into[:, a * H:(a + 1) * H], part[:, m, cols], w2q[:, m, :],
                                               start=(m == 0 and part is L.hh), stop=(m == FT - 1 and part is L.hl))
                    ins.then_inc(s["dn"], 1)

            def stacks_landed(L, half, t):
                pe.wait_ge(L.landed[half], (t + 1) * LANDED)

            def products(n, t):
                half, c = divmod(n, NT)
                cols = slice(c * P, (c + 1) * P)
                if c == 0:
                    stacks_landed(L1, half, t)
                for k in range(2):
                    into = take(L1, ("PR", n, k), t)
                    for h4 in range(4):
                        h = half * HH8 + 4 * k + h4
                        ins = T.matmul(into[:, h4 * P:(h4 + 1) * P], L1.kst[0:STK, h, cols], L1.qst[0:STK, h, cols],
                                       start=True, stop=True)
                    ins.then_inc(s1["a"], 1)

            def outputs(n, t):
                s = s1
                half, c = divmod(n, NT)
                cols = slice(c * P, (c + 1) * P)
                qh, ql = L1.sth[:, 2 * half, cols], L1.stl[:, 2 * half, cols]
                local = take(L1, ("LO", n), t)
                if c:
                    state = 3 * half + c - 1
                    for m, (a, b) in enumerate(((qh, bsh), (ql, bsh), (qh, bsl))):
                        T.matmul(local[:, 0:HH8 * VW], a, b[:, state, :], start=(m == 0), stop=(m == 2),
                                 skip_group_check=True)
                yield at1("NA", n + 1)
                pe.wait_ge(s["al_pool"], due(L1, "al_pool", t, n + 1))
                pe.wait_ge(s["al_dve"], due(L1, "al_dve", t, n + 1))
                for h in range(HH8):
                    for part in (ahp, alp):
                        ins = T.matmul(local[:, h * VW:(h + 1) * VW], part[:, n % 2, h // 4, (h % 4) * P:(h % 4 + 1) * P],
                                       L1.vp[:, c, half * HH8 + h, :],
                                       start=(c == 0 and part is ahp), stop=(part is alp), skip_group_check=True)
                ins.then_inc(s["om"], 1)
                for k in range(2):
                    into = take(L1, ("ME", n, k), t)
                    for m, (a, b) in enumerate(((qh, bmh), (ql, bmh), (qh, bml))):
                        ins = T.matmul(into[:, 0:2 * HH8 * MW], a,
                                       b[:, half, 2 * k:2 * k + 2, :, :].rearrange("p m h w -> p (m h w)"),
                                       start=(m == 0), stop=(m == 2))
                    ins.then_inc(s["om"], 1)

            def turn_back(n, t):
                into = take(L1, ("OT", n), t)
                pe.wait_ge(s1["t6"], due(L1, "t6", t, 3 * n + 3))
                for k in range(M + 2):
                    ins = T.matmul(into[:, 0:P], t6[:, n % 2, k, :], ident[:, :], is_transpose=True,
                                   start=(k == 0), stop=(k == M + 1))
                ins.then_inc(s1["ot"], 1)

            def tiles(first, end, t):
                for n in range(first, end):
                    yield at1("N", n)
                    if n < 8:
                        products(n, t)
                    yield at1("NO", n)
                    if n == 1:
                        pe.wait_ge(s1["bl"], due(L1, "bl", t, 6))
                    if 1 <= n < 9:
                        yield from outputs(n - 1, t)
                    yield at1("NT", n)
                    if n >= 2:
                        turn_back(n - 2, t)

            def lane1_start(t):
                s = s1
                yield at1("TT")
                turn(L1, 0, t)
                for q, (mat, m) in enumerate(((AQ, 0), (AK, 0), (AQ, 1), (AK, 1))):
                    yield at1("PA", q)
                    if q == 0:
                        pe.wait_ge(s["xl"], due(L1, "xl", t, 2))
                    project(L1, ("PA", q), mat, m, "proj", t)
                for j in range(2):
                    yield at1("V", j)
                    rows(L1, ("V", j), L1.xh, L1.xlo, AV, "v", t)
                for c in range(NT - 1):
                    yield at1("SK")
                    if c == 0:
                        pe.wait_ge(s["sl"], due(L1, "sl", t, 4))
                    into = take(L1, ("SK", c), t)
                    cols = slice(c * P, (c + 1) * P)
                    for n, (part, half) in enumerate(((L1.sth, 0), (L1.stl, 0), (L1.sth, 1), (L1.stl, 1))):
                        ins = T.transpose(into[:, :].bitcast(F16)[:, n * P:(n + 1) * P], part[:, 2 * half + 1, cols],
                                          identh[:, :])
                    ins.then_inc(s["sk"], 1)
                yield at1("RM")
                into = take(L1, ("RM",), t)
                pe.wait_ge(s["ssb"], due(L1, "ssb", t, 2))
                for half in range(KH):
                    ins = T.matmul(into[:, half * M * HH8:(half + 1) * M * HH8], ssb[:, half, :],
                                   bnorm[:, half, :, :].rearrange("p m h -> p (m h)"), start=True, stop=True)
                ins.then_inc(s["rm"], 1)
                for n in range(6):
                    yield at1("ST", n)
                    if n == 0:
                        pe.wait_ge(s["vl"], due(L1, "vl", t, 2))
                        pe.wait_ge(s["skt"], due(L1, "skt", t, NT - 1))
                    half, c = divmod(n, 3)
                    into = take(L1, ("ST", n), t)
                    for cc in range(c + 1):
                        for part in range(2):
                            ins = T.matmul(into[:, 0:HH8 * VW], skt[:, cc, 2 * half + part, :],
                                           L1.vp[:, cc, half * HH8:(half + 1) * HH8, :].rearrange("p h w -> p (h w)"),
                                           start=(cc == 0 and part == 0), stop=(cc == c and part == 1))
                    ins.then_inc(s["st"], 1)
                yield from tiles(0, CUT, t)
                yield None

            def lane1_end(t):
                yield from tiles(CUT, 10, t)
                yield from project_out(L1, AO, at1, t)
                yield from ffn(L1, at1, t)
                yield None

            def scores(h, t):
                if h % HH8 == 0:
                    stacks_landed(L2, h // HH8, t)
                for k, tiles in enumerate(S1_TILES):
                    into = take(L2, ("S1", h, k), t)
                    for i in tiles:
                        T.matmul(into[:, Q_AT[i]:Q_AT[i] + (i + 1) * P], L2.qst[0:STK, h, i * P:(i + 1) * P],
                                 L2.kst[0:STK, h, 0:(i + 1) * P], start=True, stop=True)
                        ins = T.matmul(into[:, Q_AT[i] + i * P:Q_AT[i] + (i + 1) * P], identb[:, :], mask_qk[:, :],
                                       start=False, stop=True, skip_group_check=True)
                    ins.then_inc(s2["s1"], 1)

            def shifted(h, t):
                if h % NT == 0:
                    pe.wait_ge(s2["mrow"], due(L2, "mrow", t, 32 * (h // NT + 1)))
                for n, tiles in enumerate(S2_TILES):
                    into = take(L2, ("S2", h, n), t)
                    for kt in tiles:
                        at = KT_AT[kt] - S2_COL[n]
                        T.matmul(into[:, at:at + (NT - kt) * P], L2.kst[:, h, kt * P:(kt + 1) * P],
                                 L2.qst[:, h, kt * P:S], start=True, stop=True)
                        ins = T.matmul(into[:, at:at + P], identb[:, :], mask_kq[:, :], start=False, stop=True,
                                       skip_group_check=True)
                    ins.then_inc(s2["s2"], 1)

            def weighted(h, t):
                into = take(L2, ("PV", h), t)
                pe.wait_ge(s2["plo_pool"], due(L2, "plo_pool", t, 2 * h + 2))
                pe.wait_ge(s2["plo_dve"], due(L2, "plo_dve", t, h + 1))
                for i in range(NT):
                    at = i * VW
                    for kt in range(i + 1):
                        p0 = KT_AT[kt] + (i - kt) * P
                        for part in (ph, pl):
                            ins = T.matmul(into[:, at:at + VW], part[h % RING][:, p0:p0 + P], L2.vp[:, kt, h, :],
                                           start=(kt == 0 and part is ph), stop=(kt == i and part is pl),
                                           skip_group_check=True)
                ins.then_inc(s2["pv"], 1)

            def lane2(t):
                s = s2
                yield at2("TT")
                turn(L2, 0, t)
                for q, (m, a, b) in enumerate(((0, BQ, BQR), (0, BK, BKR), (1, BQ, BQR), (1, BK, BKR))):
                    yield at2("PB", q)
                    if q == 0:
                        pe.wait_ge(s["xl"], due(L2, "xl", t, 2))
                    project(L2, ("PB", q, 0), a, m, "pr", t)
                    project(L2, ("PB", q, 1), b, m, "pr", t)
                for j in range(2):
                    yield at2("V", j)
                    rows(L2, ("V", j), L2.xh, L2.xlo, BV, "v", t)
                for n in range(NH + PV_LAG):
                    yield at2("N", n)
                    if n < NH:
                        scores(n, t)
                    yield at2("NS", n)
                    if n >= 4 and n % 4 == 0 and n < NH + 4:
                        q = n // 4 - 1
                        into = take(L2, ("NM", q), t)
                        pe.wait_ge(s["nl"], due(L2, "nl", t, q + 1))
                        T.transpose(into[:, :].bitcast(F16)[:, 0:P], nt[:, :, :].rearrange("p a g -> p (a g)"),
                                    identh[:, :]).then_inc(s["nm"], 1)
                    if LAG <= n < NH + LAG:
                        shifted(n - LAG, t)
                    yield at2("NP", n)
                    if n >= PV_LAG:
                        if n == PV_LAG:
                            pe.wait_ge(s["vl"], due(L2, "vl", t, 2))
                        weighted(n - PV_LAG, t)
                for half in range(KH):
                    yield at2("OT", half)
                    pe.wait_ge(s["tb"], due(L2, "tb", t, NH))
                    into = take(L2, ("OT", half), t)
                    for i in range(NT):
                        for k in range(2):
                            ins = T.matmul(into[:, i * P:(i + 1) * P],
                                           tbuf[:, i, k, half * HH8:(half + 1) * HH8, :].rearrange("p h d -> p (h d)"),
                                           ident[:, :], is_transpose=True, start=(k == 0), stop=(k == 1))
                    ins.then_inc(s["ot"], 1)
                yield from project_out(L2, BO, at2, t)
                yield from ffn(L2, at2, t)
                yield None

            alone(lane1_start(0))
            alone(lane1_end(0))
            alone(lane1_start(1))
            with pe.Fori(1, B - 1) as it:
                in_order(lane2(it - 1), after(back(lane1_end(it)), lane1_start(it + 1)))
            in_order(lane2(B - 2), back(lane1_end(B - 1)))
            alone(lane2(B - 1))


def kernel(**inputs):
    import numpy as _np
    import concourse.bacc as _bacc
    from concourse import mybir as _mybir
    from concourse.bass_utils import run_bass_kernel_spmd as _run

    a = {k: _np.asarray(v) for k, v in inputs.items()}
    pairs = _np.arange(H) ^ 1
    mats = [a["L0_attn_a_w_q"], a["L0_attn_a_w_k"], a["L0_attn_a_w_v"], a["L0_attn_a_w_o"],
            a["L0_attn_b_W_Q"], a["L0_attn_b_W_K"], a["L0_attn_b_W_V"], a["L0_attn_b_W_O"],
            a["L0_attn_b_W_Q"][pairs], a["L0_attn_b_W_K"][pairs]]
    f32 = _np.float32
    inv = (f32(THETA) ** (f32(-2.0) * _np.arange(D // 2, dtype=f32) / f32(D))).astype(f32)
    ang = (_np.arange(S, dtype=f32)[:, None] * inv).astype(f32)
    of_row = (_np.arange(P) % D) // 2
    sign = _np.where(_np.arange(P) % 2 == 0, -1.0, 1.0).astype(f32)
    cos = _np.cos(ang)[:, of_row].T
    sin = _np.sin(ang)[:, of_row].T * sign[:, None]
    arrays = {
        "x": a["L0_attn_a_hidden_states"].reshape(B * S, H),
        "wall": _np.stack([m.T for m in mats]),
        "mem": _np.concatenate([a["L0_attn_a_memories"], a["L0_attn_a_memory_norms"][..., None]],
                               axis=-1).transpose(1, 2, 0, 3),
        "gate": a["L0_attn_a_gate"].reshape(1, NH),
        "w1t": a["L0_ffn_W1"].T,
        "b1t": a["L0_ffn_b1"].reshape(FT, P).T,
        "w2t": a["L0_ffn_W2"].T,
        "b2": a["L0_ffn_b2"].reshape(1, H),
        "cos": cos,
        "sin": sin,
    }
    arrays = {k: _np.ascontiguousarray(v) for k, v in arrays.items()}
    nc = _bacc.Bacc("TRN2", target_bir_lowering=False, num_devices=1)
    args = [nc.dram_tensor(k, v.shape, _mybir.dt.from_np(v.dtype), kind="ExternalInput").ap() for k, v in arrays.items()]
    out = nc.dram_tensor("out", (B * S, H), _mybir.dt.float32, kind="ExternalOutput").ap()
    build(nc, *args, out)
    r = _run(nc, [arrays], core_ids=[0])
    return r.results[0]["out"].reshape(B, S, H)
```
